# Optimizing a Trainium2 kernel written in Bass

```python
import numpy as np
import jax
import jax.numpy as jnp

def _softmax(x, axis=-1):
    return jax.nn.softmax(x, axis=axis)

def _gelu(x):
    return jax.nn.gelu(x, approximate=True)

def _silu(x):
    return jax.nn.silu(x)

def _sigmoid(x):
    return jax.nn.sigmoid(x)

def _layernorm(x, axis=-1, eps=1e-05):
    m = jnp.mean(x, axis=axis, keepdims=True)
    v = jnp.var(x, axis=axis, keepdims=True)
    return (x - m) / jnp.sqrt(v + eps)

def _scatter_add(tgt, idx, src, axis=0):
    return tgt.at[idx].add(src)

def _segment_sum(src, seg, n):
    return jax.ops.segment_sum(src, seg, n)
kernel_name = 'mk_macaron_d2_jaxref_r8_b50540'

def setup_inputs(seed: int=0):
    np.random.seed(seed)
    _w = jnp.asarray

    def _L0_attn_setup():
        import jax, jax.numpy as jnp
        import numpy as np
        D_MODEL = 128
        N_HEAD = 16
        N_KV_HEAD = 4
        HEAD_DIM = D_MODEL // N_HEAD
        N_GROUP = N_HEAD // N_KV_HEAD
        ROPE_BASE = 10000.0
        ROPE_DIM = HEAD_DIM

        def _rope_tables(seq_len, dtype):
            half = ROPE_DIM // 2
            inv_freq = 1.0 / ROPE_BASE ** (jnp.arange(0, half, dtype=jnp.float32) * 2.0 / ROPE_DIM)
            pos = jnp.arange(seq_len, dtype=jnp.float32)
            freqs = pos[:, None] * inv_freq[None, :]
            return (jnp.cos(freqs).astype(dtype), jnp.sin(freqs).astype(dtype))

        def _apply_rope(t):
            S = t.shape[2]
            cos, sin = _rope_tables(S, t.dtype)
            half = ROPE_DIM // 2
            t1 = t[..., :half]
            t2 = t[..., half:ROPE_DIM]
            rot = jnp.concatenate([t1 * cos - t2 * sin, t1 * sin + t2 * cos], axis=-1)
            if ROPE_DIM < t.shape[-1]:
                rot = jnp.concatenate([rot, t[..., ROPE_DIM:]], axis=-1)
            return rot
        key = jax.random.key(seed)
        ks = jax.random.split(key, 5)
        B, S = (1, 512)
        sd = 1.0 / np.sqrt(D_MODEL)
        x = jax.random.normal(ks[0], (B, S, D_MODEL), dtype=jnp.float32)
        w_q = jax.random.normal(ks[1], (D_MODEL, N_HEAD * HEAD_DIM), dtype=jnp.float32) * sd
        w_k = jax.random.normal(ks[2], (D_MODEL, N_KV_HEAD * HEAD_DIM), dtype=jnp.float32) * sd
        w_v = jax.random.normal(ks[3], (D_MODEL, N_KV_HEAD * HEAD_DIM), dtype=jnp.float32) * sd
        w_o = jax.random.normal(ks[4], (D_MODEL, D_MODEL), dtype=jnp.float32) * sd
        return {'x': x, 'w_q': w_q, 'w_k': w_k, 'w_v': w_v, 'w_o': w_o}
    _L0_attn_in = _L0_attn_setup()

    def _L0_ffn_setup():
        import jax, jax.numpy as jnp
        import numpy as np
        DIM = 128

        def _reference_tuple_inner(x, W_r, W_k, W_v, mu_r, mu_k):
            B, T, C = x.shape
            x_prev = jnp.concatenate([jnp.zeros((B, 1, C), x.dtype), x[:, :-1, :]], axis=1)
            xr = mu_r * x + (1.0 - mu_r) * x_prev
            xk = mu_k * x + (1.0 - mu_k) * x_prev
            r = jax.nn.sigmoid(jnp.einsum('btc,dc->btd', xr, W_r))
            k = jnp.einsum('btc,dc->btd', xk, W_k)
            k_act = jnp.square(jax.nn.relu(k))
            out = r * jnp.einsum('btc,dc->btd', k_act, W_v)
            new_state = x[:, -1, :]
            return (out, new_state)
        key = jax.random.key(seed)
        ks = jax.random.split(key, 6)
        B, T, C = (8, 256, DIM)
        x = jax.random.normal(ks[0], (B, T, C), dtype=jnp.float32)
        s = 1.0 / np.sqrt(C)
        W_r = jax.random.uniform(ks[1], (C, C), jnp.float32, -s, s)
        W_k = jax.random.uniform(ks[2], (C, C), jnp.float32, -s, s)
        W_v = jax.random.uniform(ks[3], (C, C), jnp.float32, -s, s)
        mu_r = jax.random.uniform(ks[4], (C,), jnp.float32)
        mu_k = jax.random.uniform(ks[5], (C,), jnp.float32)
        return {'x': x, 'W_r': W_r, 'W_k': W_k, 'W_v': W_v, 'mu_r': mu_r, 'mu_k': mu_k}
    _L0_ffn_in = _L0_ffn_setup()

    def _L1_attn_setup():
        import jax, jax.numpy as jnp
        import numpy as np
        key = jax.random.key(seed)
        ks = jax.random.split(key, 5)
        Bsz, T, d = (8, 256, 128)
        x = jax.random.normal(ks[0], (Bsz, T, d), dtype=jnp.float32)
        W_in = jax.random.normal(ks[1], (d, d), dtype=jnp.float32) * (1.0 / np.sqrt(d))
        b_in = jnp.zeros((d,), dtype=jnp.float32)
        log_A = -jnp.ones((d,), dtype=jnp.float32)
        B_vec = jax.random.normal(ks[2], (d,), dtype=jnp.float32) * 0.05
        C = jax.random.normal(ks[3], (d, d), dtype=jnp.float32) * 0.05
        D = jnp.zeros((d,), dtype=jnp.float32)
        return {'x': x, 'W_in': W_in, 'b_in': b_in, 'log_A': log_A, 'B_vec': B_vec, 'C': C, 'D': D}
    _L1_attn_in = _L1_attn_setup()

    def _L1_ffn_setup():
        import jax, jax.numpy as jnp
        import numpy as np
        TOP_K = 2

        def _ffn(x, gw, uw, dw):
            return jax.nn.silu(x @ gw.T) * (x @ uw.T) @ dw.T
        key = jax.random.key(seed)
        ks = jax.random.split(key, 8)
        w = lambda k, shape: jax.random.normal(k, shape, jnp.float32) * 0.02
        return dict(x=jax.random.normal(ks[0], (4, 256, 128), jnp.float32), gate_w=w(ks[1], (8, 128)), expert_gate=w(ks[2], (8, 352, 128)), expert_up=w(ks[3], (8, 352, 128)), expert_down=w(ks[4], (8, 128, 352)), shared_gate=w(ks[5], (352, 128)), shared_up=w(ks[6], (352, 128)), shared_down=w(ks[7], (128, 352)))
    _L1_ffn_in = _L1_ffn_setup()
    _d = {'L0_attn_x': _L0_attn_in['x'], 'L0_attn_w_q': _L0_attn_in['w_q'], 'L0_attn_w_k': _L0_attn_in['w_k'], 'L0_attn_w_v': _L0_attn_in['w_v'], 'L0_attn_w_o': _L0_attn_in['w_o'], 'L0_ffn_W_r': _L0_ffn_in['W_r'], 'L0_ffn_W_k': _L0_ffn_in['W_k'], 'L0_ffn_W_v': _L0_ffn_in['W_v'], 'L0_ffn_mu_r': _L0_ffn_in['mu_r'], 'L0_ffn_mu_k': _L0_ffn_in['mu_k'], 'L1_attn_W_in': _L1_attn_in['W_in'], 'L1_attn_b_in': _L1_attn_in['b_in'], 'L1_attn_log_A': _L1_attn_in['log_A'], 'L1_attn_B_vec': _L1_attn_in['B_vec'], 'L1_attn_C': _L1_attn_in['C'], 'L1_attn_D': _L1_attn_in['D'], 'L1_ffn_gate_w': _L1_ffn_in['gate_w'], 'L1_ffn_expert_gate': _L1_ffn_in['expert_gate'], 'L1_ffn_expert_up': _L1_ffn_in['expert_up'], 'L1_ffn_expert_down': _L1_ffn_in['expert_down'], 'L1_ffn_shared_gate': _L1_ffn_in['shared_gate'], 'L1_ffn_shared_up': _L1_ffn_in['shared_up'], 'L1_ffn_shared_down': _L1_ffn_in['shared_down']}
    _x0 = _d['L0_attn_x']
    _d['L0_attn_x'] = jax.random.normal(jax.random.fold_in(jax.random.key(seed), 1), (4, 1024, 128), dtype=_x0.dtype)
    del _x0
    return _d

def reference(L0_attn_x, L0_attn_w_q, L0_attn_w_k, L0_attn_w_v, L0_attn_w_o, L0_ffn_W_r, L0_ffn_W_k, L0_ffn_W_v, L0_ffn_mu_r, L0_ffn_mu_k, L1_attn_W_in, L1_attn_b_in, L1_attn_log_A, L1_attn_B_vec, L1_attn_C, L1_attn_D, L1_ffn_gate_w, L1_ffn_expert_gate, L1_ffn_expert_up, L1_ffn_expert_down, L1_ffn_shared_gate, L1_ffn_shared_up, L1_ffn_shared_down):

    def _L0_attn_ref(x, w_q, w_k, w_v, w_o):
        import jax, jax.numpy as jnp
        import numpy as np
        D_MODEL = 128
        N_HEAD = 16
        N_KV_HEAD = 4
        HEAD_DIM = D_MODEL // N_HEAD
        N_GROUP = N_HEAD // N_KV_HEAD
        ROPE_BASE = 10000.0
        ROPE_DIM = HEAD_DIM

        def _rope_tables(seq_len, dtype):
            half = ROPE_DIM // 2
            inv_freq = 1.0 / ROPE_BASE ** (jnp.arange(0, half, dtype=jnp.float32) * 2.0 / ROPE_DIM)
            pos = jnp.arange(seq_len, dtype=jnp.float32)
            freqs = pos[:, None] * inv_freq[None, :]
            return (jnp.cos(freqs).astype(dtype), jnp.sin(freqs).astype(dtype))

        def _apply_rope(t):
            S = t.shape[2]
            cos, sin = _rope_tables(S, t.dtype)
            half = ROPE_DIM // 2
            t1 = t[..., :half]
            t2 = t[..., half:ROPE_DIM]
            rot = jnp.concatenate([t1 * cos - t2 * sin, t1 * sin + t2 * cos], axis=-1)
            if ROPE_DIM < t.shape[-1]:
                rot = jnp.concatenate([rot, t[..., ROPE_DIM:]], axis=-1)
            return rot
        B, S, _ = x.shape
        q = (x @ w_q).reshape(B, S, N_HEAD, HEAD_DIM).transpose(0, 2, 1, 3)
        k = (x @ w_k).reshape(B, S, N_KV_HEAD, HEAD_DIM).transpose(0, 2, 1, 3)
        v = (x @ w_v).reshape(B, S, N_KV_HEAD, HEAD_DIM).transpose(0, 2, 1, 3)
        q = _apply_rope(q)
        k = _apply_rope(k)
        k = jnp.repeat(k, N_GROUP, axis=1)
        v = jnp.repeat(v, N_GROUP, axis=1)
        scale = 1.0 / jnp.sqrt(jnp.asarray(HEAD_DIM, dtype=x.dtype))
        scores = jnp.einsum('bhqd,bhkd->bhqk', q, k) * scale
        attn = jax.nn.softmax(scores, axis=-1)
        out = jnp.einsum('bhqk,bhkd->bhqd', attn, v)
        out = out.transpose(0, 2, 1, 3).reshape(B, S, D_MODEL)
        return out @ w_o

    def _L0_ffn_ref(x, W_r, W_k, W_v, mu_r, mu_k):
        import jax, jax.numpy as jnp
        import numpy as np
        DIM = 128

        def _reference_tuple_inner(x, W_r, W_k, W_v, mu_r, mu_k):
            B, T, C = x.shape
            x_prev = jnp.concatenate([jnp.zeros((B, 1, C), x.dtype), x[:, :-1, :]], axis=1)
            xr = mu_r * x + (1.0 - mu_r) * x_prev
            xk = mu_k * x + (1.0 - mu_k) * x_prev
            r = jax.nn.sigmoid(jnp.einsum('btc,dc->btd', xr, W_r))
            k = jnp.einsum('btc,dc->btd', xk, W_k)
            k_act = jnp.square(jax.nn.relu(k))
            out = r * jnp.einsum('btc,dc->btd', k_act, W_v)
            new_state = x[:, -1, :]
            return (out, new_state)
        return _reference_tuple_inner(x, W_r, W_k, W_v, mu_r, mu_k)[0]

    def _L1_attn_ref(x, W_in, b_in, log_A, B_vec, C, D):
        import jax, jax.numpy as jnp
        import numpy as np
        u = jnp.einsum('btd,de->bte', x, W_in) + b_in
        A = -jnp.exp(log_A)
        b = u * B_vec
        a = jnp.broadcast_to(A, b.shape)

        def combine(e1, e2):
            a1, b1 = e1
            a2, b2 = e2
            return (a1 * a2, b1 * a2 + b2)
        _, h_seq = jax.lax.associative_scan(combine, (a, b), axis=1)
        y = jnp.einsum('bts,sd->btd', h_seq, C)
        return y + x * D

    def _L1_ffn_ref(x, gate_w, expert_gate, expert_up, expert_down, shared_gate, shared_up, shared_down):
        import jax, jax.numpy as jnp
        import numpy as np
        TOP_K = 2

        def _ffn(x, gw, uw, dw):
            return jax.nn.silu(x @ gw.T) * (x @ uw.T) @ dw.T
        B, S, H = x.shape
        xf = x.reshape(-1, H)
        T = xf.shape[0]
        E = expert_gate.shape[0]
        shared = _ffn(xf, shared_gate, shared_up, shared_down)
        logits = xf @ gate_w.T
        probs = jax.nn.softmax(logits, axis=-1)
        topw, topi = jax.lax.top_k(probs, TOP_K)
        topw = topw / (topw.sum(-1, keepdims=True) + 1e-20)
        comb = jnp.zeros((T, E), xf.dtype).at[jnp.arange(T)[:, None], topi].add(topw)

        def body(acc, ws):
            gw, uw, dw, wcol = ws
            return (acc + _ffn(xf, gw, uw, dw) * wcol[:, None], None)
        routed, _ = jax.lax.scan(body, jnp.zeros_like(xf), (expert_gate, expert_up, expert_down, comb.T))
        return (shared + routed).reshape(B, S, H)
    x = L0_attn_x
    x = x + 0.5 * _L0_ffn_ref(_layernorm(x, axis=-1), L0_ffn_W_r, L0_ffn_W_k, L0_ffn_W_v, L0_ffn_mu_r, L0_ffn_mu_k)
    x = x + _L0_attn_ref(_layernorm(x, axis=-1), L0_attn_w_q, L0_attn_w_k, L0_attn_w_v, L0_attn_w_o)
    x = x + 0.5 * _L0_ffn_ref(_layernorm(x, axis=-1), L0_ffn_W_r, L0_ffn_W_k, L0_ffn_W_v, L0_ffn_mu_r, L0_ffn_mu_k)
    x = x + 0.5 * _L1_ffn_ref(_layernorm(x, axis=-1), L1_ffn_gate_w, L1_ffn_expert_gate, L1_ffn_expert_up, L1_ffn_expert_down, L1_ffn_shared_gate, L1_ffn_shared_up, L1_ffn_shared_down)
    x = x + _L1_attn_ref(_layernorm(x, axis=-1), L1_attn_W_in, L1_attn_b_in, L1_attn_log_A, L1_attn_B_vec, L1_attn_C, L1_attn_D)
    x = x + 0.5 * _L1_ffn_ref(_layernorm(x, axis=-1), L1_ffn_gate_w, L1_ffn_expert_gate, L1_ffn_expert_up, L1_ffn_expert_down, L1_ffn_shared_gate, L1_ffn_shared_up, L1_ffn_shared_down)
    return x

_drawn_inputs = setup_inputs


def setup_inputs(seed=0):
    import zlib

    import numpy as np

    out = dict(_drawn_inputs(seed))
    spreads = {'L1_attn_b_in': (0.0, 2.0), 'L1_attn_log_A': (-1.0, 0.6), 'L1_attn_D': (0.0, 0.1)}
    factors = {'L0_ffn_W_r': 3.146,
     'L0_ffn_mu_r': 6.183,
     'L1_ffn_gate_w': 8.0,
     'L1_ffn_expert_gate': 8.0,
     'L1_ffn_expert_up': 8.0,
     'L1_ffn_expert_down': 8.0,
     'L1_ffn_shared_gate': 5.918,
     'L1_ffn_shared_up': 5.873,
     'L1_ffn_shared_down': 5.898}
    for name, (base, spread) in spreads.items():
        noise = np.random.default_rng([zlib.crc32(name.encode()), seed]).standard_normal(out[name].shape)
        drawn = base * np.exp(spread * noise) if base else spread * noise
        out[name] = jnp.asarray(drawn.astype(out[name].dtype))
    for name, factor in factors.items():
        out[name] = (out[name] * factor).astype(out[name].dtype)
    return out
```

```python
from contextlib import ExitStack

import numpy as np

import concourse.bass as bass
from concourse import mybir

F32 = mybir.dt.float32
BF16 = mybir.dt.bfloat16
ALU = mybir.AluOpType
ACT = mybir.ActivationFunctionType
AX = mybir.AxisListType
ds = bass.ds

P = 128
D = 128
B, T = 4, 1024
NT = B * T // P
TB = T // P
CH = 512
TC = CH // P
EPS = 1e-5


class Core:

    def __init__(self, nc, ctx):
        self.nc, self.ctx = nc, ctx
        self.stage = ""

    def sb(self, name, shape, dt=F32, ctx=None):
        return (ctx or self.ctx).enter_context(self.nc.sbuf_tensor(self.stage + name, shape, dt))

    def ps(self, name, shape, ctx, dt=F32):
        return ctx.enter_context(self.nc.psum_tensor(self.stage + name, shape, dt))

    def sem(self, name):
        return self.ctx.enter_context(self.nc.semaphore(self.stage + name))

    def sems(self, names):
        return {n: self.sem(n) for n in names.split()}


def nth(n):
    return n + 1


def start(sp, sems):
    for sem in sems:
        sp.sem_inc(sem, 1)


class Link:

    def __init__(self, eng, sem, base=0):
        self.eng, self.sem, self.base, self.n = eng, sem, base, 0

    def __call__(self, ins):
        ins.then_inc(self.sem, 1)
        self.n += 1
        self.eng.wait_ge(self.sem, self.base + self.n)


def sum_up(k, dve, written, count, passed, first, n):
    dve.wait_ge(written, count)
    dve.sem_inc(passed, 1)
    for j in range(n):
        last = dve.bn_stats(k.stats[:, ds(first + j, 1), :].rearrange("p a s -> p (a s)"),
                            k.x[:, ds(first + j, 1), :].rearrange("p a d -> p (a d)"))
    return last


def rstd_stage(k):
    nc = k.nc
    var_ready, root_ready, dve_link = k.sem("var_ready"), k.sem("root_ready"), k.sem("dve_link")
    mean_even, squares_even, mean_odd, squares_odd = (k.stats[:, :, j] for j in (1, 2, 4, 5))
    with nc.Block() as block:
        @block.scalar
        def _(act):
            act.wait_ge(var_ready, 1)
            act.activation(k.root[:, :], k.var[:, :], ACT.Sqrt, bias=k.eps[:, 0:1]).then_inc(root_ready, 1)

        @block.vector
        def _(dve):
            link = Link(dve, dve_link)
            dve.tensor_tensor(k.mean[:, :], mean_even, mean_odd, ALU.add)
            dve.tensor_tensor(k.var[:, :], squares_even, squares_odd, ALU.add)
            link(dve.tensor_tensor(k.root[:, :], mean_even, mean_odd, ALU.subtract))
            dve.tensor_scalar(k.mean[:, :], k.mean[:, :], 0.5, None, ALU.mult)
            link(dve.scalar_tensor_tensor(k.rstd[:, :], k.root[:, :], 0.25, k.root[:, :], ALU.mult, ALU.mult))
            dve.scalar_tensor_tensor(k.var[:, :], k.var[:, :], 1.0 / D, k.rstd[:, :], ALU.mult, ALU.add)\
               .then_inc(var_ready, 1)
            dve.wait_ge(root_ready, 1)
            link(dve.reciprocal(k.rstd[:, :], k.root[:, :]))


def load_stage(k, x, weights):
    nc = k.nc
    x_tiles = x.rearrange("b (t p) d -> p (b t) d", p=P)
    x_in = [k.sem(f"x_in{b}") for b in range(B)]
    weights_in, consts, passed, summed = (k.sem(n) for n in ("weights_in", "consts", "passed", "summed"))
    with nc.Block() as block:
        @block.sync
        def _(sp):
            for b in range(B):
                sp.dma_start(k.x[:, b * TB:(b + 1) * TB, :], x_tiles[:, b * TB:(b + 1) * TB, :]).then_inc(x_in[b], 16)
            for dst, src in weights:
                sp.dma_start(dst, src).then_inc(weights_in, 16)
            sp.wait_ge(weights_in, 16 * len(weights))

        @block.gpsimd
        def _(pool):
            pool.memset(k.ident[:, :], 0.0).then_inc(consts, 1)
            pool.wait_ge(consts, 1)
            pool.affine_select(out=k.ident[:, :], in_=k.ident[:, :], compare_op=ALU.not_equal, fill=1.0,
                               base=0, pattern=[[-1, P]], channel_multiplier=1).then_inc(consts, 1)
            pool.memset(k.eps[:, :], EPS).then_inc(consts, 1)
            for e in range(E):
                pool.memset(k.rank[:, :, e:e + 1], float(E - e)).then_inc(consts, 1)
            pool.wait_ge(consts, 3 + E)

        @block.vector
        def _(dve):
            for b in range(B):
                last = sum_up(k, dve, x_in[b], 16, passed, b * TB, TB)
            last.then_inc(summed, 1)
            dve.wait_ge(summed, 1)


def normalise(k, dve, out, tile, n):
    for j in range(n):
        last = dve.tensor_scalar(out[:, j, :], k.x[:, ds(tile + j, 1), :].rearrange("p a d -> p (a d)"),
                                 k.mean[:, ds(tile + j, 1)],
                                 k.rstd[:, ds(tile + j, 1)], ALU.subtract, ALU.mult)
    return last


def turn(k, pe, out, tiles, n):
    for j in range(n):
        last = pe.transpose(out[:, j * P:(j + 1) * P], tiles[:, j, :], k.ident[:, :])
    return last


def token_mix_stage(k, w):
    nc = k.nc
    s = k.sems("xn_ready turned xt_ready mixed key_ready gate_ready value_ready relu_done squared tanh_done "
               "product_done added zeroed")
    (xn_ready, turned, xt_ready, mixed, key_ready, gate_ready, value_ready, relu_done, squared, tanh_done,
     product_done, added, zeroed) = s.values()
    dve_link, passed = k.sem("dve_link"), k.sem("passed")
    with ExitStack() as ctx:
        xn = [k.sb(f"xn{c}", [P, TC, D], ctx=ctx) for c in range(2)]
        xt = k.sb("xt", [P, 1 + T], ctx=ctx)
        diff = k.sb("diff", [P, CH], ctx=ctx)
        xr = [k.sb(f"xr{c}", [P, CH], ctx=ctx) for c in range(2)]
        xk = [k.sb(f"xk{c}", [P, CH], ctx=ctx) for c in range(2)]
        relu = [k.sb(f"relu{c}", [P, CH], ctx=ctx) for c in range(2)]
        act_k = [k.sb(f"act_k{c}", [P, CH], ctx=ctx) for c in range(2)]
        tanh = [k.sb(f"tanh{c}", [P, TC, D], ctx=ctx) for c in range(2)]
        prod = [k.sb(f"prod{c}", [P, TC, D], ctx=ctx) for c in range(2)]
        turn_ps = [k.ps(f"turn{c}", [P, CH], ctx) for c in range(2)]
        key_ps = [k.ps(f"key{c}", [P, CH], ctx) for c in range(2)]
        gate_ps = [k.ps(f"gate{c}", [P, TC, D], ctx) for c in range(2)]
        value_ps = [k.ps(f"value{c}", [P, TC, D], ctx) for c in range(2)]
        block = ctx.enter_context(nc.Block())

        @block.sync
        def _(sp):
            start(sp, s.values())

        @block.vector
        def _(dve):
            dve.memset(xt[:, 0:1], 0.0).then_inc(zeroed, 1)
            dve.wait_ge(zeroed, nth(1))
            links = 2
            with dve.Fori(0, B) as i:
                link = Link(dve, dve_link, i * links)
                for c in range(2):
                    dve.wait_ge(turned, nth(i * 2 + c))
                    normalise(k, dve, xn[c], i * TB + c * TC, TC).then_inc(xn_ready, 1)
                for c in range(2):
                    dve.wait_ge(xt_ready, nth(i * 2 + c + 1))
                    dve.wait_ge(mixed, nth(i * 2 + c))
                    link(dve.tensor_tensor(diff[:, :], xt[:, 1 + c * CH:1 + (c + 1) * CH], xt[:, c * CH:(c + 1) * CH],
                                           ALU.subtract))
                    dve.wait_ge(gate_ready, nth(i * 2 + c))
                    dve.scalar_tensor_tensor(xr[c][:, :], diff[:, :], w["mu_r"][:, 0:1], xt[:, c * CH:(c + 1) * CH],
                                             ALU.mult, ALU.add)
                    dve.scalar_tensor_tensor(xk[c][:, :], diff[:, :], w["mu_k"][:, 0:1], xt[:, c * CH:(c + 1) * CH],
                                             ALU.mult, ALU.add).then_inc(mixed, 1)
                for c in range(2):
                    chunk = k.x[:, ds(i * TB + c * TC, TC), :]
                    dve.wait_ge(tanh_done, nth(i * 2 + c + 1))
                    dve.wait_ge(value_ready, nth(i * 2 + c + 1))
                    dve.scalar_tensor_tensor(prod[c][:, :, :], tanh[c][:, :, :], 1.0, value_ps[c][:, :, :],
                                             ALU.add, ALU.mult).then_inc(product_done, 1)
                    dve.wait_ge(product_done, nth(i * 2 + c + 1))
                    dve.scalar_tensor_tensor(chunk, prod[c][:, :, :], 0.25, chunk, ALU.mult, ALU.add).then_inc(added, 1)
                    sum_up(k, dve, added, nth(i * 2 + c + 1), passed, i * TB + c * TC, TC)
                assert link.n == links, link.n

        @block.tensor
        def _(pe):
            with pe.Fori(0, B) as i:
                for c in range(2):
                    pe.wait_ge(xn_ready, nth(i * 2 + c + 1))
                    pe.wait_ge(xt_ready, nth(i * 2 + c))
                    turn(k, pe, turn_ps[c], xn[c], TC).then_inc(turned, 1)
                for c in range(2):
                    pe.wait_ge(mixed, nth(i * 2 + c + 1))
                    pe.wait_ge(relu_done, nth(i * 2 + c))
                    pe.matmul(key_ps[c][:, :], w["mix_k"][:, :], xk[c][:, :], start=True, stop=True).then_inc(key_ready, 1)
                    pe.wait_ge(tanh_done, nth(i * 2 + c))
                    for j in range(TC):
                        last = pe.matmul(gate_ps[c][:, j, :], xr[c][:, j * P:(j + 1) * P], w["mix_r"][:, :],
                                         start=True, stop=True)
                    last.then_inc(gate_ready, 1)
                for c in range(2):
                    pe.wait_ge(squared, nth(i * 2 + c + 1))
                    pe.wait_ge(product_done, nth(i * 2 + c))
                    for j in range(TC):
                        last = pe.matmul(value_ps[c][:, j, :], act_k[c][:, j * P:(j + 1) * P], w["mix_v"][:, :],
                                         start=True, stop=True)
                    last.then_inc(value_ready, 1)

        @block.scalar
        def _(act):
            with act.Fori(0, B) as i:
                for c in range(2):
                    act.wait_ge(turned, nth(i * 2 + c + 1))
                    act.wait_ge(mixed, nth(i * 2))
                    act.activation(xt[:, 1 + c * CH:1 + (c + 1) * CH], turn_ps[c][:, :], ACT.Copy).then_inc(xt_ready, 1)
                for c in range(2):
                    act.wait_ge(key_ready, nth(i * 2 + c + 1))
                    act.wait_ge(value_ready, nth(i * 2 + c))
                    act.activation(relu[c][:, :], key_ps[c][:, :], ACT.Relu).then_inc(relu_done, 1)
                    act.wait_ge(relu_done, nth(i * 2 + c + 1))
                    act.activation(act_k[c][:, :], relu[c][:, :], ACT.Square).then_inc(squared, 1)
                    act.wait_ge(gate_ready, nth(i * 2 + c + 1))
                    act.wait_ge(product_done, nth(i * 2 + c))
                    act.activation(tanh[c][:, :, :], gate_ps[c][:, :, :], ACT.Tanh, scale=0.5).then_inc(tanh_done, 1)


H, HKV, HD = 16, 4, 8
G = H // HKV
U = B * HKV
SCALE = float(1.0 / np.sqrt(np.float32(HD)))
PARTS = 3
SPLIT = PARTS * PARTS * HD
AUG = SPLIT + 2
VW = 32
KT = T // P


def rope_tables():
    half = HD // 2
    inv = (np.float32(1.0) / np.float32(10000.0) ** (np.arange(half, dtype=np.float32) * np.float32(2.0) / np.float32(HD)))
    angle = np.arange(T, dtype=np.float32)[:, None] * inv.astype(np.float32)[None, :]
    cos, sin = np.cos(angle).T.astype(np.float32), np.sin(angle).T.astype(np.float32)
    return np.tile(np.concatenate([cos, cos]), (H, 1)), np.tile(np.concatenate([-sin, sin]), (H, 1))


def after(eng, sem, n):
    if not isinstance(n, int) or n > 0:
        eng.wait_ge(sem, nth(n))


def project_stage(k, w, qd, kd):
    nc = k.nc
    names = ("xn_ready turned xt_ready q_ready q_rotated q_split1 q_rest q_split2 q_split3 k_ready k_rotated "
             "k_split1 k_rest k_split2 k_split3 v_ready v_copied v_filled tables_in")
    s, dve_link = k.sems(names), k.sem("dve_link")
    q_out, k_out = [k.sem(f"q_out{c}") for c in range(2)], k.sem("k_out")
    cos_np, sin_np = rope_tables()
    tables = nc.inline_tensor(np.ascontiguousarray(np.stack([cos_np, sin_np])), name="rope_tables").ap()
    with ExitStack() as ctx:
        xn = [k.sb(f"xn{c}", [P, TC, D], ctx=ctx) for c in range(2)]
        xt = [k.sb(f"xt{c}", [P, CH], ctx=ctx) for c in range(2)]
        cos, sin = k.sb("cos", [P, T], ctx=ctx), k.sb("sin", [P, T], ctx=ctx)
        cos_k, sin_k = k.sb("cos_k", [2 * 32, CH], ctx=ctx), k.sb("sin_k", [2 * 32, CH], ctx=ctx)
        turn_cos, turn_sin, rot = (k.sb(n, [P, CH], ctx=ctx) for n in ("turn_cos", "turn_sin", "rot"))
        q_parts = [k.sb(f"q_parts{c}", [P, PARTS, CH], BF16, ctx) for c in range(2)]
        k_parts = k.sb("k_parts", [2 * 32, PARTS, CH], BF16, ctx)
        kcos, ksin, krot = (k.sb(n, [2 * 32, CH], ctx=ctx) for n in ("kcos", "ksin", "krot"))
        turn_ps = k.ps("turn", [P, CH], ctx)
        q_ps = [k.ps(f"q{c}", [P, CH], ctx) for c in range(2)]
        qs_ps = [k.ps(f"qs{c}", [P, CH], ctx) for c in range(2)]
        key_ps, keys_ps = k.ps("k", [2 * 32, CH], ctx), k.ps("ks", [2 * 32, CH], ctx)
        v_ps = k.ps("v", [P, TB, HKV * HD], ctx)
        block = ctx.enter_context(nc.Block())

        @block.sync
        def _(sp):
            start(sp, [*s.values(), *q_out, k_out])
            for dst, src in ((cos[:, :], tables[0]), (sin[:, :], tables[1]),
                             (cos_k[0:32, :], tables[0, 0:32, 0:CH]), (cos_k[32:64, :], tables[0, 0:32, CH:T]),
                             (sin_k[0:32, :], tables[1, 0:32, 0:CH]), (sin_k[32:64, :], tables[1, 0:32, CH:T])):
                sp.dma_start(dst, src).then_inc(s["tables_in"], 16)
            with sp.Fori(0, B) as i:
                for c in range(2):
                    sp.wait_ge(s["q_split3"], nth(i * 2 + c + 1))
                    for g in range(HKV):
                        dst = qd[ds(i * HKV + g, 1), :, :, c * CH:(c + 1) * CH].rearrange("a i r t -> r (a i) t")
                        sp.dma_start(dst, q_parts[c][g * 32:(g + 1) * 32, :, :]).then_inc(q_out[c], 16)
                sp.wait_ge(s["k_split3"], nth(i + 1))
                for c in range(2):
                    for g in range(HKV):
                        dst = kd[ds(i * HKV + g, 1), :, :, c * CH:(c + 1) * CH].rearrange("a i d t -> d (a i) t")
                        row = c * 32 + g * HD
                        sp.dma_start(dst, k_parts[row:row + HD, :, :]).then_inc(k_out, 16)
            for c in range(2):
                sp.wait_ge(q_out[c], nth(16 * HKV * B))
            sp.wait_ge(k_out, nth(16 * 2 * HKV * B))

        @block.gpsimd
        def _(pool):
            pool.memset(k.values[:, :, :, :], 0.0).then_inc(s["v_filled"], 1)
            pool.wait_ge(s["v_filled"], nth(1))
            pool.memset(k.values[:, :, :, HD:HD + 1], 1.0).then_inc(s["v_filled"], 1)
            pool.wait_ge(s["v_filled"], nth(2))

        @block.vector
        def _(dve):
            dve.wait_ge(s["tables_in"], nth(16 * 6))
            with dve.Fori(0, B) as i:
                link = Link(dve, dve_link, i * 3)
                for c in range(2):
                    dve.wait_ge(s["turned"], nth(i * 2 + c))
                    normalise(k, dve, xn[c], i * TB + c * TC, TC).then_inc(s["xn_ready"], 1)
                for c in range(2):
                    dve.wait_ge(s["q_ready"], nth(i * 2 + c + 1))
                    dve.wait_ge(s["q_split3"], nth(i * 2 + c))
                    dve.tensor_tensor(turn_cos[:, :], q_ps[c][:, :], cos[:, c * CH:(c + 1) * CH], ALU.mult)
                    link(dve.tensor_tensor(turn_sin[:, :], qs_ps[c][:, :], sin[:, c * CH:(c + 1) * CH], ALU.mult))
                    dve.tensor_tensor(rot[:, :], turn_cos[:, :], turn_sin[:, :], ALU.add).then_inc(s["q_rotated"], 1)
                    dve.wait_ge(s["q_split1"], nth(i * 2 + c + 1))
                    dve.tensor_tensor(turn_cos[:, :], rot[:, :], q_parts[c][:, 0, :], ALU.subtract).then_inc(s["q_rest"], 1)
                    dve.wait_ge(s["q_split2"], nth(i * 2 + c + 1))
                    dve.tensor_tensor(q_parts[c][:, 2, :], turn_cos[:, :], q_parts[c][:, 1, :], ALU.subtract)\
                       .then_inc(s["q_split3"], 1)
                dve.wait_ge(s["k_ready"], nth(i + 1))
                dve.wait_ge(s["k_split3"], nth(i))
                dve.tensor_tensor(kcos[:, :], key_ps[:, :], cos_k[:, :], ALU.mult)
                link(dve.tensor_tensor(ksin[:, :], keys_ps[:, :], sin_k[:, :], ALU.mult))
                dve.tensor_tensor(krot[:, :], kcos[:, :], ksin[:, :], ALU.add).then_inc(s["k_rotated"], 1)
                dve.wait_ge(s["k_split1"], nth(i + 1))
                dve.tensor_tensor(kcos[:, :], krot[:, :], k_parts[:, 0, :], ALU.subtract).then_inc(s["k_rest"], 1)
                dve.wait_ge(s["k_split2"], nth(i + 1))
                dve.tensor_tensor(k_parts[:, 2, :], kcos[:, :], k_parts[:, 1, :], ALU.subtract).then_inc(s["k_split3"], 1)

        @block.tensor
        def _(pe):
            with pe.Fori(0, B) as i:
                for c in range(2):
                    pe.wait_ge(s["xn_ready"], nth(i * 2 + c + 1))
                    pe.wait_ge(s["xt_ready"], nth(i * 2 + c))
                    turn(k, pe, turn_ps, xn[c], TC).then_inc(s["turned"], 1)
                for c in range(2):
                    pe.wait_ge(s["xt_ready"], nth(i * 2 + c + 1))
                    pe.wait_ge(s["q_rotated"], nth(i * 2 + c))
                    pe.matmul(q_ps[c][:, :], w["q"][:, :], xt[c][:, :], start=True, stop=True)
                    pe.matmul(qs_ps[c][:, :], w["q_swap"][:, :], xt[c][:, :], start=True, stop=True).then_inc(s["q_ready"], 1)
                pe.wait_ge(s["k_rotated"], nth(i))
                for c in range(2):
                    pe.matmul(key_ps[c * 32:(c + 1) * 32, :], w["k"][:, :], xt[c][:, :], start=True, stop=True)
                for c in range(2):
                    last = pe.matmul(keys_ps[c * 32:(c + 1) * 32, :], w["k_swap"][:, :], xt[c][:, :], start=True, stop=True)
                last.then_inc(s["k_ready"], 1)
                pe.wait_ge(s["v_copied"], nth(i))
                for c in range(2):
                    for j in range(TC):
                        last = pe.matmul(v_ps[:, c * TC + j, :], xt[c][:, j * P:(j + 1) * P], w["v"][:, :],
                                         start=True, stop=True)
                last.then_inc(s["v_ready"], 1)

        @block.scalar
        def _(act):
            act.wait_ge(s["v_filled"], nth(2))
            with act.Fori(0, B) as i:
                for c in range(2):
                    act.wait_ge(s["turned"], nth(i * 2 + c + 1))
                    act.wait_ge(s["v_ready"], nth(i))
                    act.activation(xt[c][:, :], turn_ps[:, :], ACT.Copy).then_inc(s["xt_ready"], 1)
                for c in range(2):
                    act.wait_ge(s["q_rotated"], nth(i * 2 + c + 1))
                    act.wait_ge(q_out[c], nth(i * (16 * HKV)))
                    act.activation(q_parts[c][:, 0, :], rot[:, :], ACT.Copy).then_inc(s["q_split1"], 1)
                    act.wait_ge(s["q_rest"], nth(i * 2 + c + 1))
                    act.activation(q_parts[c][:, 1, :], turn_cos[:, :], ACT.Copy).then_inc(s["q_split2"], 1)
                act.wait_ge(s["k_rotated"], nth(i + 1))
                act.wait_ge(k_out, nth(i * (16 * 2 * HKV)))
                act.activation(k_parts[:, 0, :], krot[:, :], ACT.Copy).then_inc(s["k_split1"], 1)
                act.wait_ge(s["k_rest"], nth(i + 1))
                act.activation(k_parts[:, 1, :], kcos[:, :], ACT.Copy).then_inc(s["k_split2"], 1)
                act.wait_ge(s["v_ready"], nth(i + 1))
                for g in range(HKV):
                    last = act.activation(k.values[:, ds(i * HKV + g, 1), :, 0:HD].rearrange("p a t d -> p (a t) d"),
                                          v_ps[:, :, g * HD:(g + 1) * HD], ACT.Copy)
                last.then_inc(s["v_copied"], 1)


def attention_stage(k, qd, kd):
    nc = k.nc
    s = k.sems("s1_full s1_max st_full exp_done pv_done o_copied o_turned o_scaled m_turned m_copied m_split "
               "v_ready den_ready ones_set")
    q1_in, q2_in, m_in = ([k.sem(f"{n}{j}") for j in range(2)] for n in ("q1_in", "q2_in", "m_in"))
    LOADS = PARTS * (1 + 2 * PARTS)
    HT = KT // 2
    with ExitStack() as ctx:
        q1 = [k.sb(f"q1{j}", [SPLIT, 2, G, CH], BF16, ctx) for j in range(2)]
        k1 = [k.sb(f"k1{j}", [SPLIT, T], BF16, ctx) for j in range(2)]
        q2 = [k.sb(f"q2{j}", [AUG, 2, G, CH], BF16, ctx) for j in range(2)]
        k2 = [k.sb(f"k2{j}", [AUG, T], BF16, ctx) for j in range(2)]
        v2 = [k.sb(f"v2{j}", [P, KT, VW], ctx=ctx) for j in range(2)]
        maxima = [k.sb(f"maxima{j}", [P, 2, G, HT], ctx=ctx) for j in range(2)]
        minus_m = k.sb("minus_m", [G * HT, 2, P], BF16, ctx)
        weights = [k.sb(f"weights{j}", [P, G, CH], ctx=ctx) for j in range(2)]
        o_sb = k.sb("o_sb", [P, CH], ctx=ctx)
        den = k.sb("den", [P, HT, G, 1], ctx=ctx)
        s1_ps = [k.ps(f"s1{j}", [P, T], ctx) for j in range(2)]
        st_ps = [k.ps(f"st{j}", [P, CH], ctx) for j in range(2)]
        pv_ps = k.ps("pv", [P, CH], ctx)
        small_ps = k.ps("small", [P, HT, G, VW], ctx)
        small_flat = small_ps[:, :, :, :].rearrange("p t g v -> p (t g v)")
        block = ctx.enter_context(nc.Block())

        def unit(i, n):
            return i * 2 + n

        def exists(i, n):
            return not isinstance(i, int) or 2 * i + n < U

        def run(eng, half_unit):
            half_unit(0, 0, 0, None)
            with eng.Fori(0, U // 2 - 1) as i:
                half_unit(i, 0, 1, (0, 0))
                half_unit(i, 1, 0, (0, 1))
                half_unit(i, 1, 1, (1, 0))
                half_unit(i, 2, 0, (1, 1))
            i = U // 2 - 1
            half_unit(i, 0, 1, (0, 0))
            half_unit(i, 1, 0, (0, 1))
            half_unit(i, 1, 1, (1, 0))

        @block.sync
        def _(sp):
            def load(q, kk, sem, i, n):
                u = unit(i, n)
                for a in range(PARTS):
                    sp.dma_start(kk[a * PARTS * HD:(a + 1) * PARTS * HD, :],
                                 kd[ds(u, 1), :, :, :].rearrange("a i d t -> (a i d) t")).then_inc(sem, 16)
                    for b in range(PARTS):
                        row = (a * PARTS + b) * HD
                        for half in range(2):
                            sp.dma_start(q[row:row + HD, half, :, :],
                                         qd[ds(u, 1), a, :, half * CH:(half + 1) * CH]
                                         .rearrange("a (r d) t -> d (a r) t", d=HD)).then_inc(sem, 16)

            def load1(i, n):
                load(q1[n % 2], k1[n % 2], q1_in[n % 2], i, n)

            def load2(i, n):
                load(q2[n % 2], k2[n % 2], q2_in[n % 2], i, n)

            def put_maxima(i, n, half):
                sp.wait_ge(s["m_split"], nth(unit(i, n) * 2 + half + 1))
                for part in range(2):
                    row = SPLIT + part
                    sp.dma_start(q2[n % 2][row:row + 1, half, :, :], minus_m[:, part, :])\
                      .then_inc(m_in[half], 16)

            def step(i, n):
                u = unit(i, n)
                if exists(i, n + 2):
                    sp.wait_ge(s["s1_full"], nth(u * 32 + 32))
                    load1(i, n + 2)
                if exists(i, n + 1):
                    after(sp, s["pv_done"], u * 16)
                    load2(i, n + 1)
                put_maxima(i, n, 1)
                if exists(i, n + 1):
                    put_maxima(i, n + 1, 0)

            start(sp, [*s.values(), *q1_in, *q2_in, *m_in])
            sp.wait_ge(s["ones_set"], nth(2))
            load1(0, 0)
            load2(0, 0)
            load1(0, 1)
            put_maxima(0, 0, 0)
            with sp.Fori(0, U // 2 - 1) as i:
                step(i, 0)
                step(i, 1)
            step(U // 2 - 1, 0)
            step(U // 2 - 1, 1)

        @block.gpsimd
        def _(pool):
            for j in range(2):
                pool.memset(k2[j][64:AUG, :], 1.0).then_inc(s["ones_set"], 1)
                pool.wait_ge(s["ones_set"], nth(j + 1))

            def copy_values(i, n):
                u = unit(i, n)
                if not (isinstance(i, int) and u == 0):
                    after(pool, s["pv_done"], (u - 1) * 16)
                pool.tensor_copy(v2[n % 2][:, :, :], k.values[:, ds(u, 1), :, :].rearrange("p a t v -> p (a t) v"))\
                    .then_inc(s["v_ready"], 1)

            copy_values(0, 0)
            with pool.Fori(0, U // 2 - 1) as i:
                copy_values(i, 1)
                copy_values(i, 2)
            copy_values(U // 2 - 1, 1)

        @block.tensor
        def _(pe):
            def pass1(i, n, half, m):
                step = half * 16 + m
                if not (isinstance(i, int) and unit(i, n) == 0 and step < 2):
                    after(pe, s["s1_max"], unit(i, n) * 32 + step - 1)
                t, r = m // G, m % G
                for j in range(2):
                    last = pe.matmul(s1_ps[m % 2][:, j * CH:(j + 1) * CH], q1[n % 2][:, half, r, t * P:(t + 1) * P],
                                     k1[n % 2][:, j * CH:(j + 1) * CH], start=True, stop=True)
                last.then_inc(s["s1_full"], 1)

            def turn_maxima(i, n, half, scaled):
                pe.wait_ge(s["s1_max"], nth(unit(i, n) * 32 + (half + 1) * 16))
                after(pe, s["o_scaled"], scaled)
                pe.transpose(small_flat[0:G * HT, 0:P], maxima[n % 2][:, half, :, :].rearrange("p g t -> p (g t)"),
                             k.ident[:, :]).then_inc(s["m_turned"], 1)

            def scores(i, n, half, kt, r):
                m = half * 32 + kt * 4 + r
                after(pe, s["exp_done"], unit(i, n) * 64 + m - 1)
                pe.matmul(st_ps[m % 2][:, :], k2[n % 2][:, kt * P:(kt + 1) * P],
                          q2[n % 2][:, half, r, :], start=True, stop=True).then_inc(s["st_full"], 1)

            def values(i, n, half, kt):
                u = unit(i, n)
                pe.wait_ge(s["exp_done"], nth(u * 64 + half * 32 + kt * 4 + 4))
                if kt == 0:
                    after(pe, s["o_copied"], u * 2 + half)
                for r in range(G):
                    last = pe.matmul(pv_ps[r * 32:(r + 1) * 32, :], v2[n % 2][:, kt, :], weights[kt % 2][:, r, :],
                                     start=(kt == 0), stop=(kt == KT - 1))
                last.then_inc(s["pv_done"], 1)

            def turn_sums(halves):
                pe.wait_ge(s["o_copied"], nth(halves))
                pe.wait_ge(s["m_split"], nth(halves + 1 if not isinstance(halves, int) else min(halves + 1, 2 * U)))
                after(pe, s["o_scaled"], halves - 1)
                for t in range(HT):
                    last = pe.transpose(small_flat[:, t * P:(t + 1) * P], o_sb[:, t * P:(t + 1) * P], k.ident[:, :])
                last.then_inc(s["o_turned"], 1)

            def half_unit(i, n, half, before):
                u, more = unit(i, n), exists(i, n + 1)
                if half == 0:
                    pe.wait_ge(q2_in[n % 2], nth((i + n // 2 + 1) * (16 * LOADS)))
                    pe.wait_ge(s["v_ready"], nth(u + 1))
                    if more:
                        pe.wait_ge(q1_in[(n + 1) % 2], nth((i + (n + 1) // 2 + 1) * (16 * LOADS)))
                pe.wait_ge(m_in[half], nth((u + 1) * 32))
                for kt in range(KT):
                    if kt == 3 and half == 0:
                        turn_maxima(i, n, 1, u * 2)
                    if kt == 3 and half == 1 and more:
                        turn_maxima(i, n + 1, 0, u * 2 + 1)
                    scores(i, n, half, kt, 0)
                    scores(i, n, half, kt, 1)
                    if kt:
                        values(i, n, half, kt - 1)
                    elif before:
                        values(i, *before, KT - 1)
                    scores(i, n, half, kt, 2)
                    scores(i, n, half, kt, 3)
                    if more:
                        pass1(i, n + 1, half, 2 * kt)
                        pass1(i, n + 1, half, 2 * kt + 1)
                    if kt == 1 and before:
                        turn_sums(u * 2 + half)

            pe.wait_ge(q1_in[0], nth(16 * LOADS))
            for half in range(2):
                for m in range(16):
                    pass1(0, 0, half, m)
                    if half == 1 and m == 2:
                        turn_maxima(0, 0, 0, 0)
            run(pe, half_unit)
            values(U // 2 - 1, 1, 1, KT - 1)
            turn_sums(2 * U)

        @block.vector
        def _(dve):
            def take_maximum(i, n, half, m):
                dve.wait_ge(s["s1_full"], nth(unit(i, n) * 32 + half * 16 + m + 1))
                dve.reduce_max(maxima[n % 2][:, half, m % G, m // G:m // G + 1], s1_ps[m % 2][:, :], AX.X)\
                   .then_inc(s["s1_max"], 1)

            def reuse_maxima(i, n):
                if not (isinstance(i, int) and 2 * i + n < 2):
                    after(dve, s["m_turned"], unit(i, n) * 2 - 2)

            def split_maxima(i, n, half):
                u = unit(i, n)
                dve.wait_ge(s["m_turned"], nth(u * 2 + half + 1))
                if half:
                    dve.wait_ge(m_in[0], nth((u + 1) * 32))
                else:
                    after(dve, m_in[1], u * 32)
                dve.tensor_scalar(minus_m[:, 0, :], small_flat[0:G * HT, 0:P], -1.0, None, ALU.mult).then_inc(s["m_copied"], 1)
                dve.wait_ge(s["m_copied"], nth(u * 2 + half + 1))
                dve.scalar_tensor_tensor(minus_m[:, 1, :], small_flat[0:G * HT, 0:P], -1.0, minus_m[:, 0, :],
                                         ALU.mult, ALU.subtract).then_inc(s["m_split"], 1)

            def copy_sums(halves):
                dve.wait_ge(s["pv_done"], nth(halves * KT))
                after(dve, s["o_turned"], halves - 1)
                dve.tensor_copy(o_sb[:, :], pv_ps[:, :]).then_inc(s["o_copied"], 1)

            def scale_sums(i, n, half):
                u = unit(i, n)
                dve.wait_ge(s["o_turned"], nth(u * 2 + half + 1))
                dve.reciprocal(den[:, :, :, :], small_ps[:, :, :, HD:HD + 1]).then_inc(s["den_ready"], 1)
                dve.wait_ge(s["den_ready"], nth(u * 2 + half + 1))
                out = k.attended[:, ds(u, 1), half * HT:(half + 1) * HT, :].rearrange("p a t (g d) -> p (a t) g d", d=HD)
                dve.tensor_tensor(out, small_ps[:, :, :, 0:HD], den[:, :, :, :].to_broadcast([P, HT, G, HD]), ALU.mult)\
                   .then_inc(s["o_scaled"], 1)

            def half_unit(i, n, half, before):
                more = exists(i, n + 1)
                if more and half == 0:
                    reuse_maxima(i, n + 1)
                if before:
                    copy_sums(unit(i, n) * 2 + half)
                for m in range(16):
                    if more:
                        take_maximum(i, n + 1, half, m)
                    if m == 4 and before:
                        scale_sums(i, *before)
                    if m == 9:
                        if half == 0:
                            split_maxima(i, n, 1)
                        elif more:
                            split_maxima(i, n + 1, 0)

            for half in range(2):
                for m in range(16):
                    take_maximum(0, 0, half, m)
                    if half == 1 and m == 7:
                        split_maxima(0, 0, 0)
            run(dve, half_unit)
            copy_sums(2 * U)
            scale_sums(U // 2 - 1, 1, 1)

        @block.scalar
        def _(act):
            def half_unit(i, n, half, before):
                u = unit(i, n)
                for kt in range(KT):
                    m = half * 8 + kt
                    after(act, s["pv_done"], u * 16 + m - 1)
                    for r in range(G):
                        act.wait_ge(s["st_full"], nth(u * 64 + m * 4 + r + 1))
                        act.activation(weights[kt % 2][:, r, :], st_ps[r % 2][:, :], ACT.Exp, scale=SCALE)\
                           .then_inc(s["exp_done"], 1)

            run(act, half_unit)


def attention_out_stage(k, w):
    nc = k.nc
    s, passed = k.sems("gathered turned at_ready out_ready added"), k.sem("passed")
    with ExitStack() as ctx:
        at_rows = [k.sb(f"rows{c}", [P, TC, D], ctx=ctx) for c in range(2)]
        at_cols = [k.sb(f"cols{c}", [P, CH], ctx=ctx) for c in range(2)]
        turn_ps = [k.ps(f"turn{c}", [P, CH], ctx) for c in range(2)]
        out_ps = [k.ps(f"out{c}", [P, TC, D], ctx) for c in range(2)]
        block = ctx.enter_context(nc.Block())

        @block.sync
        def _(sp):
            start(sp, s.values())

        @block.scalar
        def _(act):
            with act.Fori(0, B) as i:
                for c in range(2):
                    act.wait_ge(s["turned"], nth(i * 2 + c))
                    for g in range(HKV):
                        last = act.activation(at_rows[c][:, :, g * 32:(g + 1) * 32],
                                              k.attended[:, ds(i * HKV + g, 1), c * TC:(c + 1) * TC, :]
                                              .rearrange("p a t v -> p (a t) v"), ACT.Copy)
                    last.then_inc(s["gathered"], 1)
                for c in range(2):
                    act.wait_ge(s["turned"], nth(i * 2 + c + 1))
                    act.wait_ge(s["out_ready"], nth(i * 2 + c))
                    act.activation(at_cols[c][:, :], turn_ps[c][:, :], ACT.Copy).then_inc(s["at_ready"], 1)

        @block.tensor
        def _(pe):
            with pe.Fori(0, B) as i:
                for c in range(2):
                    pe.wait_ge(s["gathered"], nth(i * 2 + c + 1))
                    pe.wait_ge(s["at_ready"], nth(i * 2 + c))
                    turn(k, pe, turn_ps[c], at_rows[c], TC).then_inc(s["turned"], 1)
                for c in range(2):
                    pe.wait_ge(s["at_ready"], nth(i * 2 + c + 1))
                    pe.wait_ge(s["added"], nth(i * 2 + c))
                    for j in range(TC):
                        last = pe.matmul(out_ps[c][:, j, :], at_cols[c][:, j * P:(j + 1) * P], w["o"][:, :],
                                         start=True, stop=True)
                    last.then_inc(s["out_ready"], 1)

        @block.vector
        def _(dve):
            with dve.Fori(0, B) as i:
                for c in range(2):
                    chunk = k.x[:, ds(i * TB + c * TC, TC), :]
                    dve.wait_ge(s["out_ready"], nth(i * 2 + c + 1))
                    dve.tensor_tensor(chunk, out_ps[c][:, :, :], chunk, ALU.add).then_inc(s["added"], 1)
                    sum_up(k, dve, s["added"], nth(i * 2 + c + 1), passed, i * TB + c * TC, TC)


E = 8
F = 352
HID = [(0, 128), (128, 128), (256, 96)]


def route(k, dve, link, t, logits, shifted_ready, exp_ready, count):
    n = logits.shape[1]

    def wide(ap):
        return ap.to_broadcast([P, n, E])

    rank = k.rank[:, 0:n, :]
    link(dve.reduce_max(t["one"][:, :, :], logits, AX.X))
    dve.tensor_tensor(t["shifted"][:, :, :], logits, wide(t["one"][:, :, :]), ALU.subtract).then_inc(shifted_ready, 1)
    dve.wait_ge(exp_ready, nth(count))
    link(dve.reduce_sum(t["one"][:, :, :], t["prob"][:, :, :], AX.X))
    link(dve.reciprocal(t["two"][:, :, :], t["one"][:, :, :]))
    link(dve.tensor_tensor(t["prob"][:, :, :], t["prob"][:, :, :], wide(t["two"][:, :, :]), ALU.mult))

    def pick(values, top, hot):
        link(dve.reduce_max(top, values, AX.X))
        link(dve.tensor_tensor(hot, values, wide(top), ALU.is_equal))
        link(dve.tensor_tensor(t["shifted"][:, :, :], hot, rank, ALU.mult))
        link(dve.reduce_max(t["place"][:, :, :], t["shifted"][:, :, :], AX.X))
        link(dve.tensor_tensor(hot, rank, wide(t["place"][:, :, :]), ALU.is_equal))

    pick(t["prob"][:, :, :], t["one"][:, :, :], t["hot1"][:, :, :])
    link(dve.scalar_tensor_tensor(t["rest"][:, :, :], t["hot1"][:, :, :], -2.0, t["prob"][:, :, :], ALU.mult, ALU.add))
    pick(t["rest"][:, :, :], t["two"][:, :, :], t["hot2"][:, :, :])
    link(dve.tensor_tensor(t["hot1"][:, :, :], t["hot1"][:, :, :], t["hot2"][:, :, :], ALU.add))
    link(dve.scalar_tensor_tensor(t["one"][:, :, :], t["one"][:, :, :], 1e-20, t["two"][:, :, :], ALU.add, ALU.add))
    link(dve.reciprocal(t["two"][:, :, :], t["one"][:, :, :]))
    link(dve.scalar_tensor_tensor(t["hot1"][:, :, :], t["hot1"][:, :, :], 0.5, t["prob"][:, :, :], ALU.mult, ALU.mult))
    link(dve.tensor_tensor(t["comb"][:, :, :], t["hot1"][:, :, :], wide(t["two"][:, :, :]), ALU.mult))


ROUTE_LINKS = 20


def moe_stage(k, w):
    nc = k.nc
    s = k.sems("xn_ready turned xt_ready logits_ready shifted_ready exp_ready gate_ready silu_done hidden_done "
               "down_done added")
    passed, dve_link = k.sem("passed"), k.sem("dve_link")
    EXPERTS = E + 1
    with ExitStack() as ctx:
        xn = [k.sb(f"xn{c}", [P, TC, D], ctx=ctx) for c in range(2)]
        xt = [k.sb(f"xt{c}", [P, CH], ctx=ctx) for c in range(2)]
        silu = [k.sb(f"silu{j}", [P, CH], ctx=ctx) for j in range(2)]
        hidden = [[k.sb(f"hidden{j}{m}", [P, CH], ctx=ctx) for m in range(len(HID))] for j in range(2)]
        t = {n: k.sb(n, [P, TB, E], ctx=ctx) for n in "shifted prob rest hot1 hot2 comb".split()}
        t.update({n: k.sb(n, [P, TB, 1], ctx=ctx) for n in "one two place".split()})
        turn_ps = k.ps("turn", [P, CH], ctx)
        logits_ps = k.ps("logits", [P, TB, E], ctx)
        gate_ps = [k.ps(f"gate{j}", [P, CH], ctx) for j in range(2)]
        up_ps = [k.ps(f"up{j}", [P, CH], ctx) for j in range(2)]
        down_ps = [k.ps(f"down{j}", [P, TC, D], ctx) for j in range(2)]
        block = ctx.enter_context(nc.Block())
        @block.sync
        def _(sp):
            start(sp, s.values())

        STEPS = [(c, e) for c in range(2) for e in range(EXPERTS)]
        NS, NH = len(STEPS), len(STEPS) * len(HID)

        @block.vector
        def _(dve):
            links = ROUTE_LINKS
            with dve.Fori(0, B) as i:
                link = Link(dve, dve_link, i * links)
                for c in range(2):
                    dve.wait_ge(s["turned"], nth(i * 2 + c))
                    normalise(k, dve, xn[c], i * TB + c * TC, TC).then_inc(s["xn_ready"], 1)
                dve.wait_ge(s["logits_ready"], nth(i + 1))

                route(k, dve, link, t, logits_ps[:, :, :], s["shifted_ready"], s["exp_ready"], i + 1)

                def add(n):
                    c, e = STEPS[n]
                    dve.wait_ge(s["down_done"], nth(i * NS + n + 1))
                    if n:
                        dve.wait_ge(s["added"], nth(i * NS + n))
                    if e == E:
                        chunk = k.x[:, ds(i * TB + c * TC, TC), :]
                        last = dve.scalar_tensor_tensor(chunk, down_ps[n % 2][:, :, :], 0.5, chunk, ALU.mult, ALU.add)
                    else:
                        for j in range(TC):
                            tile = k.x[:, ds(i * TB + c * TC + j, 1), :].rearrange("p a d -> p (a d)")
                            last = dve.scalar_tensor_tensor(tile, down_ps[n % 2][:, j, :], t["comb"][:, c * TC + j, e:e + 1],
                                                            tile, ALU.mult, ALU.add)
                    last.then_inc(s["added"], 1)

                for n in range(NS):
                    for m, (_, width) in enumerate(HID):
                        q = n * len(HID) + m
                        dve.wait_ge(s["silu_done"], nth(i * NH + q + 1))
                        if m == 0:
                            after(dve, s["down_done"], i * NS + n - 1 if n else i * NS)
                        dve.tensor_tensor(hidden[n % 2][m][0:width, :], silu[q % 2][0:width, :], up_ps[q % 2][0:width, :],
                                          ALU.mult).then_inc(s["hidden_done"], 1)
                        if m == 1 and n:
                            add(n - 1)
                add(NS - 1)
                sum_up(k, dve, s["added"], nth(i * NS + NS), passed, i * TB, TB)
                assert link.n == links, link.n

        @block.tensor
        def _(pe):
            with pe.Fori(0, B) as i:
                for c in range(2):
                    pe.wait_ge(s["xn_ready"], nth(i * 2 + c + 1))
                    pe.wait_ge(s["xt_ready"], nth(i * 2 + c))
                    turn(k, pe, turn_ps, xn[c], TC).then_inc(s["turned"], 1)
                pe.wait_ge(s["xt_ready"], nth(i * 2 + 2))
                for j in range(TB):
                    last = pe.matmul(logits_ps[:, j, :], xt[j // TC][:, (j % TC) * P:(j % TC + 1) * P], w["router"][:, :],
                                     start=True, stop=True)
                last.then_inc(s["logits_ready"], 1)

                def up(n, m):
                    c, e = STEPS[n]
                    first, width = HID[m]
                    q = n * len(HID) + m
                    after(pe, s["hidden_done"], i * NH + (q - 1 if q > 1 else 0))
                    pe.matmul(gate_ps[q % 2][0:width, :], w["gate"][:, e, first:first + width], xt[c][:, :],
                              start=True, stop=True)
                    pe.matmul(up_ps[q % 2][0:width, :], w["up"][:, e, first:first + width], xt[c][:, :],
                              start=True, stop=True).then_inc(s["gate_ready"], 1)

                def down(n):
                    e = STEPS[n][1]
                    pe.wait_ge(s["hidden_done"], nth(i * NH + (n + 1) * len(HID)))
                    after(pe, s["added"], i * NS + (n - 1 if n > 1 else 0))
                    for j in range(TC):
                        for m, (_, width) in enumerate(HID):
                            last = pe.matmul(down_ps[n % 2][:, j, :], hidden[n % 2][m][0:width, j * P:(j + 1) * P],
                                             w["down"][0:width, e, m, :], start=(m == 0), stop=(m == len(HID) - 1))
                    last.then_inc(s["down_done"], 1)

                for n in range(NS):
                    up(n, 0)
                    if n:
                        down(n - 1)
                    up(n, 1)
                    up(n, 2)
                down(NS - 1)

        @block.scalar
        def _(act):
            with act.Fori(0, B) as i:
                for c in range(2):
                    act.wait_ge(s["turned"], nth(i * 2 + c + 1))
                    act.wait_ge(s["gate_ready"], nth(i * NH))
                    act.activation(xt[c][:, :], turn_ps[:, :], ACT.Copy).then_inc(s["xt_ready"], 1)
                act.wait_ge(s["shifted_ready"], nth(i + 1))
                act.activation(t["prob"][:, :, :], t["shifted"][:, :, :], ACT.Exp).then_inc(s["exp_ready"], 1)
                for q in range(NH):
                    width = HID[q % len(HID)][1]
                    act.wait_ge(s["gate_ready"], nth(i * NH + q + 1))
                    after(act, s["hidden_done"], i * NH + (q - 1 if q > 1 else 0))
                    act.activation(silu[q % 2][0:width, :], gate_ps[q % 2][0:width, :], ACT.Silu).then_inc(s["silu_done"], 1)


def recurrence_stage(k, w):
    nc = k.nc
    s = k.sems("xn_ready turned xt_ready input_ready driven scanned out_ready added exp_ready consts")
    passed = k.sem("passed")
    with ExitStack() as ctx:
        xn = [k.sb(f"xn{c}", [P, TC, D], ctx=ctx) for c in range(2)]
        xt = [k.sb(f"xt{c}", [P, CH], ctx=ctx) for c in range(2)]
        drive = [k.sb(f"drive{c}", [P, CH], ctx=ctx) for c in range(2)]
        state = [k.sb(f"state{c}", [P, CH], ctx=ctx) for c in range(2)]
        decay, one_decay = k.sb("decay", [P, CH], ctx=ctx), k.sb("one_decay", [P, 1], ctx=ctx)
        skip, bias = k.sb("skip", [P, D], ctx=ctx), k.sb("bias", [P, 1], ctx=ctx)
        turn_ps = [k.ps(f"turn{c}", [P, CH], ctx) for c in range(2)]
        in_ps = [k.ps(f"in{c}", [P, CH], ctx) for c in range(2)]
        out_ps = [k.ps(f"out{c}", [P, TC, D], ctx) for c in range(2)]
        block = ctx.enter_context(nc.Block())

        @block.sync
        def _(sp):
            start(sp, s.values())

        @block.vector
        def _(dve):
            dve.tensor_scalar(skip[:, :], k.ident[:, :], w["skip"][:, 0:1], None, ALU.mult)
            dve.tensor_tensor(bias[:, :], w["b_in"][:, :], w["b_vec"][:, :], ALU.mult)
            dve.memset(decay[:, :], -1.0).then_inc(s["consts"], 1)
            dve.wait_ge(s["consts"], nth(1))
            dve.wait_ge(s["exp_ready"], nth(1))
            dve.tensor_scalar(decay[:, :], decay[:, :], one_decay[:, 0:1], None, ALU.mult).then_inc(s["consts"], 1)
            dve.wait_ge(s["consts"], nth(2))
            with dve.Fori(0, B) as i:
                for c in range(2):
                    dve.wait_ge(s["turned"], nth(i * 2 + c))
                    normalise(k, dve, xn[c], i * TB + c * TC, TC).then_inc(s["xn_ready"], 1)
                for c in range(2):
                    dve.wait_ge(s["driven"], nth(i * 2 + c + 1))
                    dve.wait_ge(s["out_ready"], nth(i * 2 + c))
                    dve.wait_ge(s["scanned"], nth(i * 2 + c))
                    dve.tensor_tensor_scan(state[c][:, :], decay[:, :], drive[c][:, :],
                                           state[0][:, CH - 1:CH] if c else 0.0, ALU.mult, ALU.add)\
                       .then_inc(s["scanned"], 1)
                for c in range(2):
                    chunk = k.x[:, ds(i * TB + c * TC, TC), :]
                    dve.wait_ge(s["out_ready"], nth(i * 2 + c + 1))
                    dve.tensor_tensor(chunk, out_ps[c][:, :, :], chunk, ALU.add).then_inc(s["added"], 1)
                    sum_up(k, dve, s["added"], nth(i * 2 + c + 1), passed, i * TB + c * TC, TC)

        @block.tensor
        def _(pe):
            pe.wait_ge(s["consts"], nth(2))
            with pe.Fori(0, B) as i:
                for c in range(2):
                    pe.wait_ge(s["xn_ready"], nth(i * 2 + c + 1))
                    pe.wait_ge(s["xt_ready"], nth(i * 2 + c))
                    turn(k, pe, turn_ps[c], xn[c], TC).then_inc(s["turned"], 1)
                for c in range(2):
                    pe.wait_ge(s["xt_ready"], nth(i * 2 + c + 1))
                    pe.wait_ge(s["driven"], nth(i * 2 + c))
                    pe.matmul(in_ps[c][:, :], w["in"][:, :], xt[c][:, :], start=True, stop=True).then_inc(s["input_ready"], 1)
                for c in range(2):
                    pe.wait_ge(s["scanned"], nth(i * 2 + c + 1))
                    pe.wait_ge(s["added"], nth(i * 2 + c))
                    for j in range(TC):
                        pe.matmul(out_ps[c][:, j, :], state[c][:, j * P:(j + 1) * P], w["out"][:, :], start=True, stop=False)
                        last = pe.matmul(out_ps[c][:, j, :], xt[c][:, j * P:(j + 1) * P], skip[:, :], start=False, stop=True)
                    last.then_inc(s["out_ready"], 1)

        @block.scalar
        def _(act):
            act.activation(one_decay[:, :], w["log_a"][:, :], ACT.Exp).then_inc(s["exp_ready"], 1)
            act.wait_ge(s["consts"], nth(2))
            with act.Fori(0, B) as i:
                for c in range(2):
                    act.wait_ge(s["turned"], nth(i * 2 + c + 1))
                    act.wait_ge(s["out_ready"], nth(i * 2))
                    act.activation(xt[c][:, :], turn_ps[c][:, :], ACT.Copy).then_inc(s["xt_ready"], 1)
                for c in range(2):
                    act.wait_ge(s["input_ready"], nth(i * 2 + c + 1))
                    act.wait_ge(s["scanned"], nth(i * 2 + c))
                    act.activation(drive[c][:, :], in_ps[c][:, :], ACT.Identity, bias=bias[:, 0:1],
                                   scale=w["b_vec"][:, 0:1]).then_inc(s["driven"], 1)


def store_stage(k, out):
    nc = k.nc
    stored = k.sem("stored")
    out_tiles = out.rearrange("b (t p) d -> p (b t) d", p=P)
    with nc.Block() as block:
        @block.sync
        def _(sp):
            for b in range(B):
                sp.dma_start(out_tiles[:, b * TB:(b + 1) * TB, :], k.x[:, b * TB:(b + 1) * TB, :]).then_inc(stored, 16)
            sp.wait_ge(stored, 16 * B)


WEIGHTS = {
    "mix_r": [P, D], "mix_k": [P, D], "mix_v": [P, D], "mu_r": [P, 1], "mu_k": [P, 1],
    "q": [P, D], "q_swap": [P, D], "k": [P, HKV * HD], "k_swap": [P, HKV * HD], "v": [P, HKV * HD], "o": [P, D],
    "in": [P, D], "out": [P, D], "log_a": [P, 1], "b_in": [P, 1], "b_vec": [P, 1], "skip": [P, 1],
    "router": [P, E], "gate": [P, E + 1, F], "up": [P, E + 1, F], "down": [P, E + 1, 3, D],
}


def macaron_kernel(nc, x, sources, out):
    with ExitStack() as ctx:
        k = Core(nc, ctx)
        k.x = k.sb("x", [P, NT, D])
        k.mean, k.var, k.root, k.rstd = (k.sb(n, [P, NT]) for n in ("mean", "var", "root", "rstd"))
        k.stats = k.sb("stats", [P, NT, 6])
        k.ident, k.eps, k.rank = k.sb("ident", [P, P]), k.sb("eps", [P, 1]), k.sb("rank", [P, TB, E])
        w = {n: k.sb("w_" + n, shape) for n, shape in WEIGHTS.items()}
        qd = nc.dram_tensor("query_parts", (U, PARTS, G * HD, T), BF16).ap()
        kd = nc.dram_tensor("key_parts", (U, PARTS, HD, T), BF16).ap()

        def stage(name, build, *args):
            k.stage = name + "_"
            build(k, *args)

        stage("load", load_stage, x, [(w[n][:], sources[n]) for n in WEIGHTS])
        stage("norm1", rstd_stage)
        stage("mix1", token_mix_stage, w)
        stage("norm2", rstd_stage)
        with ExitStack() as attention:
            k.values, k.attended = (k.sb(n, [P, U, KT, VW], ctx=attention) for n in ("values", "attended"))
            stage("project", project_stage, w, qd, kd)
            stage("attend", attention_stage, qd, kd)
            stage("attended", attention_out_stage, w)
        stage("norm3", rstd_stage)
        stage("mix2", token_mix_stage, w)
        stage("norm4", rstd_stage)
        stage("moe1", moe_stage, w)
        stage("norm5", rstd_stage)
        stage("recur", recurrence_stage, w)
        stage("norm6", rstd_stage)
        stage("moe2", moe_stage, w)
        stage("store", store_stage, out)


def lay_out(a):
    def column(v):
        return v.reshape(D, 1)

    def swap(m, heads):
        return m.reshape(D, heads, 2, HD // 2)[:, :, ::-1].reshape(D, heads * HD)

    def by_feature(experts, shared):
        return np.concatenate([experts, shared[None]]).transpose(2, 0, 1)

    down = np.zeros((E + 1, 3 * P, D), np.float32)
    down[:, :F] = np.concatenate([a["L1_ffn_expert_down"], a["L1_ffn_shared_down"][None]]).transpose(0, 2, 1)
    return {
        "mix_r": a["L0_ffn_W_r"].T, "mix_k": a["L0_ffn_W_k"].T, "mix_v": a["L0_ffn_W_v"].T,
        "mu_r": column(a["L0_ffn_mu_r"]), "mu_k": column(a["L0_ffn_mu_k"]),
        "q": a["L0_attn_w_q"], "q_swap": swap(a["L0_attn_w_q"], H),
        "k": a["L0_attn_w_k"], "k_swap": swap(a["L0_attn_w_k"], HKV),
        "v": a["L0_attn_w_v"], "o": a["L0_attn_w_o"],
        "in": a["L1_attn_W_in"], "out": a["L1_attn_C"],
        "log_a": column(a["L1_attn_log_A"]), "b_in": column(a["L1_attn_b_in"]), "b_vec": column(a["L1_attn_B_vec"]),
        "skip": column(a["L1_attn_D"]), "router": a["L1_ffn_gate_w"].T,
        "gate": by_feature(a["L1_ffn_expert_gate"], a["L1_ffn_shared_gate"]),
        "up": by_feature(a["L1_ffn_expert_up"], a["L1_ffn_shared_up"]),
        "down": down.reshape(E + 1, 3, P, D).transpose(2, 0, 1, 3),
    }


def kernel(**inputs):
    import concourse.bacc as bacc
    from concourse.bass_utils import run_bass_kernel_spmd

    inputs = {n: np.asarray(v) for n, v in inputs.items()}
    nc = bacc.Bacc("TRN2", target_bir_lowering=False, num_devices=1)
    arrays = {"in_x": np.ascontiguousarray(inputs["L0_attn_x"])}
    arrays.update({"in_" + n: np.ascontiguousarray(v) for n, v in lay_out(inputs).items()})
    aps = {n: nc.dram_tensor(n, v.shape, F32, kind="ExternalInput").ap() for n, v in arrays.items()}
    out = nc.dram_tensor("out_x", (B, T, D), F32, kind="ExternalOutput").ap()
    macaron_kernel(nc, aps["in_x"], {n: aps["in_" + n] for n in WEIGHTS}, out)
    return run_bass_kernel_spmd(nc, [arrays], core_ids=[0]).results[0]["out_x"]
```

```python
from contextlib import ExitStack

import numpy as np

import concourse.bass as bass
from concourse import mybir

F32 = mybir.dt.float32
BF16 = mybir.dt.bfloat16
U32 = mybir.dt.uint32
ALU = mybir.AluOpType
ACT = mybir.ActivationFunctionType
AX = mybir.AxisListType
ds = bass.ds

P = 128
D = 128
B, T = 4, 1024
NT = B * T // P
TB = T // P
CH = 512
TC = CH // P
EPS = 1e-5


class Core:

    def __init__(self, nc, ctx):
        self.nc, self.ctx = nc, ctx
        self.stage, self.used = "", []

    def sb(self, name, shape, dt=F32, ctx=None):
        return (ctx or self.ctx).enter_context(self.nc.sbuf_tensor(self.stage + name, shape, dt))

    def ps(self, name, shape, ctx, dt=F32):
        return ctx.enter_context(self.nc.psum_tensor(self.stage + name, shape, dt))

    def sem(self, name):
        sem = self.nc.alloc_semaphore(name=self.stage + name)
        self.used.append(sem)
        return sem

    def sems(self, names):
        return {n: self.sem(n) for n in names.split()}


def nth(n):
    return n + 1


def start(sp, sems):
    for sem in sems:
        sp.sem_inc(sem, 1)


class Link:

    def __init__(self, eng, sem, base=0):
        self.eng, self.sem, self.base, self.n = eng, sem, base, 0

    def __call__(self, ins):
        ins.then_inc(self.sem, 1)
        self.n += 1
        self.eng.wait_ge(self.sem, self.base + self.n)


def sum_up(k, dve, written, count, passed, first, n):
    dve.wait_ge(written, count)
    dve.sem_inc(passed, 1)
    for j in range(n):
        last = dve.bn_stats(k.stats[:, ds(first + j, 1), :].rearrange("p a s -> p (a s)"),
                            k.x[:, ds(first + j, 1), :].rearrange("p a d -> p (a d)"))
    return last


def rstd_stage(k):
    nc = k.nc
    var_ready, root_ready, dve_link = k.sem("var_ready"), k.sem("root_ready"), k.sem("dve_link")
    mean_even, squares_even, mean_odd, squares_odd = (k.stats[:, :, j] for j in (1, 2, 4, 5))
    with nc.Block() as block:
        @block.scalar
        def _(act):
            act.wait_ge(var_ready, 1)
            act.activation(k.root[:, :], k.var[:, :], ACT.Sqrt, bias=k.eps[:, 0:1]).then_inc(root_ready, 1)

        @block.vector
        def _(dve):
            link = Link(dve, dve_link)
            dve.tensor_tensor(k.mean[:, :], mean_even, mean_odd, ALU.add)
            dve.tensor_tensor(k.var[:, :], squares_even, squares_odd, ALU.add)
            link(dve.tensor_tensor(k.root[:, :], mean_even, mean_odd, ALU.subtract))
            dve.tensor_scalar(k.mean[:, :], k.mean[:, :], 0.5, None, ALU.mult)
            link(dve.scalar_tensor_tensor(k.rstd[:, :], k.root[:, :], 0.25, k.root[:, :], ALU.mult, ALU.mult))
            dve.scalar_tensor_tensor(k.var[:, :], k.var[:, :], 1.0 / D, k.rstd[:, :], ALU.mult, ALU.add)\
               .then_inc(var_ready, 1)
            dve.wait_ge(root_ready, 1)
            link(dve.reciprocal(k.rstd[:, :], k.root[:, :]))


def recycle_stage(k):
    nc = k.nc
    numbers = sorted(sem.num for sem in k.used)
    with nc.Block() as block:
        @block.sync
        def _(sp):
            sp.sem_clear(range(numbers[0], numbers[-1] + 1))
    assert numbers == list(range(numbers[0], numbers[-1] + 1)), numbers
    for sem in k.used:
        nc.release_semaphore(sem)
    k.used.clear()


def load_stage(k, x, weights):
    nc = k.nc
    x_tiles = x.rearrange("b (t p) d -> p (b t) d", p=P)
    x_in = [k.sem(f"x_in{b}") for b in range(B)]
    weights_in, consts, passed, summed = (k.sem(n) for n in ("weights_in", "consts", "passed", "summed"))
    with nc.Block() as block:
        @block.sync
        def _(sp):
            for b in range(B):
                sp.dma_start(k.x[:, b * TB:(b + 1) * TB, :], x_tiles[:, b * TB:(b + 1) * TB, :]).then_inc(x_in[b], 16)
            for dst, src in weights:
                sp.dma_start(dst, src).then_inc(weights_in, 16)
            sp.wait_ge(weights_in, 16 * len(weights))

        @block.gpsimd
        def _(pool):
            pool.memset(k.ident[:, :], 0.0).then_inc(consts, 1)
            pool.wait_ge(consts, 1)
            pool.affine_select(out=k.ident[:, :], in_=k.ident[:, :], compare_op=ALU.not_equal, fill=1.0,
                               base=0, pattern=[[-1, P]], channel_multiplier=1).then_inc(consts, 1)
            pool.memset(k.eps[:, :], EPS).then_inc(consts, 1)
            pool.wait_ge(consts, 3)

        @block.vector
        def _(dve):
            for b in range(B):
                last = sum_up(k, dve, x_in[b], 16, passed, b * TB, TB)
            last.then_inc(summed, 1)
            dve.wait_ge(summed, 1)


def normalise(k, dve, out, tile, n):
    for j in range(n):
        last = dve.tensor_scalar(out[:, j, :], k.x[:, ds(tile + j, 1), :].rearrange("p a d -> p (a d)"),
                                 k.mean[:, ds(tile + j, 1)],
                                 k.rstd[:, ds(tile + j, 1)], ALU.subtract, ALU.mult)
    return last


def turn(k, pe, out, tiles, n):
    for j in range(n):
        last = pe.transpose(out[:, j * P:(j + 1) * P], tiles[:, j, :], k.ident[:, :])
    return last


def token_mix_stage(k, w):
    nc = k.nc
    s = k.sems("xn_ready turned xt_ready mixed key_ready gate_ready value_ready relu_done squared tanh_done "
               "product_done added zeroed")
    (xn_ready, turned, xt_ready, mixed, key_ready, gate_ready, value_ready, relu_done, squared, tanh_done,
     product_done, added, zeroed) = s.values()
    dve_link, passed = k.sem("dve_link"), k.sem("passed")
    with ExitStack() as ctx:
        xn = [k.sb(f"xn{c}", [P, TC, D], ctx=ctx) for c in range(2)]
        xt = k.sb("xt", [P, 1 + T], ctx=ctx)
        diff = k.sb("diff", [P, CH], ctx=ctx)
        xr = [k.sb(f"xr{c}", [P, CH], ctx=ctx) for c in range(2)]
        xk = [k.sb(f"xk{c}", [P, CH], ctx=ctx) for c in range(2)]
        relu = [k.sb(f"relu{c}", [P, CH], ctx=ctx) for c in range(2)]
        act_k = [k.sb(f"act_k{c}", [P, CH], ctx=ctx) for c in range(2)]
        tanh = [k.sb(f"tanh{c}", [P, TC, D], ctx=ctx) for c in range(2)]
        prod = [k.sb(f"prod{c}", [P, TC, D], ctx=ctx) for c in range(2)]
        turn_ps = [k.ps(f"turn{c}", [P, CH], ctx) for c in range(2)]
        key_ps = [k.ps(f"key{c}", [P, CH], ctx) for c in range(2)]
        gate_ps = [k.ps(f"gate{c}", [P, TC, D], ctx) for c in range(2)]
        value_ps = [k.ps(f"value{c}", [P, TC, D], ctx) for c in range(2)]
        block = ctx.enter_context(nc.Block())

        @block.sync
        def _(sp):
            start(sp, s.values())

        @block.vector
        def _(dve):
            dve.memset(xt[:, 0:1], 0.0).then_inc(zeroed, 1)
            dve.wait_ge(zeroed, nth(1))
            links = 2
            with dve.Fori(0, B) as i:
                link = Link(dve, dve_link, i * links)
                for c in range(2):
                    dve.wait_ge(turned, nth(i * 2 + c))
                    normalise(k, dve, xn[c], i * TB + c * TC, TC).then_inc(xn_ready, 1)
                for c in range(2):
                    dve.wait_ge(xt_ready, nth(i * 2 + c + 1))
                    dve.wait_ge(mixed, nth(i * 2 + c))
                    link(dve.tensor_tensor(diff[:, :], xt[:, 1 + c * CH:1 + (c + 1) * CH], xt[:, c * CH:(c + 1) * CH],
                                           ALU.subtract))
                    dve.wait_ge(gate_ready, nth(i * 2 + c))
                    dve.scalar_tensor_tensor(xr[c][:, :], diff[:, :], w["mu_r"][:, 0:1], xt[:, c * CH:(c + 1) * CH],
                                             ALU.mult, ALU.add)
                    dve.scalar_tensor_tensor(xk[c][:, :], diff[:, :], w["mu_k"][:, 0:1], xt[:, c * CH:(c + 1) * CH],
                                             ALU.mult, ALU.add).then_inc(mixed, 1)
                for c in range(2):
                    chunk = k.x[:, ds(i * TB + c * TC, TC), :]
                    dve.wait_ge(tanh_done, nth(i * 2 + c + 1))
                    dve.wait_ge(value_ready, nth(i * 2 + c + 1))
                    dve.scalar_tensor_tensor(prod[c][:, :, :], tanh[c][:, :, :], 1.0, value_ps[c][:, :, :],
                                             ALU.add, ALU.mult).then_inc(product_done, 1)
                    dve.wait_ge(product_done, nth(i * 2 + c + 1))
                    dve.scalar_tensor_tensor(chunk, prod[c][:, :, :], 0.25, chunk, ALU.mult, ALU.add).then_inc(added, 1)
                    sum_up(k, dve, added, nth(i * 2 + c + 1), passed, i * TB + c * TC, TC)
                assert link.n == links, link.n

        @block.tensor
        def _(pe):
            with pe.Fori(0, B) as i:
                for c in range(2):
                    pe.wait_ge(xn_ready, nth(i * 2 + c + 1))
                    pe.wait_ge(xt_ready, nth(i * 2 + c))
                    turn(k, pe, turn_ps[c], xn[c], TC).then_inc(turned, 1)
                for c in range(2):
                    pe.wait_ge(mixed, nth(i * 2 + c + 1))
                    pe.wait_ge(relu_done, nth(i * 2 + c))
                    pe.matmul(key_ps[c][:, :], w["mix_k"][:, :], xk[c][:, :], start=True, stop=True).then_inc(key_ready, 1)
                    pe.wait_ge(tanh_done, nth(i * 2 + c))
                    for j in range(TC):
                        last = pe.matmul(gate_ps[c][:, j, :], xr[c][:, j * P:(j + 1) * P], w["mix_r"][:, :],
                                         start=True, stop=True)
                    last.then_inc(gate_ready, 1)
                for c in range(2):
                    pe.wait_ge(squared, nth(i * 2 + c + 1))
                    pe.wait_ge(product_done, nth(i * 2 + c))
                    for j in range(TC):
                        last = pe.matmul(value_ps[c][:, j, :], act_k[c][:, j * P:(j + 1) * P], w["mix_v"][:, :],
                                         start=True, stop=True)
                    last.then_inc(value_ready, 1)

        @block.scalar
        def _(act):
            with act.Fori(0, B) as i:
                for c in range(2):
                    act.wait_ge(turned, nth(i * 2 + c + 1))
                    act.wait_ge(mixed, nth(i * 2))
                    act.activation(xt[:, 1 + c * CH:1 + (c + 1) * CH], turn_ps[c][:, :], ACT.Copy).then_inc(xt_ready, 1)
                for c in range(2):
                    act.wait_ge(key_ready, nth(i * 2 + c + 1))
                    act.wait_ge(value_ready, nth(i * 2 + c))
                    act.activation(relu[c][:, :], key_ps[c][:, :], ACT.Relu).then_inc(relu_done, 1)
                    act.wait_ge(relu_done, nth(i * 2 + c + 1))
                    act.activation(act_k[c][:, :], relu[c][:, :], ACT.Square).then_inc(squared, 1)
                    act.wait_ge(gate_ready, nth(i * 2 + c + 1))
                    act.wait_ge(product_done, nth(i * 2 + c))
                    act.activation(tanh[c][:, :, :], gate_ps[c][:, :, :], ACT.Tanh, scale=0.5).then_inc(tanh_done, 1)


H, HKV, HD = 16, 4, 8
G = H // HKV
U = B * HKV
SCALE = float(1.0 / np.sqrt(np.float32(HD)))
PARTS = 3
SPLIT = PARTS * PARTS * HD
AUG = SPLIT + 2
VW = 32
KT = T // P


def rope_tables():
    half = HD // 2
    inv = (np.float32(1.0) / np.float32(10000.0) ** (np.arange(half, dtype=np.float32) * np.float32(2.0) / np.float32(HD)))
    angle = np.arange(T, dtype=np.float32)[:, None] * inv.astype(np.float32)[None, :]
    cos, sin = np.cos(angle).T.astype(np.float32), np.sin(angle).T.astype(np.float32)
    return np.tile(np.concatenate([cos, cos]), (H, 1)), np.tile(np.concatenate([-sin, sin]), (H, 1))


def after(eng, sem, n):
    if not isinstance(n, int) or n > 0:
        eng.wait_ge(sem, nth(n))


def project_stage(k, w, qd, kd):
    nc = k.nc
    names = ("xn_ready turned xt_ready q_ready q_rotated q_split1 q_rest q_split2 q_split3 k_ready k_rotated "
             "k_split1 k_rest k_split2 k_split3 v_ready v_copied v_filled tables_in")
    s, dve_link = k.sems(names), k.sem("dve_link")
    q_out, k_out = [k.sem(f"q_out{c}") for c in range(2)], k.sem("k_out")
    cos_np, sin_np = rope_tables()
    tables = nc.inline_tensor(np.ascontiguousarray(np.stack([cos_np, sin_np])), name="rope_tables").ap()
    with ExitStack() as ctx:
        xn = [k.sb(f"xn{c}", [P, TC, D], ctx=ctx) for c in range(2)]
        xt = [k.sb(f"xt{c}", [P, CH], ctx=ctx) for c in range(2)]
        cos, sin = k.sb("cos", [P, T], ctx=ctx), k.sb("sin", [P, T], ctx=ctx)
        cos_k, sin_k = k.sb("cos_k", [2 * 32, CH], ctx=ctx), k.sb("sin_k", [2 * 32, CH], ctx=ctx)
        turn_cos, turn_sin, rot = (k.sb(n, [P, CH], ctx=ctx) for n in ("turn_cos", "turn_sin", "rot"))
        q_parts = [k.sb(f"q_parts{c}", [P, PARTS, CH], BF16, ctx) for c in range(2)]
        k_parts = k.sb("k_parts", [2 * 32, PARTS, CH], BF16, ctx)
        kcos, ksin, krot = (k.sb(n, [2 * 32, CH], ctx=ctx) for n in ("kcos", "ksin", "krot"))
        turn_ps = k.ps("turn", [P, CH], ctx)
        q_ps = [k.ps(f"q{c}", [P, CH], ctx) for c in range(2)]
        qs_ps = [k.ps(f"qs{c}", [P, CH], ctx) for c in range(2)]
        key_ps, keys_ps = k.ps("k", [2 * 32, CH], ctx), k.ps("ks", [2 * 32, CH], ctx)
        v_ps = k.ps("v", [P, TB, HKV * HD], ctx)
        block = ctx.enter_context(nc.Block())

        @block.sync
        def _(sp):
            start(sp, [*s.values(), *q_out, k_out])
            for dst, src in ((cos[:, :], tables[0]), (sin[:, :], tables[1]),
                             (cos_k[0:32, :], tables[0, 0:32, 0:CH]), (cos_k[32:64, :], tables[0, 0:32, CH:T]),
                             (sin_k[0:32, :], tables[1, 0:32, 0:CH]), (sin_k[32:64, :], tables[1, 0:32, CH:T])):
                sp.dma_start(dst, src).then_inc(s["tables_in"], 16)
            with sp.Fori(0, B) as i:
                for c in range(2):
                    sp.wait_ge(s["q_split3"], nth(i * 2 + c + 1))
                    for g in range(HKV):
                        dst = qd[ds(i * HKV + g, 1), :, :, c * CH:(c + 1) * CH].rearrange("a i r t -> r (a i) t")
                        sp.dma_start(dst, q_parts[c][g * 32:(g + 1) * 32, :, :]).then_inc(q_out[c], 16)
                sp.wait_ge(s["k_split3"], nth(i + 1))
                for c in range(2):
                    for g in range(HKV):
                        dst = kd[ds(i * HKV + g, 1), :, :, c * CH:(c + 1) * CH].rearrange("a i d t -> d (a i) t")
                        row = c * 32 + g * HD
                        sp.dma_start(dst, k_parts[row:row + HD, :, :]).then_inc(k_out, 16)
            for c in range(2):
                sp.wait_ge(q_out[c], nth(16 * HKV * B))
            sp.wait_ge(k_out, nth(16 * 2 * HKV * B))

        @block.gpsimd
        def _(pool):
            pool.memset(k.values[:, :, :, :], 0.0).then_inc(s["v_filled"], 1)
            pool.wait_ge(s["v_filled"], nth(1))
            pool.memset(k.values[:, :, :, HD:HD + 1], 1.0).then_inc(s["v_filled"], 1)
            pool.wait_ge(s["v_filled"], nth(2))

        @block.vector
        def _(dve):
            dve.wait_ge(s["tables_in"], nth(16 * 6))
            with dve.Fori(0, B) as i:
                link = Link(dve, dve_link, i * 3)
                for c in range(2):
                    dve.wait_ge(s["turned"], nth(i * 2 + c))
                    normalise(k, dve, xn[c], i * TB + c * TC, TC).then_inc(s["xn_ready"], 1)
                for c in range(2):
                    dve.wait_ge(s["q_ready"], nth(i * 2 + c + 1))
                    dve.wait_ge(s["q_split3"], nth(i * 2 + c))
                    dve.tensor_tensor(turn_cos[:, :], q_ps[c][:, :], cos[:, c * CH:(c + 1) * CH], ALU.mult)
                    link(dve.tensor_tensor(turn_sin[:, :], qs_ps[c][:, :], sin[:, c * CH:(c + 1) * CH], ALU.mult))
                    dve.tensor_tensor(rot[:, :], turn_cos[:, :], turn_sin[:, :], ALU.add).then_inc(s["q_rotated"], 1)
                    dve.wait_ge(s["q_split1"], nth(i * 2 + c + 1))
                    dve.tensor_tensor(turn_cos[:, :], rot[:, :], q_parts[c][:, 0, :], ALU.subtract).then_inc(s["q_rest"], 1)
                    dve.wait_ge(s["q_split2"], nth(i * 2 + c + 1))
                    dve.tensor_tensor(q_parts[c][:, 2, :], turn_cos[:, :], q_parts[c][:, 1, :], ALU.subtract)\
                       .then_inc(s["q_split3"], 1)
                dve.wait_ge(s["k_ready"], nth(i + 1))
                dve.wait_ge(s["k_split3"], nth(i))
                dve.tensor_tensor(kcos[:, :], key_ps[:, :], cos_k[:, :], ALU.mult)
                link(dve.tensor_tensor(ksin[:, :], keys_ps[:, :], sin_k[:, :], ALU.mult))
                dve.tensor_tensor(krot[:, :], kcos[:, :], ksin[:, :], ALU.add).then_inc(s["k_rotated"], 1)
                dve.wait_ge(s["k_split1"], nth(i + 1))
                dve.tensor_tensor(kcos[:, :], krot[:, :], k_parts[:, 0, :], ALU.subtract).then_inc(s["k_rest"], 1)
                dve.wait_ge(s["k_split2"], nth(i + 1))
                dve.tensor_tensor(k_parts[:, 2, :], kcos[:, :], k_parts[:, 1, :], ALU.subtract).then_inc(s["k_split3"], 1)

        @block.tensor
        def _(pe):
            with pe.Fori(0, B) as i:
                for c in range(2):
                    pe.wait_ge(s["xn_ready"], nth(i * 2 + c + 1))
                    pe.wait_ge(s["xt_ready"], nth(i * 2 + c))
                    turn(k, pe, turn_ps, xn[c], TC).then_inc(s["turned"], 1)
                for c in range(2):
                    pe.wait_ge(s["xt_ready"], nth(i * 2 + c + 1))
                    pe.wait_ge(s["q_rotated"], nth(i * 2 + c))
                    pe.matmul(q_ps[c][:, :], w["q"][:, :], xt[c][:, :], start=True, stop=True)
                    pe.matmul(qs_ps[c][:, :], w["q_swap"][:, :], xt[c][:, :], start=True, stop=True).then_inc(s["q_ready"], 1)
                pe.wait_ge(s["k_rotated"], nth(i))
                for c in range(2):
                    pe.matmul(key_ps[c * 32:(c + 1) * 32, :], w["k"][:, :], xt[c][:, :], start=True, stop=True)
                for c in range(2):
                    last = pe.matmul(keys_ps[c * 32:(c + 1) * 32, :], w["k_swap"][:, :], xt[c][:, :], start=True, stop=True)
                last.then_inc(s["k_ready"], 1)
                pe.wait_ge(s["v_copied"], nth(i))
                for c in range(2):
                    for j in range(TC):
                        last = pe.matmul(v_ps[:, c * TC + j, :], xt[c][:, j * P:(j + 1) * P], w["v"][:, :],
                                         start=True, stop=True)
                last.then_inc(s["v_ready"], 1)

        @block.scalar
        def _(act):
            act.wait_ge(s["v_filled"], nth(2))
            with act.Fori(0, B) as i:
                for c in range(2):
                    act.wait_ge(s["turned"], nth(i * 2 + c + 1))
                    act.wait_ge(s["v_ready"], nth(i))
                    act.activation(xt[c][:, :], turn_ps[:, :], ACT.Copy).then_inc(s["xt_ready"], 1)
                for c in range(2):
                    act.wait_ge(s["q_rotated"], nth(i * 2 + c + 1))
                    act.wait_ge(q_out[c], nth(i * (16 * HKV)))
                    act.activation(q_parts[c][:, 0, :], rot[:, :], ACT.Copy).then_inc(s["q_split1"], 1)
                    act.wait_ge(s["q_rest"], nth(i * 2 + c + 1))
                    act.activation(q_parts[c][:, 1, :], turn_cos[:, :], ACT.Copy).then_inc(s["q_split2"], 1)
                act.wait_ge(s["k_rotated"], nth(i + 1))
                act.wait_ge(k_out, nth(i * (16 * 2 * HKV)))
                act.activation(k_parts[:, 0, :], krot[:, :], ACT.Copy).then_inc(s["k_split1"], 1)
                act.wait_ge(s["k_rest"], nth(i + 1))
                act.activation(k_parts[:, 1, :], kcos[:, :], ACT.Copy).then_inc(s["k_split2"], 1)
                act.wait_ge(s["v_ready"], nth(i + 1))
                for g in range(HKV):
                    last = act.activation(k.values[:, ds(i * HKV + g, 1), :, 0:HD].rearrange("p a t d -> p (a t) d"),
                                          v_ps[:, :, g * HD:(g + 1) * HD], ACT.Copy)
                last.then_inc(s["v_copied"], 1)


def attention_stage(k, qd, kd):
    nc = k.nc
    s = k.sems("s1_full s1_max st_full exp_done pv_done o_copied o_turned o_scaled m_turned m_copied m_split "
               "v_ready den_ready ones_set")
    q1_in, q2_in, m_in = ([k.sem(f"{n}{j}") for j in range(2)] for n in ("q1_in", "q2_in", "m_in"))
    LOADS = PARTS * (1 + 2 * PARTS)
    HT = KT // 2
    with ExitStack() as ctx:
        q1 = [k.sb(f"q1{j}", [SPLIT, 2, G, CH], BF16, ctx) for j in range(2)]
        k1 = [k.sb(f"k1{j}", [SPLIT, T], BF16, ctx) for j in range(2)]
        q2 = [k.sb(f"q2{j}", [AUG, 2, G, CH], BF16, ctx) for j in range(2)]
        k2 = [k.sb(f"k2{j}", [AUG, T], BF16, ctx) for j in range(2)]
        v2 = [k.sb(f"v2{j}", [P, KT, VW], ctx=ctx) for j in range(2)]
        maxima = [k.sb(f"maxima{j}", [P, 2, G, HT], ctx=ctx) for j in range(2)]
        minus_m = k.sb("minus_m", [G * HT, 2, P], BF16, ctx)
        weights = [k.sb(f"weights{j}", [P, G, CH], ctx=ctx) for j in range(2)]
        o_sb = k.sb("o_sb", [P, CH], ctx=ctx)
        den = k.sb("den", [P, HT, G, 1], ctx=ctx)
        s1_ps = [k.ps(f"s1{j}", [P, T], ctx) for j in range(2)]
        st_ps = [k.ps(f"st{j}", [P, CH], ctx) for j in range(2)]
        pv_ps = k.ps("pv", [P, CH], ctx)
        small_ps = k.ps("small", [P, HT, G, VW], ctx)
        small_flat = small_ps[:, :, :, :].rearrange("p t g v -> p (t g v)")
        block = ctx.enter_context(nc.Block())

        def unit(i, n):
            return i * 2 + n

        def exists(i, n):
            return not isinstance(i, int) or 2 * i + n < U

        def run(eng, half_unit):
            half_unit(0, 0, 0, None)
            with eng.Fori(0, U // 2 - 1) as i:
                half_unit(i, 0, 1, (0, 0))
                half_unit(i, 1, 0, (0, 1))
                half_unit(i, 1, 1, (1, 0))
                half_unit(i, 2, 0, (1, 1))
            i = U // 2 - 1
            half_unit(i, 0, 1, (0, 0))
            half_unit(i, 1, 0, (0, 1))
            half_unit(i, 1, 1, (1, 0))

        @block.sync
        def _(sp):
            def load(q, kk, sem, i, n):
                u = unit(i, n)
                for a in range(PARTS):
                    sp.dma_start(kk[a * PARTS * HD:(a + 1) * PARTS * HD, :],
                                 kd[ds(u, 1), :, :, :].rearrange("a i d t -> (a i d) t")).then_inc(sem, 16)
                    for b in range(PARTS):
                        row = (a * PARTS + b) * HD
                        for half in range(2):
                            sp.dma_start(q[row:row + HD, half, :, :],
                                         qd[ds(u, 1), a, :, half * CH:(half + 1) * CH]
                                         .rearrange("a (r d) t -> d (a r) t", d=HD)).then_inc(sem, 16)

            def load1(i, n):
                load(q1[n % 2], k1[n % 2], q1_in[n % 2], i, n)

            def load2(i, n):
                load(q2[n % 2], k2[n % 2], q2_in[n % 2], i, n)

            def put_maxima(i, n, half):
                sp.wait_ge(s["m_split"], nth(unit(i, n) * 2 + half + 1))
                for part in range(2):
                    row = SPLIT + part
                    sp.dma_start(q2[n % 2][row:row + 1, half, :, :], minus_m[:, part, :])\
                      .then_inc(m_in[half], 16)

            def step(i, n):
                u = unit(i, n)
                if exists(i, n + 2):
                    sp.wait_ge(s["s1_full"], nth(u * 32 + 32))
                    load1(i, n + 2)
                if exists(i, n + 1):
                    after(sp, s["pv_done"], u * 16)
                    load2(i, n + 1)
                put_maxima(i, n, 1)
                if exists(i, n + 1):
                    put_maxima(i, n + 1, 0)

            start(sp, [*s.values(), *q1_in, *q2_in, *m_in])
            sp.wait_ge(s["ones_set"], nth(2))
            load1(0, 0)
            load2(0, 0)
            load1(0, 1)
            put_maxima(0, 0, 0)
            with sp.Fori(0, U // 2 - 1) as i:
                step(i, 0)
                step(i, 1)
            step(U // 2 - 1, 0)
            step(U // 2 - 1, 1)

        @block.gpsimd
        def _(pool):
            for j in range(2):
                pool.memset(k2[j][64:AUG, :], 1.0).then_inc(s["ones_set"], 1)
                pool.wait_ge(s["ones_set"], nth(j + 1))

            def copy_values(i, n):
                u = unit(i, n)
                if not (isinstance(i, int) and u == 0):
                    after(pool, s["pv_done"], (u - 1) * 16)
                pool.tensor_copy(v2[n % 2][:, :, :], k.values[:, ds(u, 1), :, :].rearrange("p a t v -> p (a t) v"))\
                    .then_inc(s["v_ready"], 1)

            copy_values(0, 0)
            with pool.Fori(0, U // 2 - 1) as i:
                copy_values(i, 1)
                copy_values(i, 2)
            copy_values(U // 2 - 1, 1)

        @block.tensor
        def _(pe):
            def pass1(i, n, half, m):
                step = half * 16 + m
                if not (isinstance(i, int) and unit(i, n) == 0 and step < 2):
                    after(pe, s["s1_max"], unit(i, n) * 32 + step - 1)
                t, r = m // G, m % G
                for j in range(2):
                    last = pe.matmul(s1_ps[m % 2][:, j * CH:(j + 1) * CH], q1[n % 2][:, half, r, t * P:(t + 1) * P],
                                     k1[n % 2][:, j * CH:(j + 1) * CH], start=True, stop=True)
                last.then_inc(s["s1_full"], 1)

            def turn_maxima(i, n, half, scaled):
                pe.wait_ge(s["s1_max"], nth(unit(i, n) * 32 + (half + 1) * 16))
                after(pe, s["o_scaled"], scaled)
                pe.transpose(small_flat[0:G * HT, 0:P], maxima[n % 2][:, half, :, :].rearrange("p g t -> p (g t)"),
                             k.ident[:, :]).then_inc(s["m_turned"], 1)

            def scores(i, n, half, kt, r):
                m = half * 32 + kt * 4 + r
                after(pe, s["exp_done"], unit(i, n) * 64 + m - 1)
                pe.matmul(st_ps[m % 2][:, :], k2[n % 2][:, kt * P:(kt + 1) * P],
                          q2[n % 2][:, half, r, :], start=True, stop=True).then_inc(s["st_full"], 1)

            def values(i, n, half, kt):
                u = unit(i, n)
                pe.wait_ge(s["exp_done"], nth(u * 64 + half * 32 + kt * 4 + 4))
                if kt == 0:
                    after(pe, s["o_copied"], u * 2 + half)
                for r in range(G):
                    last = pe.matmul(pv_ps[r * 32:(r + 1) * 32, :], v2[n % 2][:, kt, :], weights[kt % 2][:, r, :],
                                     start=(kt == 0), stop=(kt == KT - 1))
                last.then_inc(s["pv_done"], 1)

            def turn_sums(halves):
                pe.wait_ge(s["o_copied"], nth(halves))
                pe.wait_ge(s["m_split"], nth(halves + 1 if not isinstance(halves, int) else min(halves + 1, 2 * U)))
                after(pe, s["o_scaled"], halves - 1)
                for t in range(HT):
                    last = pe.transpose(small_flat[:, t * P:(t + 1) * P], o_sb[:, t * P:(t + 1) * P], k.ident[:, :])
                last.then_inc(s["o_turned"], 1)

            def half_unit(i, n, half, before):
                u, more = unit(i, n), exists(i, n + 1)
                if half == 0:
                    pe.wait_ge(q2_in[n % 2], nth((i + n // 2 + 1) * (16 * LOADS)))
                    pe.wait_ge(s["v_ready"], nth(u + 1))
                    if more:
                        pe.wait_ge(q1_in[(n + 1) % 2], nth((i + (n + 1) // 2 + 1) * (16 * LOADS)))
                pe.wait_ge(m_in[half], nth((u + 1) * 32))
                for kt in range(KT):
                    if kt == 3 and half == 0:
                        turn_maxima(i, n, 1, u * 2)
                    if kt == 3 and half == 1 and more:
                        turn_maxima(i, n + 1, 0, u * 2 + 1)
                    scores(i, n, half, kt, 0)
                    scores(i, n, half, kt, 1)
                    if kt:
                        values(i, n, half, kt - 1)
                    elif before:
                        values(i, *before, KT - 1)
                    scores(i, n, half, kt, 2)
                    scores(i, n, half, kt, 3)
                    if more:
                        pass1(i, n + 1, half, 2 * kt)
                        pass1(i, n + 1, half, 2 * kt + 1)
                    if kt == 1 and before:
                        turn_sums(u * 2 + half)

            pe.wait_ge(q1_in[0], nth(16 * LOADS))
            for half in range(2):
                for m in range(16):
                    pass1(0, 0, half, m)
                    if half == 1 and m == 2:
                        turn_maxima(0, 0, 0, 0)
            run(pe, half_unit)
            values(U // 2 - 1, 1, 1, KT - 1)
            turn_sums(2 * U)

        @block.vector
        def _(dve):
            def take_maximum(i, n, half, m):
                dve.wait_ge(s["s1_full"], nth(unit(i, n) * 32 + half * 16 + m + 1))
                dve.reduce_max(maxima[n % 2][:, half, m % G, m // G:m // G + 1], s1_ps[m % 2][:, :], AX.X)\
                   .then_inc(s["s1_max"], 1)

            def reuse_maxima(i, n):
                if not (isinstance(i, int) and 2 * i + n < 2):
                    after(dve, s["m_turned"], unit(i, n) * 2 - 2)

            def split_maxima(i, n, half):
                u = unit(i, n)
                dve.wait_ge(s["m_turned"], nth(u * 2 + half + 1))
                if half:
                    dve.wait_ge(m_in[0], nth((u + 1) * 32))
                else:
                    after(dve, m_in[1], u * 32)
                dve.tensor_scalar(minus_m[:, 0, :], small_flat[0:G * HT, 0:P], -1.0, None, ALU.mult).then_inc(s["m_copied"], 1)
                dve.wait_ge(s["m_copied"], nth(u * 2 + half + 1))
                dve.scalar_tensor_tensor(minus_m[:, 1, :], small_flat[0:G * HT, 0:P], -1.0, minus_m[:, 0, :],
                                         ALU.mult, ALU.subtract).then_inc(s["m_split"], 1)

            def copy_sums(halves):
                dve.wait_ge(s["pv_done"], nth(halves * KT))
                after(dve, s["o_turned"], halves - 1)
                dve.tensor_copy(o_sb[:, :], pv_ps[:, :]).then_inc(s["o_copied"], 1)

            def scale_sums(i, n, half):
                u = unit(i, n)
                dve.wait_ge(s["o_turned"], nth(u * 2 + half + 1))
                dve.reciprocal(den[:, :, :, :], small_ps[:, :, :, HD:HD + 1]).then_inc(s["den_ready"], 1)
                dve.wait_ge(s["den_ready"], nth(u * 2 + half + 1))
                out = k.attended[:, ds(u, 1), half * HT:(half + 1) * HT, :].rearrange("p a t (g d) -> p (a t) g d", d=HD)
                dve.tensor_tensor(out, small_ps[:, :, :, 0:HD], den[:, :, :, :].to_broadcast([P, HT, G, HD]), ALU.mult)\
                   .then_inc(s["o_scaled"], 1)

            def half_unit(i, n, half, before):
                more = exists(i, n + 1)
                if more and half == 0:
                    reuse_maxima(i, n + 1)
                if before:
                    copy_sums(unit(i, n) * 2 + half)
                for m in range(16):
                    if more:
                        take_maximum(i, n + 1, half, m)
                    if m == 4 and before:
                        scale_sums(i, *before)
                    if m == 9:
                        if half == 0:
                            split_maxima(i, n, 1)
                        elif more:
                            split_maxima(i, n + 1, 0)

            for half in range(2):
                for m in range(16):
                    take_maximum(0, 0, half, m)
                    if half == 1 and m == 7:
                        split_maxima(0, 0, 0)
            run(dve, half_unit)
            copy_sums(2 * U)
            scale_sums(U // 2 - 1, 1, 1)

        @block.scalar
        def _(act):
            def half_unit(i, n, half, before):
                u = unit(i, n)
                for kt in range(KT):
                    m = half * 8 + kt
                    after(act, s["pv_done"], u * 16 + m - 1)
                    for r in range(G):
                        act.wait_ge(s["st_full"], nth(u * 64 + m * 4 + r + 1))
                        act.activation(weights[kt % 2][:, r, :], st_ps[r % 2][:, :], ACT.Exp, scale=SCALE)\
                           .then_inc(s["exp_done"], 1)

            run(act, half_unit)


def attention_out_stage(k, w):
    nc = k.nc
    s, passed = k.sems("gathered turned at_ready out_ready added"), k.sem("passed")
    with ExitStack() as ctx:
        at_rows = [k.sb(f"rows{c}", [P, TC, D], ctx=ctx) for c in range(2)]
        at_cols = [k.sb(f"cols{c}", [P, CH], ctx=ctx) for c in range(2)]
        turn_ps = [k.ps(f"turn{c}", [P, CH], ctx) for c in range(2)]
        out_ps = [k.ps(f"out{c}", [P, TC, D], ctx) for c in range(2)]
        block = ctx.enter_context(nc.Block())

        @block.sync
        def _(sp):
            start(sp, s.values())

        @block.scalar
        def _(act):
            with act.Fori(0, B) as i:
                for c in range(2):
                    act.wait_ge(s["turned"], nth(i * 2 + c))
                    for g in range(HKV):
                        last = act.activation(at_rows[c][:, :, g * 32:(g + 1) * 32],
                                              k.attended[:, ds(i * HKV + g, 1), c * TC:(c + 1) * TC, :]
                                              .rearrange("p a t v -> p (a t) v"), ACT.Copy)
                    last.then_inc(s["gathered"], 1)
                for c in range(2):
                    act.wait_ge(s["turned"], nth(i * 2 + c + 1))
                    act.wait_ge(s["out_ready"], nth(i * 2 + c))
                    act.activation(at_cols[c][:, :], turn_ps[c][:, :], ACT.Copy).then_inc(s["at_ready"], 1)

        @block.tensor
        def _(pe):
            with pe.Fori(0, B) as i:
                for c in range(2):
                    pe.wait_ge(s["gathered"], nth(i * 2 + c + 1))
                    pe.wait_ge(s["at_ready"], nth(i * 2 + c))
                    turn(k, pe, turn_ps[c], at_rows[c], TC).then_inc(s["turned"], 1)
                for c in range(2):
                    pe.wait_ge(s["at_ready"], nth(i * 2 + c + 1))
                    pe.wait_ge(s["added"], nth(i * 2 + c))
                    for j in range(TC):
                        last = pe.matmul(out_ps[c][:, j, :], at_cols[c][:, j * P:(j + 1) * P], w["o"][:, :],
                                         start=True, stop=True)
                    last.then_inc(s["out_ready"], 1)

        @block.vector
        def _(dve):
            with dve.Fori(0, B) as i:
                for c in range(2):
                    chunk = k.x[:, ds(i * TB + c * TC, TC), :]
                    dve.wait_ge(s["out_ready"], nth(i * 2 + c + 1))
                    dve.tensor_tensor(chunk, out_ps[c][:, :, :], chunk, ALU.add).then_inc(s["added"], 1)
                    sum_up(k, dve, s["added"], nth(i * 2 + c + 1), passed, i * TB + c * TC, TC)


E = 8
F = 352
HID = [(0, 128), (128, 128), (256, 96)]
CHOICES = 2
SLOT_TILES = CHOICES * NT + E
SLOTS = SLOT_TILES * P
ROW = D + 2
NOWHERE = 2 * B * T * CHOICES
FILL = 9


def moe_constants():
    def wide(v):
        return np.broadcast_to(np.asarray(v, np.float32), (P, *np.shape(v)))

    token = np.arange(NT)[None, :] * P + np.arange(P)[:, None]
    return {
        "rank": wide(np.broadcast_to(E - np.arange(E), (NT, E))),
        "before": np.triu(np.ones((P, P), np.float32), 1),
        "ones": np.ones((P, P), np.float32),
        "runs": wide(np.broadcast_to(np.arange(NT) > 0, (E, NT))),
        "tile_starts": wide(np.broadcast_to(P * np.arange(NT), (E, NT))),
        "slot_tile": wide(np.broadcast_to(np.arange(SLOT_TILES)[:, None], (SLOT_TILES, E))),
        "target": np.stack([token * CHOICES + c for c in range(CHOICES)], 1).astype(np.float32),
    }


CONSTANTS = {"rank": [P, NT, E], "before": [P, P], "ones": [P, P], "runs": [P, E, NT], "tile_starts": [P, E, NT],
             "slot_tile": [P, SLOT_TILES, E], "target": [P, CHOICES, NT]}


def fill_stage(k, buffers):
    nc = k.nc
    filler = k.sb("filler", [P, FILL, ROW])
    made = k.sem("made")
    with nc.Block() as block:
        @block.gpsimd
        def _(pool):
            pool.memset(filler[:, :, :], 0.0).then_inc(made, 1)
            pool.wait_ge(made, 1)
            pool.memset(filler[:, :, D:D + 1], float(NOWHERE)).then_inc(made, 1)

        @block.sync
        def _(sp):
            sp.wait_ge(made, 2)
            for buffer in buffers:
                parts = buffer.rearrange("(p m r) f -> p m (r f)", p=P, r=FILL)
                for m in range(SLOT_TILES // FILL):
                    sp.dma_start(parts[:, m, :], filler[:, :, :].rearrange("p r f -> p (r f)")).then_inc(k.filled, 16)


FILLED = 16 * SLOT_TILES // FILL


def route_stage(k, w, m):
    nc = k.nc
    s = {n: k.sem(n) for n in ("xn_ready turned xt_ready logits_ready copied shifted_ready exp_ready chosen counted "
                               "dve_link rows_ready").split()}
    CHUNKS = NT // TC
    with ExitStack() as ctx:
        t = {n: k.sb(n, [P, NT, E], ctx=ctx) for n in "shifted prob rest hot hot1 hot2 place_in".split()}
        t.update({n: k.sb(n, [P, NT, 1], ctx=ctx) for n in "one two place inv slot1 slot2".split()})
        totals, up_to, offset, over = (k.sb(n, [P, E, NT], ctx=ctx) for n in ("totals", "up_to", "offset", "over"))
        tiles, tiles_to, base = (k.sb(n, [P, E, 1], ctx=ctx) for n in ("tiles", "tiles_to", "base"))
        passed_by, expert = k.sb("passed_by", [P, SLOT_TILES, E], ctx=ctx), k.sb("expert", [P, SLOT_TILES, 1], ctx=ctx)
        turn_ps = [k.ps(f"turn{c}", [P, CH], ctx) for c in range(2)]
        logits_ps = k.ps("logits", [P, NT, E], ctx)
        before_ps, totals_ps = (k.ps(n, [P, NT, E], ctx) for n in ("before_ps", "totals_ps"))
        block = ctx.enter_context(nc.Block())

        @block.vector
        def _(dve):
            link = Link(dve, s["dve_link"])

            def wide(ap):
                return ap.to_broadcast([P, NT, E])

            for c in range(CHUNKS):
                for j in range(c * TC, (c + 1) * TC):
                    last = dve.tensor_scalar(m["rows"][0][:, j, 0:D], k.x[:, j, :], k.mean[:, j:j + 1], k.rstd[:, j:j + 1],
                                             ALU.subtract, ALU.mult)
                last.then_inc(s["xn_ready"], 1)
            dve.wait_ge(s["logits_ready"], 1)
            link(dve.reduce_max(t["one"][:, :, :], logits_ps[:, :, :], AX.X))
            dve.tensor_tensor(t["shifted"][:, :, :], logits_ps[:, :, :], wide(t["one"][:, :, :]), ALU.subtract)\
               .then_inc(s["shifted_ready"], 1)
            for c in range(CHOICES):
                dve.tensor_copy(m["rows"][c][:, :, D:D + 1], w["target"][:, c, :].rearrange("p (n a) -> p n a", a=1))
            dve.wait_ge(s["exp_ready"], 1)
            link(dve.reduce_sum(t["one"][:, :, :], t["prob"][:, :, :], AX.X))
            link(dve.reciprocal(t["two"][:, :, :], t["one"][:, :, :]))
            link(dve.tensor_tensor(t["prob"][:, :, :], t["prob"][:, :, :], wide(t["two"][:, :, :]), ALU.mult))

            def pick(values, top, hot):
                link(dve.reduce_max(top, values, AX.X))
                link(dve.tensor_tensor(hot, values, wide(top), ALU.is_equal))
                link(dve.tensor_tensor(t["shifted"][:, :, :], hot, w["rank"][:, :, :], ALU.mult))
                link(dve.reduce_max(t["place"][:, :, :], t["shifted"][:, :, :], AX.X))
                return dve.tensor_tensor(hot, w["rank"][:, :, :], wide(t["place"][:, :, :]), ALU.is_equal)

            link(pick(t["prob"][:, :, :], t["one"][:, :, :], t["hot1"][:, :, :]))
            link(dve.scalar_tensor_tensor(t["rest"][:, :, :], t["hot1"][:, :, :], -2.0, t["prob"][:, :, :], ALU.mult, ALU.add))
            link(pick(t["rest"][:, :, :], t["two"][:, :, :], t["hot2"][:, :, :]))
            dve.tensor_tensor(t["hot"][:, :, :], t["hot1"][:, :, :], t["hot2"][:, :, :], ALU.add).then_inc(s["chosen"], 1)
            link(dve.scalar_tensor_tensor(t["place"][:, :, :], t["one"][:, :, :], 1e-20, t["two"][:, :, :], ALU.add, ALU.add))
            link(dve.reciprocal(t["inv"][:, :, :], t["place"][:, :, :]))
            for c, top in enumerate(("one", "two")):
                dve.scalar_tensor_tensor(m["rows"][c][:, :, D + 1:D + 2], t[top][:, :, :], 0.5, t["inv"][:, :, :],
                                         ALU.mult, ALU.mult)
            dve.wait_ge(s["counted"], 1)
            link(dve.tensor_copy(totals[:, :, :], totals_ps[:, :, :].rearrange("p n e -> p e n")))
            flat = [a[:, :, :].rearrange("p e n -> p (e n)") for a in (up_to, w["runs"], totals)]
            link(dve.tensor_tensor_scan(flat[0], flat[1], flat[2], 0.0, ALU.mult, ALU.add))
            dve.tensor_tensor(offset[:, :, :], up_to[:, :, :], totals[:, :, :], ALU.subtract)
            link(dve.tensor_tensor(over[:, :, :], up_to[:, :, NT - 1:NT].to_broadcast([P, E, NT]), w["tile_starts"][:, :, :],
                                   ALU.is_gt))
            link(dve.reduce_sum(tiles[:, :, :], over[:, :, :], AX.X))
            link(dve.tensor_tensor_scan(tiles_to[:, :, 0], w["ones"][:, 0:E], tiles[:, :, 0], 0.0, ALU.mult, ALU.add))
            link(dve.tensor_tensor(base[:, :, :], tiles_to[:, :, :], tiles[:, :, :], ALU.subtract))
            link(dve.scalar_tensor_tensor(offset[:, :, :], base[:, :, :].to_broadcast([P, E, NT]), float(P), offset[:, :, :],
                                          ALU.mult, ALU.add))
            link(dve.tensor_tensor(t["place_in"][:, :, :], before_ps[:, :, :], offset[:, :, :].rearrange("p e n -> p n e"),
                                   ALU.add))
            for c, (hot, slot) in enumerate((("hot1", "slot1"), ("hot2", "slot2"))):
                link(dve.tensor_tensor(t[hot][:, :, :], t[hot][:, :, :], t["place_in"][:, :, :], ALU.mult))
                link(dve.reduce_sum(t[slot][:, :, :], t[hot][:, :, :], AX.X))
                dve.tensor_copy(m["slot"][c][:, :], t[slot][:, :, 0]).then_inc(s["rows_ready"], 1)
            link(dve.tensor_tensor(passed_by[:, :, :], w["slot_tile"][:, :, :],
                                   tiles_to[:, :, :].rearrange("p e a -> p a e").to_broadcast([P, SLOT_TILES, E]), ALU.is_ge))
            link(dve.reduce_sum(expert[:, :, :], passed_by[:, :, :], AX.X))
            dve.tensor_scalar(m["expert"][:, :], expert[:, :, 0], float(E - 1), None, ALU.min).then_inc(s["rows_ready"], 1)

        @block.tensor
        def _(pe):
            def logits(c):
                pe.wait_ge(s["xt_ready"], c + 1)
                for j in range(c * TC, (c + 1) * TC):
                    last = pe.matmul(logits_ps[:, j, :], m["xt"][:, j * P:(j + 1) * P], w["router"][:, :],
                                     start=True, stop=True)
                return last

            for c in range(CHUNKS):
                pe.wait_ge(s["xn_ready"], c + 1)
                if c > 1:
                    pe.wait_ge(s["xt_ready"], c - 1)
                for j in range(TC):
                    last = pe.transpose(turn_ps[c % 2][:, j * P:(j + 1) * P], m["rows"][0][:, c * TC + j, 0:D], k.ident[:, :])
                last.then_inc(s["turned"], 1)
                if c:
                    logits(c - 1)
            logits(CHUNKS - 1).then_inc(s["logits_ready"], 1)
            pe.wait_ge(s["chosen"], 1)
            pe.matmul(before_ps[:, :, :], w["before"][:, :], t["hot"][:, :, :], start=True, stop=True)
            pe.matmul(totals_ps[:, :, :], w["ones"][:, :], t["hot"][:, :, :], start=True, stop=True)\
              .then_inc(s["counted"], 1)

        @block.scalar
        def _(act):
            for c in range(CHUNKS):
                act.wait_ge(s["turned"], c + 1)
                act.activation(m["xt"][:, c * CH:(c + 1) * CH], turn_ps[c % 2][:, :], ACT.Copy).then_inc(s["xt_ready"], 1)
            act.wait_ge(s["shifted_ready"], 1)
            act.activation(t["prob"][:, :, :], t["shifted"][:, :, :], ACT.Exp).then_inc(s["exp_ready"], 1)
            for c in range(CHUNKS):
                tiles_of = slice(c * TC, (c + 1) * TC)
                act.activation(m["rows"][1][:, tiles_of, 0:D], m["rows"][0][:, tiles_of, 0:D], ACT.Copy)\
                   .then_inc(s["copied"], 1)


def shared_stage(k, w, m, slots, scattered):
    nc = k.nc
    s = k.sems("gate_ready silu_done hidden_done down_done added")
    with ExitStack() as ctx:
        silu = [k.sb(f"silu{j}", [P, CH], ctx=ctx) for j in range(2)]
        hidden = [[k.sb(f"hidden{j}{n}", [P, CH], ctx=ctx) for n in range(len(HID))] for j in range(2)]
        gate_ps = [k.ps(f"gate{j}", [P, CH], ctx) for j in range(2)]
        up_ps = [k.ps(f"up{j}", [P, CH], ctx) for j in range(2)]
        down_ps = [k.ps(f"down{j}", [P, TC, D], ctx) for j in range(2)]
        block = ctx.enter_context(nc.Block())
        NS, NH = 2, 2 * len(HID)

        @block.sync
        def _(sp):
            start(sp, s.values())

        @block.gpsimd
        def _(pool):
            pool.wait_ge(k.filled, k.fills)
            for n in range(NT):
                for c in range(CHOICES):
                    pool.indirect_dma_start(slots[:, :], bass.IndirectOffsetOnAxis(m["slot"][c][:, n:n + 1], 0),
                                            m["rows"][c][:, n, :], None).then_inc(scattered, 16)

        @block.vector
        def _(dve):
            with dve.Fori(0, B) as i:
                def add(n):
                    dve.wait_ge(s["down_done"], nth(i * NS + n + 1))
                    chunk = k.x[:, ds(i * TB + n * TC, TC), :]
                    dve.scalar_tensor_tensor(chunk, down_ps[n][:, :, :], 0.5, chunk, ALU.mult, ALU.add)\
                       .then_inc(s["added"], 1)

                for n in range(NS):
                    for h, (_, width) in enumerate(HID):
                        q = n * len(HID) + h
                        dve.wait_ge(s["silu_done"], nth(i * NH + q + 1))
                        if h == 0:
                            dve.wait_ge(s["down_done"], nth(i * NS + (n - 1 if n else 0)))
                        dve.tensor_tensor(hidden[n][h][0:width, :], silu[q % 2][0:width, :], up_ps[q % 2][0:width, :],
                                          ALU.mult).then_inc(s["hidden_done"], 1)
                        if h == 1 and n:
                            add(n - 1)
                add(NS - 1)

        @block.tensor
        def _(pe):
            with pe.Fori(0, B) as i:
                def up(n, h):
                    first, width = HID[h]
                    q = n * len(HID) + h
                    tokens = m["xt"][:, ds((i * NS + n) * CH, CH)]
                    after(pe, s["hidden_done"], i * NH + (q - 1 if q > 1 else 0))
                    pe.matmul(gate_ps[q % 2][0:width, :], w["gate"][:, E, first:first + width], tokens, start=True, stop=True)
                    pe.matmul(up_ps[q % 2][0:width, :], w["up"][:, E, first:first + width], tokens, start=True, stop=True)\
                      .then_inc(s["gate_ready"], 1)

                def down(n):
                    pe.wait_ge(s["hidden_done"], nth(i * NH + (n + 1) * len(HID)))
                    pe.wait_ge(s["added"], nth(i * NS + (n - 1 if n else 0)))
                    for j in range(TC):
                        for h, (_, width) in enumerate(HID):
                            last = pe.matmul(down_ps[n][:, j, :], hidden[n][h][0:width, j * P:(j + 1) * P],
                                             w["down"][0:width, E, h, :], start=(h == 0), stop=(h == len(HID) - 1))
                    last.then_inc(s["down_done"], 1)

                for n in range(NS):
                    up(n, 0)
                    if n:
                        down(n - 1)
                    up(n, 1)
                    up(n, 2)
                down(NS - 1)

        @block.scalar
        def _(act):
            with act.Fori(0, B) as i:
                for q in range(NH):
                    width = HID[q % len(HID)][1]
                    act.wait_ge(s["gate_ready"], nth(i * NH + q + 1))
                    after(act, s["hidden_done"], i * NH + (q - 1 if q > 1 else 0))
                    act.activation(silu[q % 2][0:width, :], gate_ps[q % 2][0:width, :], ACT.Silu).then_inc(s["silu_done"], 1)


def expert_stage(k, w, m, slots, results, scattered):
    nc = k.nc
    DEPTH = 8
    s = k.sems("turned xt_ready gate_ready silu_done hidden_done hidden_turned ht_ready down_done scaled")
    loaded, stored = ([k.sem(f"{n}{j}") for j in range(DEPTH)] for n in ("loaded", "stored"))
    pool_passed = k.sem("pool_passed")
    with ExitStack() as ctx:
        rows = [k.sb(f"rows{j}", [P, ROW], ctx=ctx) for j in range(DEPTH)]
        xt = [k.sb(f"xt{j}", [P, P], ctx=ctx) for j in range(DEPTH)]
        silu, hidden = ([k.sb(f"{n}{j}", [P, F], ctx=ctx) for j in range(2)] for n in ("silu", "hidden"))
        ht = [k.sb(f"ht{j}", [P, len(HID), P], ctx=ctx) for j in range(2)]
        index = [k.sb(f"index{j}", [P, 1], U32, ctx) for j in range(DEPTH)]
        y = [k.sb(f"y{j}", [P, D], ctx=ctx) for j in range(DEPTH)]
        gate_ps, up_ps = ([k.ps(f"{n}{j}", [P, F], ctx) for j in range(2)] for n in ("gate", "up"))
        turn_ps, ht_ps = k.ps("turn", [P, P], ctx), k.ps("ht", [P, len(HID), P], ctx)
        down_ps = [k.ps(f"down{j}", [P, D], ctx) for j in range(2)]
        block = ctx.enter_context(nc.Block())

        def within(n):
            return not isinstance(n, int) or 0 <= n < SLOT_TILES

        def steps(eng, step, ahead):
            for n in range(-ahead, DEPTH + 2):
                step(n, n % DEPTH)
            with eng.Fori(1, SLOT_TILES // DEPTH - 1) as i:
                for j in range(2, DEPTH + 2):
                    step(i * DEPTH + j, j % DEPTH)
            for n in range(SLOT_TILES - DEPTH + 2, SLOT_TILES + 2):
                step(n, n % DEPTH)

        def turn_of(n, j):
            return n // DEPTH if isinstance(n, int) else (n - j) // DEPTH

        @block.sync
        def _(sp):
            start(sp, [*s.values(), *loaded])
            sp.wait_ge(scattered, 16 * CHOICES * NT)

            def load(n, j):
                if within(n):
                    after(sp, s["scaled"], n - DEPTH + 1)
                    sp.dma_start(rows[j][:, :], slots[ds(n * P, P), :]).then_inc(loaded[j], 16)

            steps(sp, load, 0)

        @block.tensor
        def _(pe):
            experts = m["expert"]

            def step(n, j):
                if within(n):
                    e = pe.value_load(experts[0:1, ds(n, 1)], min_val=0, max_val=E - 1)
                    pe.wait_ge(s["xt_ready"], nth(n + 1))
                    after(pe, s["hidden_done"], n - 1)
                    for out, weights in ((gate_ps, w["gate"]), (up_ps, w["up"])):
                        last = pe.matmul(out[j % 2][:, :], xt[j][:, :], weights[:, ds(e, 1), :].rearrange("p a f -> p (a f)"),
                                         start=True, stop=True)
                    last.then_inc(s["gate_ready"], 1)
                if within(n - 1):
                    pe.wait_ge(s["hidden_done"], nth(n))
                    after(pe, s["ht_ready"], n - 1)
                    for h, (first, width) in enumerate(HID):
                        last = pe.transpose(ht_ps[0:width, h, :], hidden[(j - 1) % 2][:, first:first + width], k.ident[:, :])
                    last.then_inc(s["hidden_turned"], 1)
                if within(n + 2):
                    q = (j + 2) % DEPTH
                    pe.wait_ge(loaded[q], 16 * (turn_of(n + 2, q) + 1) + 1)
                    after(pe, s["xt_ready"], n + 2)
                    pe.transpose(turn_ps[:, :], rows[q][:, 0:D], k.ident[:, :]).then_inc(s["turned"], 1)
                if within(n - 2):
                    e = pe.value_load(experts[0:1, ds(n - 2, 1)], min_val=0, max_val=E - 1)
                    pe.wait_ge(s["ht_ready"], nth(n - 1))
                    after(pe, s["scaled"], n - 3)
                    for h, (_, width) in enumerate(HID):
                        last = pe.matmul(down_ps[j % 2][:, :], ht[j % 2][0:width, h, :],
                                         w["down"][0:width, ds(e, 1), h, :].rearrange("p a f -> p (a f)"),
                                         start=(h == 0), stop=(h == len(HID) - 1))
                    last.then_inc(s["down_done"], 1)

            steps(pe, step, 2)

        @block.scalar
        def _(act):
            def step(n, j):
                if within(n):
                    act.wait_ge(s["gate_ready"], nth(n + 1))
                    after(act, s["hidden_done"], n - 1)
                    act.activation(silu[j % 2][:, :], gate_ps[j % 2][:, :], ACT.Silu).then_inc(s["silu_done"], 1)
                if within(n - 1):
                    act.wait_ge(s["hidden_turned"], nth(n))
                    after(act, s["down_done"], n - 2)
                    q = (j - 1) % 2
                    act.activation(ht[q][:, 0:2, :], ht_ps[:, 0:2, :], ACT.Copy)
                    act.activation(ht[q][0:HID[2][1], 2, :], ht_ps[0:HID[2][1], 2, :], ACT.Copy).then_inc(s["ht_ready"], 1)

            steps(act, step, 0)

        @block.vector
        def _(dve):
            def step(n, j):
                if within(n):
                    dve.wait_ge(s["silu_done"], nth(n + 1))
                    after(dve, s["hidden_turned"], n - 1)
                    dve.tensor_tensor(hidden[j % 2][:, :], silu[j % 2][:, :], up_ps[j % 2][:, :], ALU.mult)\
                       .then_inc(s["hidden_done"], 1)
                if within(n + 2):
                    q = (j + 2) % DEPTH
                    dve.wait_ge(s["turned"], nth(n + 3))
                    after(dve, s["gate_ready"], n - 1)
                    dve.tensor_scalar(xt[q][:, :], turn_ps[:, :], 1.0, None, ALU.mult).then_inc(s["xt_ready"], 1)
                if within(n - 2):
                    q = (j - 2) % DEPTH
                    if not isinstance(n, int) or n - 2 >= DEPTH:
                        dve.wait_ge(stored[q], 16 * turn_of(n - 2, q))
                    dve.wait_ge(loaded[q], 16 * (turn_of(n - 2, q) + 1) + 1)
                    dve.tensor_scalar(index[q][:, :], rows[q][:, D:D + 1], 1.0, None, ALU.mult)
                    dve.wait_ge(s["down_done"], nth(n - 1))
                    dve.tensor_scalar(y[q][:, :], down_ps[j % 2][:, :], rows[q][:, D + 1:D + 2], None, ALU.mult)\
                       .then_inc(s["scaled"], 1)

            steps(dve, step, 2)

        @block.gpsimd
        def _(pool):
            def store(n, j):
                if within(n):
                    pool.wait_ge(s["scaled"], nth(n + 1))
                    pool.sem_inc(pool_passed, 1)
                    pool.indirect_dma_start(results[:, :], bass.IndirectOffsetOnAxis(index[j][:, :], 0), y[j][:, :], None,
                                            bounds_check=B * T * CHOICES - 1, oob_is_err=False).then_inc(stored[j], 16)

            steps(pool, store, 0)
            for q in range(DEPTH):
                pool.wait_ge(stored[q], 16 * (SLOT_TILES // DEPTH))


def combine_stage(k, results, sums):
    nc = k.nc
    fetched = [k.sem(f"fetched{b}") for b in range(B)]
    added, passed = k.sem("added"), k.sem("passed")
    pairs = results.rearrange("(n p c) d -> p n (c d)", p=P, c=CHOICES)
    with ExitStack() as ctx:
        both = k.sb("both", [P, NT, CHOICES * D], ctx=ctx)
        with nc.Block() as block:
            @block.sync
            def _(sp):
                for b in range(B):
                    tiles = slice(b * TB, (b + 1) * TB)
                    sp.dma_start(both[:, tiles, :], pairs[:, tiles, :]).then_inc(fetched[b], 16)

            @block.vector
            def _(dve):
                for b in range(B):
                    tiles = slice(b * TB, (b + 1) * TB)
                    dve.wait_ge(fetched[b], 16)
                    for c in range(CHOICES):
                        dve.tensor_tensor(k.x[:, tiles, :], k.x[:, tiles, :], both[:, tiles, c * D:(c + 1) * D], ALU.add)\
                           .then_inc(added, 1)
                        dve.wait_ge(added, b * CHOICES + c + 1)
                    if sums:
                        sum_up(k, dve, added, (b + 1) * CHOICES, passed, b * TB, TB)


def mixture(k, stage, name, w, slots, results, last):
    scattered = k.sem(name + "_scattered")
    k.fills += FILLED
    with ExitStack() as ctx:
        m = {"rows": [k.sb(f"{name}_rows{c}", [P, NT, ROW], ctx=ctx) for c in range(CHOICES)],
             "xt": k.sb(name + "_xt", [P, B * T], ctx=ctx),
             "slot": [k.sb(f"{name}_slot{c}", [P, NT], U32, ctx) for c in range(CHOICES)],
             "expert": k.sb(name + "_expert", [P, SLOT_TILES], U32, ctx)}
        stage(name + "_route", route_stage, w, m)
        stage(name + "_shared", shared_stage, w, m, slots, scattered)
        stage(name + "_experts", expert_stage, w, m, slots, results, scattered)
    stage(name + "_combine", combine_stage, results, not last)


def recurrence_stage(k, w):
    nc = k.nc
    s = k.sems("xn_ready turned xt_ready input_ready driven scanned out_ready added exp_ready consts")
    passed = k.sem("passed")
    with ExitStack() as ctx:
        xn = [k.sb(f"xn{c}", [P, TC, D], ctx=ctx) for c in range(2)]
        xt = [k.sb(f"xt{c}", [P, CH], ctx=ctx) for c in range(2)]
        drive = [k.sb(f"drive{c}", [P, CH], ctx=ctx) for c in range(2)]
        state = [k.sb(f"state{c}", [P, CH], ctx=ctx) for c in range(2)]
        decay, one_decay = k.sb("decay", [P, CH], ctx=ctx), k.sb("one_decay", [P, 1], ctx=ctx)
        skip, bias = k.sb("skip", [P, D], ctx=ctx), k.sb("bias", [P, 1], ctx=ctx)
        turn_ps = [k.ps(f"turn{c}", [P, CH], ctx) for c in range(2)]
        in_ps = [k.ps(f"in{c}", [P, CH], ctx) for c in range(2)]
        out_ps = [k.ps(f"out{c}", [P, TC, D], ctx) for c in range(2)]
        block = ctx.enter_context(nc.Block())

        @block.sync
        def _(sp):
            start(sp, s.values())

        @block.vector
        def _(dve):
            dve.tensor_scalar(skip[:, :], k.ident[:, :], w["skip"][:, 0:1], None, ALU.mult)
            dve.tensor_tensor(bias[:, :], w["b_in"][:, :], w["b_vec"][:, :], ALU.mult)
            dve.memset(decay[:, :], -1.0).then_inc(s["consts"], 1)
            dve.wait_ge(s["consts"], nth(1))
            dve.wait_ge(s["exp_ready"], nth(1))
            dve.tensor_scalar(decay[:, :], decay[:, :], one_decay[:, 0:1], None, ALU.mult).then_inc(s["consts"], 1)
            dve.wait_ge(s["consts"], nth(2))
            with dve.Fori(0, B) as i:
                for c in range(2):
                    dve.wait_ge(s["turned"], nth(i * 2 + c))
                    normalise(k, dve, xn[c], i * TB + c * TC, TC).then_inc(s["xn_ready"], 1)
                for c in range(2):
                    dve.wait_ge(s["driven"], nth(i * 2 + c + 1))
                    dve.wait_ge(s["out_ready"], nth(i * 2 + c))
                    dve.wait_ge(s["scanned"], nth(i * 2 + c))
                    dve.tensor_tensor_scan(state[c][:, :], decay[:, :], drive[c][:, :],
                                           state[0][:, CH - 1:CH] if c else 0.0, ALU.mult, ALU.add)\
                       .then_inc(s["scanned"], 1)
                for c in range(2):
                    chunk = k.x[:, ds(i * TB + c * TC, TC), :]
                    dve.wait_ge(s["out_ready"], nth(i * 2 + c + 1))
                    dve.tensor_tensor(chunk, out_ps[c][:, :, :], chunk, ALU.add).then_inc(s["added"], 1)
                    sum_up(k, dve, s["added"], nth(i * 2 + c + 1), passed, i * TB + c * TC, TC)

        @block.tensor
        def _(pe):
            pe.wait_ge(s["consts"], nth(2))
            with pe.Fori(0, B) as i:
                for c in range(2):
                    pe.wait_ge(s["xn_ready"], nth(i * 2 + c + 1))
                    pe.wait_ge(s["xt_ready"], nth(i * 2 + c))
                    turn(k, pe, turn_ps[c], xn[c], TC).then_inc(s["turned"], 1)
                for c in range(2):
                    pe.wait_ge(s["xt_ready"], nth(i * 2 + c + 1))
                    pe.wait_ge(s["driven"], nth(i * 2 + c))
                    pe.matmul(in_ps[c][:, :], w["in"][:, :], xt[c][:, :], start=True, stop=True).then_inc(s["input_ready"], 1)
                for c in range(2):
                    pe.wait_ge(s["scanned"], nth(i * 2 + c + 1))
                    pe.wait_ge(s["added"], nth(i * 2 + c))
                    for j in range(TC):
                        pe.matmul(out_ps[c][:, j, :], state[c][:, j * P:(j + 1) * P], w["out"][:, :], start=True, stop=False)
                        last = pe.matmul(out_ps[c][:, j, :], xt[c][:, j * P:(j + 1) * P], skip[:, :], start=False, stop=True)
                    last.then_inc(s["out_ready"], 1)

        @block.scalar
        def _(act):
            act.activation(one_decay[:, :], w["log_a"][:, :], ACT.Exp).then_inc(s["exp_ready"], 1)
            act.wait_ge(s["consts"], nth(2))
            with act.Fori(0, B) as i:
                for c in range(2):
                    act.wait_ge(s["turned"], nth(i * 2 + c + 1))
                    act.wait_ge(s["out_ready"], nth(i * 2))
                    act.activation(xt[c][:, :], turn_ps[c][:, :], ACT.Copy).then_inc(s["xt_ready"], 1)
                for c in range(2):
                    act.wait_ge(s["input_ready"], nth(i * 2 + c + 1))
                    act.wait_ge(s["scanned"], nth(i * 2 + c))
                    act.activation(drive[c][:, :], in_ps[c][:, :], ACT.Identity, bias=bias[:, 0:1],
                                   scale=w["b_vec"][:, 0:1]).then_inc(s["driven"], 1)


def store_stage(k, out):
    nc = k.nc
    stored = k.sem("stored")
    out_tiles = out.rearrange("b (t p) d -> p (b t) d", p=P)
    with nc.Block() as block:
        @block.sync
        def _(sp):
            for b in range(B):
                sp.dma_start(out_tiles[:, b * TB:(b + 1) * TB, :], k.x[:, b * TB:(b + 1) * TB, :]).then_inc(stored, 16)
            sp.wait_ge(stored, 16 * B)


WEIGHTS = {
    "mix_r": [P, D], "mix_k": [P, D], "mix_v": [P, D], "mu_r": [P, 1], "mu_k": [P, 1],
    "q": [P, D], "q_swap": [P, D], "k": [P, HKV * HD], "k_swap": [P, HKV * HD], "v": [P, HKV * HD], "o": [P, D],
    "in": [P, D], "out": [P, D], "log_a": [P, 1], "b_in": [P, 1], "b_vec": [P, 1], "skip": [P, 1],
    "router": [P, E], "gate": [P, E + 1, F], "up": [P, E + 1, F], "down": [P, E + 1, 3, D],
    **CONSTANTS,
}


def macaron_kernel(nc, x, sources, out):
    with ExitStack() as ctx:
        k = Core(nc, ctx)
        k.x = k.sb("x", [P, NT, D])
        k.mean, k.var, k.root, k.rstd = (k.sb(n, [P, NT]) for n in ("mean", "var", "root", "rstd"))
        k.stats = k.sb("stats", [P, NT, 6])
        k.ident, k.eps = k.sb("ident", [P, P]), k.sb("eps", [P, 1])
        k.filled, k.fills = ctx.enter_context(nc.semaphore("filled")), 0
        w = {n: k.sb("w_" + n, shape) for n, shape in WEIGHTS.items()}
        slots = [nc.dram_tensor(f"slots{j}", (SLOTS, ROW), F32).ap() for j in range(2)]
        results = [nc.dram_tensor(f"results{j}", (B * T * CHOICES, D), F32).ap() for j in range(2)]
        qd = nc.dram_tensor("query_parts", (U, PARTS, G * HD, T), BF16).ap()
        kd = nc.dram_tensor("key_parts", (U, PARTS, HD, T), BF16).ap()

        def stage(name, build, *args):
            k.stage = name + "_"
            build(k, *args)

        stage("load", load_stage, x, [(w[n][:], sources[n]) for n in WEIGHTS])
        stage("fill", fill_stage, slots)
        stage("norm1", rstd_stage)
        stage("mix1", token_mix_stage, w)
        stage("norm2", rstd_stage)
        with ExitStack() as attention:
            k.values, k.attended = (k.sb(n, [P, U, KT, VW], ctx=attention) for n in ("values", "attended"))
            stage("project", project_stage, w, qd, kd)
            stage("attend", attention_stage, qd, kd)
            stage("attended", attention_out_stage, w)
        stage("recycle", recycle_stage)
        stage("norm3", rstd_stage)
        stage("mix2", token_mix_stage, w)
        stage("norm4", rstd_stage)
        mixture(k, stage, "moe1", w, slots[0], results[0], False)
        stage("norm5", rstd_stage)
        stage("recur", recurrence_stage, w)
        stage("norm6", rstd_stage)
        mixture(k, stage, "moe2", w, slots[1], results[1], True)
        stage("store", store_stage, out)


def lay_out(a):
    def column(v):
        return v.reshape(D, 1)

    def swap(m, heads):
        return m.reshape(D, heads, 2, HD // 2)[:, :, ::-1].reshape(D, heads * HD)

    def by_feature(experts, shared):
        return np.concatenate([experts, shared[None]]).transpose(2, 0, 1)

    down = np.zeros((E + 1, 3 * P, D), np.float32)
    down[:, :F] = np.concatenate([a["L1_ffn_expert_down"], a["L1_ffn_shared_down"][None]]).transpose(0, 2, 1)
    return {
        "mix_r": a["L0_ffn_W_r"].T, "mix_k": a["L0_ffn_W_k"].T, "mix_v": a["L0_ffn_W_v"].T,
        "mu_r": column(a["L0_ffn_mu_r"]), "mu_k": column(a["L0_ffn_mu_k"]),
        "q": a["L0_attn_w_q"], "q_swap": swap(a["L0_attn_w_q"], H),
        "k": a["L0_attn_w_k"], "k_swap": swap(a["L0_attn_w_k"], HKV),
        "v": a["L0_attn_w_v"], "o": a["L0_attn_w_o"],
        "in": a["L1_attn_W_in"], "out": a["L1_attn_C"],
        "log_a": column(a["L1_attn_log_A"]), "b_in": column(a["L1_attn_b_in"]), "b_vec": column(a["L1_attn_B_vec"]),
        "skip": column(a["L1_attn_D"]), "router": a["L1_ffn_gate_w"].T,
        "gate": by_feature(a["L1_ffn_expert_gate"], a["L1_ffn_shared_gate"]),
        "up": by_feature(a["L1_ffn_expert_up"], a["L1_ffn_shared_up"]),
        "down": down.reshape(E + 1, 3, P, D).transpose(2, 0, 1, 3),
        **moe_constants(),
    }


def kernel(**inputs):
    import concourse.bacc as bacc
    from concourse.bass_utils import run_bass_kernel_spmd

    inputs = {n: np.asarray(v) for n, v in inputs.items()}
    nc = bacc.Bacc("TRN2", target_bir_lowering=False, num_devices=1)
    arrays = {"in_x": np.ascontiguousarray(inputs["L0_attn_x"])}
    arrays.update({"in_" + n: np.ascontiguousarray(v) for n, v in lay_out(inputs).items()})
    aps = {n: nc.dram_tensor(n, v.shape, F32, kind="ExternalInput").ap() for n, v in arrays.items()}
    out = nc.dram_tensor("out_x", (B, T, D), F32, kind="ExternalOutput").ap()
    macaron_kernel(nc, aps["in_x"], {n: aps["in_" + n] for n in WEIGHTS}, out)
    return run_bass_kernel_spmd(nc, [arrays], core_ids=[0]).results[0]["out_x"]
```

```python
from contextlib import ExitStack

import numpy as np

import concourse.bass as bass
from concourse import mybir

F32 = mybir.dt.float32
BF16 = mybir.dt.bfloat16
U32 = mybir.dt.uint32
F32R = mybir.dt.float32r
ALU = mybir.AluOpType
ACT = mybir.ActivationFunctionType
AX = mybir.AxisListType
ds = bass.ds

P = 128
D = 128
B, T = 4, 1024
NT = B * T // P
TB = T // P
CH = 512
TC = CH // P
CHUNKS = NT // TC
EPS = 1e-5


class Core:

    def __init__(self, nc, ctx):
        self.nc, self.ctx = nc, ctx
        self.stage, self.used = "", []

    def sb(self, name, shape, dt=F32, ctx=None):
        return (ctx or self.ctx).enter_context(self.nc.sbuf_tensor(self.stage + name, shape, dt))

    def ps(self, name, shape, ctx, dt=F32):
        return ctx.enter_context(self.nc.psum_tensor(self.stage + name, shape, dt))

    def sem(self, name):
        sem = self.nc.alloc_semaphore(name=self.stage + name)
        self.used.append(sem)
        return sem

    def sems(self, names):
        return {n: self.sem(n) for n in names.split()}


def nth(n):
    return n + 1


def start(sp, sems):
    for sem in sems:
        sp.sem_inc(sem, 1)


class Link:

    def __init__(self, eng, sem, base=0):
        self.eng, self.sem, self.base, self.n = eng, sem, base, 0

    def __call__(self, ins):
        ins.then_inc(self.sem, 1)
        self.n += 1
        self.eng.wait_ge(self.sem, self.base + self.n)


class Factors:

    def __init__(self, k, name=""):
        self.k = k
        self.summed, self.var_ready, self.root_ready, self.link_sem = (
            k.sem(n + name) for n in ("summed", "var_ready", "root_ready", "factor_link"))
        self.link = None

    def variance(self, dve, last_sums, tiles, turn):
        k = self.k
        if not turn:
            self.link = Link(dve, self.link_sem)
        link = self.link
        mean, var, root, rstd = (a[:, tiles] for a in (k.mean, k.var, k.root, k.rstd))
        mean_even, squares_even, mean_odd, squares_odd = (k.stats[:, tiles, j] for j in (1, 2, 4, 5))
        last_sums.then_inc(self.summed, 1)
        dve.wait_ge(self.summed, turn + 1)
        dve.tensor_tensor(mean, mean_even, mean_odd, ALU.add)
        dve.tensor_tensor(var, squares_even, squares_odd, ALU.add)
        link(dve.tensor_tensor(root, mean_even, mean_odd, ALU.subtract))
        dve.tensor_scalar(mean, mean, 0.5, None, ALU.mult)
        link(dve.scalar_tensor_tensor(rstd, root, 0.25, root, ALU.mult, ALU.mult))
        dve.scalar_tensor_tensor(var, var, 1.0 / D, rstd, ALU.mult, ALU.add).then_inc(self.var_ready, 1)

    def root(self, act, tiles, turn):
        k = self.k
        act.wait_ge(self.var_ready, turn + 1)
        act.activation(k.root[:, tiles], k.var[:, tiles], ACT.Sqrt, bias=k.eps[:, 0:1]).then_inc(self.root_ready, 1)

    def finish(self, dve, tiles, turn):
        k = self.k
        dve.wait_ge(self.root_ready, turn + 1)
        self.link(dve.reciprocal(k.rstd[:, tiles], k.root[:, tiles]))
        self.link(dve.scalar_tensor_tensor(k.shift[:, tiles], k.mean[:, tiles], -1.0, k.rstd[:, tiles], ALU.mult, ALU.mult))

    def on_dve(self, dve, last_sums):
        self.variance(dve, last_sums, slice(0, NT), 0)
        self.finish(dve, slice(0, NT), 0)

    def on_act(self, act):
        self.root(act, slice(0, NT), 0)


def recycle_stage(k):
    nc = k.nc
    numbers = sorted(sem.num for sem in k.used)
    with nc.Block() as block:
        @block.sync
        def _(sp):
            sp.sem_clear(range(numbers[0], numbers[-1] + 1))
    assert numbers == list(range(numbers[0], numbers[-1] + 1)), numbers
    for sem in k.used:
        nc.release_semaphore(sem)
    k.used.clear()


def load_stage(k, x, weights):
    nc = k.nc
    x_tiles = x.rearrange("b (t p) d -> p (b t) d", p=P)
    x_in = [k.sem(f"x_in{b}") for b in range(B)]
    weights_in, consts, factors = k.sem("weights_in"), k.sem("consts"), Factors(k)
    with nc.Block() as block:
        @block.sync
        def _(sp):
            for b in range(B):
                sp.dma_start(k.x[:, b * TB:(b + 1) * TB, :], x_tiles[:, b * TB:(b + 1) * TB, :]).then_inc(x_in[b], 16)
            for dst, src in weights:
                sp.dma_start(dst, src).then_inc(weights_in, 16)
            sp.wait_ge(weights_in, 16 * len(weights))

        @block.gpsimd
        def _(pool):
            pool.memset(k.ident[:, :], 0.0).then_inc(consts, 1)
            pool.wait_ge(consts, 1)
            pool.affine_select(out=k.ident[:, :], in_=k.ident[:, :], compare_op=ALU.not_equal, fill=1.0,
                               base=0, pattern=[[-1, P]], channel_multiplier=1).then_inc(consts, 1)
            pool.memset(k.eps[:, :], EPS).then_inc(consts, 1)
            pool.memset(k.filler[:, :, :], 0.0).then_inc(consts, 1)
            pool.wait_ge(consts, 4)
            pool.memset(k.filler[:, :, D:D + 1], float(NOWHERE)).then_inc(consts, 1)
            pool.wait_ge(consts, 5)

        @block.vector
        def _(dve):
            for b in range(B):
                dve.wait_ge(x_in[b], 16)
                for j in range(b * TB, (b + 1) * TB):
                    last = dve.bn_stats(k.stats[:, j, :], k.x[:, j, :])
            factors.on_dve(dve, last)

        @block.scalar
        def _(act):
            act.wait_ge(consts, 5)
            factors.on_act(act)


def load_beside(k, sp, weights, buffers, weights_in):
    for dst, src in weights:
        sp.dma_start(dst, src).then_inc(weights_in, 16)
    for buffer in buffers:
        parts = buffer.rearrange("(p m r) f -> p m (r f)", p=P, r=FILL)
        for m in range(SLOT_TILES // FILL):
            sp.dma_start(parts[:, m, :], k.filler[:, :, :].rearrange("p r f -> p (r f)")).then_inc(k.filled, 16)
    sp.wait_ge(weights_in, 16 * len(weights))


def wait_if(eng, sem, n):
    if n > 0:
        eng.wait_ge(sem, n)


def chunk_tiles(n):
    return slice(n * TC, (n + 1) * TC)


def chunk_norm(k, act, out, n):
    for j in range(TC):
        tile = n * TC + j
        last = act.activation(out[:, j, :], k.x[:, tile, :], ACT.Identity, bias=k.shift[:, tile:tile + 1],
                              scale=k.rstd[:, tile:tile + 1])
    return last


def chunk_sums(k, dve, written, count, n):
    dve.wait_ge(written, count)
    for j in range(n * TC, (n + 1) * TC):
        last = dve.bn_stats(k.stats[:, j, :], k.x[:, j, :])
    return last


def turn(k, pe, out, tiles, n):
    for j in range(n):
        last = pe.transpose(out[:, j * P:(j + 1) * P], tiles[:, j, :], k.ident[:, :])
    return last


def token_mix_stage(k, w, weights=(), buffers=()):
    nc = k.nc
    s = {n: k.sem(n) for n in ("xn_ready turned xt_ready differed mixed key_ready gate_ready value_ready relu_done "
                               "squared tanh_done product_done added zeroed").split()}
    factors = Factors(k)
    with ExitStack() as ctx:
        xn = [k.sb(f"xn{c}", [P, TC, D], ctx=ctx) for c in range(2)]
        xt = [k.sb(f"xt{c}", [P, 1 + CH], ctx=ctx) for c in range(2)]
        diff = [k.sb(f"diff{c}", [P, CH], ctx=ctx) for c in range(2)]
        xr = [k.sb(f"xr{c}", [P, CH], ctx=ctx) for c in range(2)]
        xk = [k.sb(f"xk{c}", [P, CH], ctx=ctx) for c in range(2)]
        relu = [k.sb(f"relu{c}", [P, CH], ctx=ctx) for c in range(2)]
        act_k = [k.sb(f"act_k{c}", [P, CH], ctx=ctx) for c in range(2)]
        tanh = [k.sb(f"tanh{c}", [P, TC, D], ctx=ctx) for c in range(2)]
        prod = [k.sb(f"prod{c}", [P, TC, D], ctx=ctx) for c in range(2)]
        turn_ps = [k.ps(f"turn{c}", [P, CH], ctx) for c in range(2)]
        key_ps = [k.ps(f"key{c}", [P, CH], ctx) for c in range(2)]
        gate_ps = [k.ps(f"gate{c}", [P, TC, D], ctx) for c in range(2)]
        value_ps = [k.ps(f"value{c}", [P, TC, D], ctx) for c in range(2)]
        block = ctx.enter_context(nc.Block())

        if weights:
            @block.sync
            def _(sp):
                load_beside(k, sp, weights, buffers, k.sem("weights_in"))

        @block.gpsimd
        def _(pool):
            pool.memset(xt[0][:, 0:1], 0.0).then_inc(s["zeroed"], 1)
            pool.wait_ge(s["zeroed"], 1)
            for n in range(CHUNKS):
                pool.wait_ge(s["xt_ready"], n + 1)
                wait_if(pool, s["mixed"], n - 1)
                xt_n = xt[n % 2]
                pool.tensor_tensor(diff[n % 2][:, :], xt_n[:, 1:1 + CH], xt_n[:, 0:CH], ALU.subtract)\
                    .then_inc(s["differed"], 1)

        @block.vector
        def _(dve):
            for n in range(-1, CHUNKS + 1):
                if n + 1 < CHUNKS:
                    c = (n + 1) % 2
                    dve.wait_ge(s["differed"], n + 2)
                    wait_if(dve, s["gate_ready"], n)
                    for out, mu in ((xk, w["mu_k"]), (xr, w["mu_r"])):
                        last = dve.scalar_tensor_tensor(out[c][:, :], diff[c][:, :], mu[:, 0:1], xt[c][:, 0:CH], ALU.mult, ALU.add)
                    last.then_inc(s["mixed"], 1)
                if n > 0:
                    c, tiles = (n - 1) % 2, chunk_tiles(n - 1)
                    dve.wait_ge(s["tanh_done"], n)
                    dve.wait_ge(s["value_ready"], n)
                    wait_if(dve, s["added"], n - 2)
                    dve.scalar_tensor_tensor(prod[c][:, :, :], tanh[c][:, :, :], 1.0, value_ps[c][:, :, :],
                                             ALU.add, ALU.mult).then_inc(s["product_done"], 1)
                    dve.wait_ge(s["product_done"], n)
                    dve.scalar_tensor_tensor(k.x[:, tiles, :], prod[c][:, :, :], 0.25, k.x[:, tiles, :],
                                             ALU.mult, ALU.add).then_inc(s["added"], 1)
                    last = chunk_sums(k, dve, s["added"], n, n - 1)
            factors.on_dve(dve, last)

        @block.tensor
        def _(pe):
            for n in range(-2, CHUNKS + 1):
                if n + 2 < CHUNKS:
                    pe.wait_ge(s["xn_ready"], n + 3)
                    wait_if(pe, s["xt_ready"], n + 1)
                    turn(k, pe, turn_ps[n % 2], xn[n % 2], TC).then_inc(s["turned"], 1)
                if 0 <= n < CHUNKS:
                    c = n % 2
                    pe.wait_ge(s["mixed"], n + 1)
                    wait_if(pe, s["relu_done"], n - 1)
                    pe.matmul(key_ps[c][:, :], w["mix_k"][:, :], xk[c][:, :], start=True, stop=True)\
                      .then_inc(s["key_ready"], 1)
                    wait_if(pe, s["tanh_done"], n - 1)
                    for j in range(TC):
                        last = pe.matmul(gate_ps[c][:, j, :], xr[c][:, j * P:(j + 1) * P], w["mix_r"][:, :],
                                         start=True, stop=True)
                    last.then_inc(s["gate_ready"], 1)
                if n > 0:
                    c = (n - 1) % 2
                    pe.wait_ge(s["squared"], n)
                    wait_if(pe, s["product_done"], n - 2)
                    for j in range(TC):
                        last = pe.matmul(value_ps[c][:, j, :], act_k[c][:, j * P:(j + 1) * P], w["mix_v"][:, :],
                                         start=True, stop=True)
                    last.then_inc(s["value_ready"], 1)

        @block.scalar
        def _(act):
            for n in range(-3, CHUNKS):
                if 0 <= n + 2 < CHUNKS:
                    c = n % 2
                    act.wait_ge(s["turned"], n + 3)
                    wait_if(act, s["mixed"], n + 1)
                    if c == 1:
                        act.wait_ge(s["xt_ready"], n + 2)
                        act.activation(xt[1][:, 0:1], xt[0][:, CH:CH + 1], ACT.Copy)
                    act.activation(xt[c][:, 1:1 + CH], turn_ps[c][:, :], ACT.Copy).then_inc(s["xt_ready"], 1)
                if n + 3 < CHUNKS:
                    wait_if(act, s["turned"], n + 2)
                    chunk_norm(k, act, xn[(n + 1) % 2], n + 3).then_inc(s["xn_ready"], 1)
                if n >= 0:
                    c = n % 2
                    act.wait_ge(s["key_ready"], n + 1)
                    wait_if(act, s["squared"], n - 1)
                    act.activation(relu[c][:, :], key_ps[c][:, :], ACT.Relu).then_inc(s["relu_done"], 1)
                    act.wait_ge(s["relu_done"], n + 1)
                    wait_if(act, s["value_ready"], n - 1)
                    act.activation(act_k[c][:, :], relu[c][:, :], ACT.Square).then_inc(s["squared"], 1)
                    act.wait_ge(s["gate_ready"], n + 1)
                    wait_if(act, s["product_done"], n - 1)
                    act.activation(tanh[c][:, :, :], gate_ps[c][:, :, :], ACT.Tanh, scale=0.5)\
                       .then_inc(s["tanh_done"], 1)
            factors.on_act(act)


H, HKV, HD = 16, 4, 8
G = H // HKV
U = B * HKV
SCALE = float(1.0 / np.sqrt(np.float32(HD)))
PARTS = 3
SPLIT = PARTS * PARTS * HD
AUG = SPLIT + 2
VW = 32
KT = T // P


def rope_tables():
    half = HD // 2
    inv = (np.float32(1.0) / np.float32(10000.0) ** (np.arange(half, dtype=np.float32) * np.float32(2.0) / np.float32(HD)))
    angle = np.arange(T, dtype=np.float32)[:, None] * inv.astype(np.float32)[None, :]
    cos, sin = np.cos(angle).T.astype(np.float32), np.sin(angle).T.astype(np.float32)
    return np.stack([np.concatenate([cos, cos]), np.concatenate([-sin, sin])])


def after(eng, sem, n):
    if not isinstance(n, int) or n > 0:
        eng.wait_ge(sem, nth(n))


class Units:
    LOADS = 2 * PARTS

    BUFFERS, QUAD = 4, 4

    def __init__(self, k, ctx, qd, kd):
        self.qd, self.kd = qd, kd
        self.q_parts = [k.sb(f"q_parts{c}", [P, PARTS, CH], BF16, ctx) for c in range(self.BUFFERS)]
        self.k_parts = k.sb("k_parts", [P, PARTS, CH], BF16, ctx)
        self.q_out, self.k_out = [k.sem(f"q_out{c}") for c in range(self.BUFFERS)], k.sem("k_out")
        self.parts_out = [(sem, 16 * PARTS * CHUNKS // self.BUFFERS) for sem in self.q_out] + [(self.k_out, 16 * CHUNKS)]
        self.q1 = [k.sb(f"q1{j}", [SPLIT, 2, G, CH], BF16, ctx) for j in range(2)]
        self.k1 = [k.sb(f"k1{j}", [SPLIT, T], BF16, ctx) for j in range(2)]
        self.q2 = [k.sb(f"q2{j}", [AUG, 2, G, CH], BF16, ctx) for j in range(2)]
        self.k2 = [k.sb(f"k2{j}", [AUG, T], BF16, ctx) for j in range(2)]
        self.q1_in, self.q2_in = ([k.sem(f"{n}{j}") for j in range(2)] for n in ("q1_in", "q2_in"))

    def load(self, sp, q, kk, sem, u):
        unit_q, unit_k = self.qd[ds(u, 1), :, :, :, :, :], self.kd[ds(u, 1), :, :, :]
        for a in range(PARTS):
            rows = slice(a * HD * PARTS, (a + 1) * HD * PARTS)
            sp.dma_start(kk[rows, :], unit_k.rearrange("u d i t -> (u d i) t")).then_inc(sem, 16)
            sp.dma_start(q[rows, :, :, :], unit_q[:, :, a, :, :, :].rearrange("u d (b h) r t -> (u d) b (h r t)", b=1)
                         .to_broadcast([HD, PARTS, G * T])).then_inc(sem, 16)

    def store_queries(self, sp, n):
        group = slice(n // 2 * HKV, (n // 2 + 1) * HKV)
        for part in range(PARTS):
            sp.dma_start(self.qd[group, :, part, n % 2, :, :].rearrange("u d r t -> (u d) r t"),
                         self.q_parts[n % self.BUFFERS][:, part, :]).then_inc(self.q_out[n % self.BUFFERS], 16)

    def store_keys(self, sp, n):
        for c in range(self.QUAD):
            m = n + c
            group, columns = slice(m // 2 * HKV, (m // 2 + 1) * HKV), slice(m % 2 * CH, (m % 2 + 1) * CH)
            sp.dma_start(self.kd[group, :, :, columns].rearrange("u d i t -> (u d) i t"),
                         self.k_parts[c * 32:(c + 1) * 32, :, :]).then_inc(self.k_out, 16)

    def load1(self, sp, u, j):
        self.load(sp, self.q1[j], self.k1[j], self.q1_in[j], u)

    def load2(self, sp, u, j):
        self.load(sp, self.q2[j], self.k2[j], self.q2_in[j], u)


def project_stage(k, w, units):
    nc, qd, kd = k.nc, units.qd, units.kd
    s = {n: k.sem(n) for n in ("xn_ready turned xt_ready q_ready q_turned q_rotated q_split1 q_rest q_split2 q_split3 "
                               "k_ready k_turned k_rotated k_split1 k_rest k_split2 k_split3 v_ready v_copied v_filled "
                               "tables_in ones_set").split()}
    XT, QB, QUAD = 3, units.BUFFERS, units.QUAD
    q_parts, k_parts, q_out, k_out = units.q_parts, units.k_parts, units.q_out, units.k_out
    table = np.tile(np.repeat(rope_tables(), G, 1), (1, HKV, 1))
    key_table = np.tile(rope_tables(), (1, HKV, 1))
    table_k = np.concatenate([key_table[:, :, 0:CH], key_table[:, :, CH:T]] * (QUAD // 2), 1)
    tables = nc.inline_tensor(np.ascontiguousarray(table), name="rope_tables").ap()
    tables_k = nc.inline_tensor(np.ascontiguousarray(table_k), name="rope_tables_k").ap()
    with ExitStack() as ctx:
        def pair(name):
            return [k.sb(f"{name}{c}", [P, CH], ctx=ctx) for c in range(2)]

        xn = [k.sb(f"xn{c}", [P, TC, D], ctx=ctx) for c in range(2)]
        xt = [k.sb(f"xt{c}", [P, CH], ctx=ctx) for c in range(XT)]
        q_cos, q_sin, rot, rest = (pair(n) for n in ("q_cos", "q_sin", "rot", "rest"))
        cos, sin = k.sb("cos", [P, T], ctx=ctx), k.sb("sin", [P, T], ctx=ctx)
        cos_k, sin_k, k_cos, k_sin, k_rot, k_rest = (k.sb(n, [P, CH], ctx=ctx) for n in
                                                     "cos_k sin_k k_cos k_sin k_rot k_rest".split())
        turn_ps = k.ps("turn", [P, CH], ctx)
        q_ps = [k.ps(f"q{c}", [P, CH], ctx) for c in range(2)]
        qs_ps = [k.ps(f"qs{c}", [P, CH], ctx) for c in range(2)]
        key_ps, keys_ps = k.ps("k", [P, CH], ctx), k.ps("ks", [P, CH], ctx)
        v_ps = k.ps("v", [P, TB, HKV * HD], ctx)
        block = ctx.enter_context(nc.Block())

        @block.sync
        def _(sp):
            start(sp, [*units.q1_in, *units.q2_in])
            for dst, src in ((cos, tables[0]), (sin, tables[1]), (cos_k, tables_k[0]), (sin_k, tables_k[1])):
                sp.dma_start(dst[:, :], src).then_inc(s["tables_in"], 16)
            for n in range(QUAD):
                sp.wait_ge(s["q_split3"], n + 1)
                units.store_queries(sp, n)
            sp.wait_ge(s["k_split3"], 1)
            units.store_keys(sp, 0)
            for c in range(2):
                sp.wait_ge(q_out[c], 16 * PARTS)
            sp.wait_ge(k_out, 16 * QUAD)
            sp.wait_ge(s["ones_set"], 2)
            units.load1(sp, 0, 0)

        @block.gpsimd
        def _(pool):
            for n in range(CHUNKS + 1):
                c = n % 2
                if n < CHUNKS:
                    pool.wait_ge(s["q_turned"], n + 1)
                    wait_if(pool, s["q_rest"], n - 1)
                    pool.tensor_tensor(rot[c][:, :], q_cos[c][:, :], q_sin[c][:, :], ALU.add).then_inc(s["q_rotated"], 1)
                if n == 0:
                    pool.memset(k.values[:, :, :, :], 0.0).then_inc(s["v_filled"], 1)
                    pool.wait_ge(s["v_filled"], 1)
                    pool.memset(k.values[:, :, :, HD:HD + 1], 1.0).then_inc(s["v_filled"], 1)
                if n == 1:
                    pool.wait_ge(s["q_rotated"], 2)
                    for j, k2 in enumerate(units.k2):
                        pool.memset(k2[64:AUG, :], 1.0).then_inc(s["ones_set"], 1)
                        pool.wait_ge(s["ones_set"], j + 1)
                if n > 0:
                    c, parts = (n - 1) % 2, q_parts[(n - 1) % QB]
                    pool.wait_ge(s["q_split2"], n)
                    pool.tensor_tensor(parts[:, 2, :], rest[c][:, :], parts[:, 1, :], ALU.subtract)\
                        .then_inc(s["q_split3"], 1)

        @block.vector
        def _(dve):
            def norm(n):
                if n < CHUNKS:
                    wait_if(dve, s["turned"], n - 1)
                    for j in range(TC):
                        tile = n * TC + j
                        last = dve.tensor_scalar(xn[n % 2][:, j, :], k.x[:, tile, :], k.mean[:, tile:tile + 1],
                                                 k.rstd[:, tile:tile + 1], ALU.subtract, ALU.mult)
                    last.then_inc(s["xn_ready"], 1)

            for n in range(3):
                norm(n)
            dve.wait_ge(s["tables_in"], 16 * 4)
            for n in range(CHUNKS + 1):
                if n < CHUNKS:
                    c, columns = n % 2, slice(n % 2 * CH, (n % 2 + 1) * CH)
                    dve.wait_ge(s["q_ready"], n + 1)
                    wait_if(dve, s["q_rotated"], n - 1)
                    dve.tensor_tensor(q_cos[c][:, :], q_ps[c][:, :], cos[:, columns], ALU.mult)
                    dve.tensor_tensor(q_sin[c][:, :], qs_ps[c][:, :], sin[:, columns], ALU.mult).then_inc(s["q_turned"], 1)
                if n > 0:
                    c = (n - 1) % 2
                    dve.wait_ge(s["q_split1"], n)
                    wait_if(dve, s["q_split3"], n - 2)
                    dve.tensor_tensor(rest[c][:, :], rot[c][:, :], q_parts[(n - 1) % QB][:, 0, :], ALU.subtract)\
                       .then_inc(s["q_rest"], 1)
                norm(n + 3)
                if n % QUAD == QUAD - 1:
                    dve.wait_ge(s["k_ready"], n + 1)
                    wait_if(dve, s["k_rotated"], n // QUAD)
                    dve.tensor_tensor(k_cos[:, :], key_ps[:, :], cos_k[:, :], ALU.mult)
                    dve.tensor_tensor(k_sin[:, :], keys_ps[:, :], sin_k[:, :], ALU.mult).then_inc(s["k_turned"], 1)
                    dve.wait_ge(s["k_turned"], n // QUAD + 1)
                    dve.tensor_tensor(k_rot[:, :], k_cos[:, :], k_sin[:, :], ALU.add).then_inc(s["k_rotated"], 1)
                if n > 0 and n % QUAD == 0:
                    dve.wait_ge(s["k_split1"], n // QUAD)
                    wait_if(dve, s["k_split3"], n // QUAD - 1)
                    dve.tensor_tensor(k_rest[:, :], k_rot[:, :], k_parts[:, 0, :], ALU.subtract).then_inc(s["k_rest"], 1)
                    dve.wait_ge(s["k_split2"], n // QUAD)
                    dve.tensor_tensor(k_parts[:, 2, :], k_rest[:, :], k_parts[:, 1, :], ALU.subtract).then_inc(s["k_split3"], 1)

        @block.tensor
        def _(pe):
            for n in range(-2, CHUNKS):
                if n >= 0:
                    c, quad = n % 2, slice(n % QUAD * 32, (n % QUAD + 1) * 32)
                    pe.wait_ge(s["xt_ready"], n + 1)
                    wait_if(pe, s["q_turned"], n - 1)
                    pe.matmul(q_ps[c][:, :], w["q"][:, :], xt[n % XT][:, :], start=True, stop=True)
                    pe.matmul(qs_ps[c][:, :], w["q_swap"][:, :], xt[n % XT][:, :], start=True, stop=True).then_inc(s["q_ready"], 1)
                if n + 2 < CHUNKS:
                    pe.wait_ge(s["xn_ready"], n + 3)
                    wait_if(pe, s["xt_ready"], n + 2)
                    turn(k, pe, turn_ps, xn[n % 2], TC).then_inc(s["turned"], 1)
                if n >= 0:
                    wait_if(pe, s["k_turned"], n // QUAD)
                    pe.matmul(key_ps[quad, :], w["k"][:, :], xt[n % XT][:, :], start=True, stop=True)
                    pe.matmul(keys_ps[quad, :], w["k_swap"][:, :], xt[n % XT][:, :], start=True, stop=True)\
                      .then_inc(s["k_ready"], 1)
                    wait_if(pe, s["v_copied"], n // 2)
                    for j in range(TC):
                        last = pe.matmul(v_ps[:, c * TC + j, :], xt[n % XT][:, j * P:(j + 1) * P], w["v"][:, :],
                                         start=True, stop=True)
                    last.then_inc(s["v_ready"], 1)

        @block.scalar
        def _(act):
            for n in range(-2, CHUNKS + 1):
                if n + 2 < CHUNKS:
                    act.wait_ge(s["turned"], n + 3)
                    wait_if(act, s["v_ready"], n)
                    act.activation(xt[(n + 2) % XT][:, :], turn_ps[:, :], ACT.Copy).then_inc(s["xt_ready"], 1)
                if 0 <= n < CHUNKS and n % 2:
                    act.wait_ge(s["v_filled"], 2)
                    act.wait_ge(s["v_ready"], n + 1)
                    for g in range(HKV):
                        last = act.activation(k.values[:, n // 2 * HKV + g, :, 0:HD], v_ps[:, :, g * HD:(g + 1) * HD],
                                              ACT.Copy)
                    last.then_inc(s["v_copied"], 1)
                if 0 <= n < CHUNKS:
                    act.wait_ge(s["q_rotated"], n + 1)
                    wait_if(act, q_out[n % QB], 16 * PARTS * (n // QB))
                    act.activation(q_parts[n % QB][:, 0, :], rot[n % 2][:, :], ACT.Copy).then_inc(s["q_split1"], 1)
                if n > 0:
                    act.wait_ge(s["q_rest"], n)
                    act.activation(q_parts[(n - 1) % QB][:, 1, :], rest[(n - 1) % 2][:, :], ACT.Copy)\
                       .then_inc(s["q_split2"], 1)
                if n > 0 and n % QUAD == 0:
                    act.wait_ge(s["k_rotated"], n // QUAD)
                    wait_if(act, k_out, 16 * (n - QUAD))
                    act.activation(k_parts[:, 0, :], k_rot[:, :], ACT.Copy).then_inc(s["k_split1"], 1)
                    act.wait_ge(s["k_rest"], n // QUAD)
                    act.activation(k_parts[:, 1, :], k_rest[:, :], ACT.Copy).then_inc(s["k_split2"], 1)


def attention_stage(k, units):
    nc = k.nc
    s = k.sems("s1_full s1_max st_full exp_done pv_done o_copied o_turned o_scaled m_turned m_copied m_split "
               "v_ready den_ready")
    m_in = [k.sem(f"m_in{j}") for j in range(2)]
    q1, k1, q2, k2, q1_in, q2_in = units.q1, units.k1, units.q2, units.k2, units.q1_in, units.q2_in
    LOADS = units.LOADS
    HT = KT // 2
    with ExitStack() as ctx:
        v2 = [k.sb(f"v2{j}", [P, KT, VW], ctx=ctx) for j in range(2)]
        maxima = [k.sb(f"maxima{j}", [P, 2, G, HT], ctx=ctx) for j in range(2)]
        minus_m = k.sb("minus_m", [G * HT, 2, P], BF16, ctx)
        weights = [k.sb(f"weights{j}", [P, G, CH], ctx=ctx) for j in range(2)]
        o_sb = k.sb("o_sb", [P, CH], ctx=ctx)
        den = k.sb("den", [P, HT, G, 1], ctx=ctx)
        s1_ps = [k.ps(f"s1{j}", [P, T], ctx) for j in range(2)]
        st_ps = [k.ps(f"st{j}", [P, CH], ctx) for j in range(2)]
        pv_ps = k.ps("pv", [P, CH], ctx)
        small_ps = k.ps("small", [P, HT, G, VW], ctx)
        small_flat = small_ps[:, :, :, :].rearrange("p t g v -> p (t g v)")
        block = ctx.enter_context(nc.Block())

        def unit(i, n):
            return i * 2 + n

        def exists(i, n):
            return not isinstance(i, int) or 2 * i + n < U

        def score_bank(i, n, m):
            if exists(i, n + 1):
                return st_ps[m % 2][:, :], 2
            bank = (st_ps[0], st_ps[1], s1_ps[0], s1_ps[1])[m % 4]
            return bank[:, 0:CH], 2 if m < 4 else 4

        def run(eng, half_unit):
            half_unit(0, 0, 0, None)
            with eng.Fori(0, U // 2 - 1) as i:
                half_unit(i, 0, 1, (0, 0))
                half_unit(i, 1, 0, (0, 1))
                half_unit(i, 1, 1, (1, 0))
                half_unit(i, 2, 0, (1, 1))
            i = U // 2 - 1
            half_unit(i, 0, 1, (0, 0))
            half_unit(i, 1, 0, (0, 1))
            half_unit(i, 1, 1, (1, 0))

        @block.sync
        def _(sp):
            def put_maxima(i, n, half):
                sp.wait_ge(s["m_split"], nth(unit(i, n) * 2 + half + 1))
                for part in range(2):
                    row = SPLIT + part
                    sp.dma_start(q2[n % 2][row:row + 1, half, :, :], minus_m[:, part, :])\
                      .then_inc(m_in[half], 16)

            def step(i, n):
                u = unit(i, n)
                if exists(i, n + 2):
                    sp.wait_ge(s["s1_full"], nth(u * 32 + 32))
                    units.load1(sp, u + 2, n % 2)
                if exists(i, n + 1):
                    after(sp, s["pv_done"], u * 16)
                    units.load2(sp, u + 1, (n + 1) % 2)
                put_maxima(i, n, 1)
                if exists(i, n + 1):
                    put_maxima(i, n + 1, 0)

            start(sp, [*s.values(), *m_in])
            units.load2(sp, 0, 0)
            units.load1(sp, 1, 1)
            for n in range(units.QUAD, CHUNKS):
                units.store_queries(sp, n)
            units.store_keys(sp, units.QUAD)
            for sem, count in units.parts_out:
                sp.wait_ge(sem, count)
            put_maxima(0, 0, 0)
            with sp.Fori(0, U // 2 - 1) as i:
                step(i, 0)
                step(i, 1)
            step(U // 2 - 1, 0)
            step(U // 2 - 1, 1)

        @block.gpsimd
        def _(pool):
            def copy_values(i, n):
                u = unit(i, n)
                if not (isinstance(i, int) and u == 0):
                    after(pool, s["pv_done"], (u - 1) * 16)
                pool.tensor_copy(v2[n % 2][:, :, :], k.values[:, ds(u, 1), :, :].rearrange("p a t v -> p (a t) v"))\
                    .then_inc(s["v_ready"], 1)

            copy_values(0, 0)
            with pool.Fori(0, U // 2 - 1) as i:
                copy_values(i, 1)
                copy_values(i, 2)
            copy_values(U // 2 - 1, 1)

        @block.tensor
        def _(pe):
            def pass1(i, n, half, m):
                step = half * 16 + m
                if not (isinstance(i, int) and unit(i, n) == 0 and step < 2):
                    after(pe, s["s1_max"], unit(i, n) * 32 + step - 1)
                t, r = m // G, m % G
                for j in range(2):
                    last = pe.matmul(s1_ps[m % 2][:, j * CH:(j + 1) * CH], q1[n % 2][:, half, r, t * P:(t + 1) * P],
                                     k1[n % 2][:, j * CH:(j + 1) * CH], start=True, stop=True)
                last.then_inc(s["s1_full"], 1)

            def turn_maxima(i, n, half, scaled):
                pe.wait_ge(s["s1_max"], nth(unit(i, n) * 32 + (half + 1) * 16))
                after(pe, s["o_scaled"], scaled)
                pe.transpose(small_flat[0:G * HT, 0:P], maxima[n % 2][:, half, :, :].rearrange("p g t -> p (g t)"),
                             k.ident[:, :]).then_inc(s["m_turned"], 1)

            def scores(i, n, half, kt, r):
                m = half * 32 + kt * 4 + r
                bank, ahead = score_bank(i, n, m)
                after(pe, s["exp_done"], unit(i, n) * 64 + m + 1 - ahead)
                pe.matmul(bank, k2[n % 2][:, kt * P:(kt + 1) * P],
                          q2[n % 2][:, half, r, :], start=True, stop=True).then_inc(s["st_full"], 1)

            def values(i, n, half, kt):
                u = unit(i, n)
                pe.wait_ge(s["exp_done"], nth(u * 64 + half * 32 + kt * 4 + 4))
                if kt == 0:
                    after(pe, s["o_copied"], u * 2 + half)
                for r in range(G):
                    last = pe.matmul(pv_ps[r * 32:(r + 1) * 32, :], v2[n % 2][:, kt, :], weights[kt % 2][:, r, :],
                                     start=(kt == 0), stop=(kt == KT - 1))
                last.then_inc(s["pv_done"], 1)

            def turn_sums(halves):
                pe.wait_ge(s["o_copied"], nth(halves))
                pe.wait_ge(s["m_split"], nth(halves + 1 if not isinstance(halves, int) else min(halves + 1, 2 * U)))
                after(pe, s["o_scaled"], halves - 1)
                for t in range(HT):
                    last = pe.transpose(small_flat[:, t * P:(t + 1) * P], o_sb[:, t * P:(t + 1) * P], k.ident[:, :])
                last.then_inc(s["o_turned"], 1)

            def half_unit(i, n, half, before):
                u, more = unit(i, n), exists(i, n + 1)
                if half == 0:
                    pe.wait_ge(q2_in[n % 2], nth((i + n // 2 + 1) * (16 * LOADS)))
                    pe.wait_ge(s["v_ready"], nth(u + 1))
                    if more:
                        pe.wait_ge(q1_in[(n + 1) % 2], nth((i + (n + 1) // 2 + 1) * (16 * LOADS)))
                pe.wait_ge(m_in[half], nth((u + 1) * 32))
                for kt in range(KT):
                    if kt == 3 and half == 0:
                        turn_maxima(i, n, 1, u * 2)
                    if kt == 3 and half == 1 and more:
                        turn_maxima(i, n + 1, 0, u * 2 + 1)
                    scores(i, n, half, kt, 0)
                    scores(i, n, half, kt, 1)
                    all_first = not more and (half or kt)
                    if all_first:
                        scores(i, n, half, kt, 2)
                        scores(i, n, half, kt, 3)
                    if kt:
                        values(i, n, half, kt - 1)
                    elif before:
                        values(i, *before, KT - 1)
                    if not more and not all_first:
                        pe.wait_ge(s["s1_max"], nth(U * 32))
                    if not all_first:
                        scores(i, n, half, kt, 2)
                        scores(i, n, half, kt, 3)
                    if more:
                        pass1(i, n + 1, half, 2 * kt)
                        pass1(i, n + 1, half, 2 * kt + 1)
                    if kt == 1 and before:
                        turn_sums(u * 2 + half)

            pe.wait_ge(m_in[1], nth(0))
            pe.wait_ge(q1_in[0], nth(16 * LOADS))
            for half in range(2):
                for m in range(16):
                    pass1(0, 0, half, m)
                    if half == 1 and m == 2:
                        turn_maxima(0, 0, 0, 0)
            run(pe, half_unit)
            values(U // 2 - 1, 1, 1, KT - 1)
            turn_sums(2 * U)

        @block.vector
        def _(dve):
            def take_maximum(i, n, half, m):
                dve.wait_ge(s["s1_full"], nth(unit(i, n) * 32 + half * 16 + m + 1))
                dve.reduce_max(maxima[n % 2][:, half, m % G, m // G:m // G + 1], s1_ps[m % 2][:, :], AX.X)\
                   .then_inc(s["s1_max"], 1)

            def reuse_maxima(i, n):
                if not (isinstance(i, int) and 2 * i + n < 2):
                    after(dve, s["m_turned"], unit(i, n) * 2 - 2)

            def split_maxima(i, n, half):
                u = unit(i, n)
                dve.wait_ge(s["m_turned"], nth(u * 2 + half + 1))
                if half:
                    dve.wait_ge(m_in[0], nth((u + 1) * 32))
                else:
                    after(dve, m_in[1], u * 32)
                dve.tensor_scalar(minus_m[:, 0, :], small_flat[0:G * HT, 0:P], -1.0, None, ALU.mult).then_inc(s["m_copied"], 1)
                dve.wait_ge(s["m_copied"], nth(u * 2 + half + 1))
                dve.scalar_tensor_tensor(minus_m[:, 1, :], small_flat[0:G * HT, 0:P], -1.0, minus_m[:, 0, :],
                                         ALU.mult, ALU.subtract).then_inc(s["m_split"], 1)

            def copy_sums(halves):
                dve.wait_ge(s["pv_done"], nth(halves * KT))
                after(dve, s["o_turned"], halves - 1)
                dve.tensor_copy(o_sb[:, :], pv_ps[:, :]).then_inc(s["o_copied"], 1)

            def scale_sums(i, n, half):
                u = unit(i, n)
                dve.wait_ge(s["o_turned"], nth(u * 2 + half + 1))
                dve.reciprocal(den[:, :, :, :], small_ps[:, :, :, HD:HD + 1]).then_inc(s["den_ready"], 1)
                dve.wait_ge(s["den_ready"], nth(u * 2 + half + 1))
                out = k.attended[:, ds(u, 1), half * HT:(half + 1) * HT, :].rearrange("p a t (g d) -> p (a t) g d", d=HD)
                dve.tensor_tensor(out, small_ps[:, :, :, 0:HD], den[:, :, :, :].to_broadcast([P, HT, G, HD]), ALU.mult)\
                   .then_inc(s["o_scaled"], 1)

            def half_unit(i, n, half, before):
                more = exists(i, n + 1)
                if more and half == 0:
                    reuse_maxima(i, n + 1)
                if before:
                    copy_sums(unit(i, n) * 2 + half)
                for m in range(16):
                    if more:
                        take_maximum(i, n + 1, half, m)
                    if m == 3 and before:
                        scale_sums(i, *before)
                    if m == 9:
                        if half == 0:
                            split_maxima(i, n, 1)
                        elif more:
                            split_maxima(i, n + 1, 0)

            for half in range(2):
                for m in range(16):
                    take_maximum(0, 0, half, m)
                    if half == 1 and m == 7:
                        split_maxima(0, 0, 0)
            run(dve, half_unit)
            copy_sums(2 * U)
            scale_sums(U // 2 - 1, 1, 1)

        @block.scalar
        def _(act):
            def half_unit(i, n, half, before):
                u = unit(i, n)
                for kt in range(KT):
                    m = half * 8 + kt
                    after(act, s["pv_done"], u * 16 + m - 1)
                    for r in range(G):
                        act.wait_ge(s["st_full"], nth(u * 64 + m * 4 + r + 1))
                        act.activation(weights[kt % 2][:, r, :], score_bank(i, n, m * 4 + r)[0], ACT.Exp, scale=SCALE)\
                           .then_inc(s["exp_done"], 1)

            run(act, half_unit)


def attention_out_stage(k, w):
    nc = k.nc
    s = {n: k.sem(n) for n in "gathered turned at_ready out_ready added".split()}
    factors = Factors(k)
    with ExitStack() as ctx:
        at_rows = [k.sb(f"rows{c}", [P, TC, D], ctx=ctx) for c in range(2)]
        at_cols = [k.sb(f"cols{c}", [P, CH], ctx=ctx) for c in range(2)]
        turn_ps = [k.ps(f"turn{c}", [P, CH], ctx) for c in range(2)]
        out_ps = [k.ps(f"out{c}", [P, TC, D], ctx) for c in range(2)]
        block = ctx.enter_context(nc.Block())

        @block.scalar
        def _(act):
            for n in range(-2, CHUNKS):
                if n + 2 < CHUNKS:
                    i, c = (n + 2) // 2, n % 2
                    wait_if(act, s["turned"], n + 1)
                    for g in range(HKV):
                        last = act.activation(at_rows[c][:, :, g * 32:(g + 1) * 32],
                                              k.attended[:, i * HKV + g, c * TC:(c + 1) * TC, :], ACT.Copy)
                    last.then_inc(s["gathered"], 1)
                if 0 <= n + 1 < CHUNKS:
                    act.wait_ge(s["turned"], n + 2)
                    wait_if(act, s["out_ready"], n)
                    act.activation(at_cols[(n + 1) % 2][:, :], turn_ps[(n + 1) % 2][:, :], ACT.Copy)\
                       .then_inc(s["at_ready"], 1)
            factors.on_act(act)

        @block.tensor
        def _(pe):
            for n in range(-1, CHUNKS):
                if n + 1 < CHUNKS:
                    pe.wait_ge(s["gathered"], n + 2)
                    wait_if(pe, s["at_ready"], n)
                    turn(k, pe, turn_ps[(n + 1) % 2], at_rows[(n + 1) % 2], TC).then_inc(s["turned"], 1)
                if n >= 0:
                    c = n % 2
                    pe.wait_ge(s["at_ready"], n + 1)
                    wait_if(pe, s["added"], n - 1)
                    for j in range(TC):
                        last = pe.matmul(out_ps[c][:, j, :], at_cols[c][:, j * P:(j + 1) * P], w["o"][:, :],
                                         start=True, stop=True)
                    last.then_inc(s["out_ready"], 1)

        @block.vector
        def _(dve):
            for n in range(CHUNKS):
                tiles = chunk_tiles(n)
                dve.wait_ge(s["out_ready"], n + 1)
                dve.tensor_tensor(k.x[:, tiles, :], out_ps[n % 2][:, :, :], k.x[:, tiles, :], ALU.add)\
                   .then_inc(s["added"], 1)
                last = chunk_sums(k, dve, s["added"], n + 1, n)
            factors.on_dve(dve, last)


E = 8
F = 352
HID = [(0, 128), (128, 128), (256, 96)]
CHOICES = 2
SLOT_TILES = CHOICES * NT + E
SLOTS = SLOT_TILES * P
ROW = D + 2
NOWHERE = 2 * B * T * CHOICES
FILL = 9


def moe_constants():
    def wide(v):
        return np.broadcast_to(np.asarray(v, np.float32), (P, *np.shape(v)))

    token = np.arange(NT)[None, :] * P + np.arange(P)[:, None]
    return {
        "rank": wide(np.broadcast_to(E - np.arange(E), (NT, E))),
        "before": np.triu(np.ones((P, P), np.float32), 1),
        "ones": np.ones((P, P), np.float32),
        "runs": wide(np.broadcast_to(np.arange(NT) > 0, (E, NT))),
        "tile_starts": wide(np.broadcast_to(P * np.arange(NT), (E, NT))),
        "slot_tile": wide(np.broadcast_to(np.arange(SLOT_TILES)[:, None], (SLOT_TILES, E))),
        "target": np.stack([token * CHOICES + c for c in range(CHOICES)], 1).astype(np.float32),
    }


CONSTANTS = {"rank": [P, NT, E], "before": [P, P], "ones": [P, P], "runs": [P, E, NT], "tile_starts": [P, E, NT],
             "slot_tile": [P, SLOT_TILES, E], "target": [P, CHOICES, NT]}


FILLED = 16 * SLOT_TILES // FILL


def route_stage(k, w, m, split):
    nc = k.nc
    s = {n: k.sem(n) for n in ("xn_ready turned xt_ready logits_ready copied shifted_ready exp_ready chosen counted "
                               "dve_link rows_ready upper_ready").split()}
    with ExitStack() as ctx:
        t = {n: k.sb(n, [P, NT, E], ctx=ctx) for n in "shifted prob rest hot hot1 hot2 place_in".split()}
        t.update({n: k.sb(n, [P, NT, 1], ctx=ctx) for n in "one two place inv slot1 slot2".split()})
        totals, up_to, offset, over = (k.sb(n, [P, E, NT], ctx=ctx) for n in ("totals", "up_to", "offset", "over"))
        tiles, tiles_to, base = (k.sb(n, [P, E, 1], ctx=ctx) for n in ("tiles", "tiles_to", "base"))
        passed_by, expert = k.sb("passed_by", [P, SLOT_TILES, E], ctx=ctx), k.sb("expert", [P, SLOT_TILES, 1], ctx=ctx)
        turn_ps = [k.ps(f"turn{c}", [P, CH], ctx) for c in range(2)]
        logits_ps = k.ps("logits", [P, NT, E], ctx)
        before_ps, totals_ps = (k.ps(n, [P, NT, E], ctx) for n in ("before_ps", "totals_ps"))
        block = ctx.enter_context(nc.Block())

        @block.vector
        def _(dve):
            link = Link(dve, s["dve_link"])

            def wide(ap):
                return ap.to_broadcast([P, NT, E])

            for c in range(CHUNKS):
                for j in range(c * TC, (c + 1) * TC):
                    last = dve.tensor_scalar(m["rows"][0][:, j, 0:D], k.x[:, j, :], k.mean[:, j:j + 1], k.rstd[:, j:j + 1],
                                             ALU.subtract, ALU.mult)
                last.then_inc(s["xn_ready"], 1)
            if split:
                for e in range(E):
                    dve.wait_ge(s["upper_ready"], e + 1)
                    for n in ("gate", "up"):
                        dve.tensor_tensor(w[n][:, e, :].bitcast(F32R), w[n][:, e, :], k.upper[n][:, e, :].bitcast(F32),
                                          ALU.subtract)
            dve.wait_ge(s["logits_ready"], 1)
            link(dve.reduce_max(t["one"][:, :, :], logits_ps[:, :, :], AX.X))
            dve.tensor_tensor(t["shifted"][:, :, :], logits_ps[:, :, :], wide(t["one"][:, :, :]), ALU.subtract)\
               .then_inc(s["shifted_ready"], 1)
            for c in range(CHOICES):
                dve.tensor_copy(m["rows"][c][:, :, D:D + 1], w["target"][:, c, :].rearrange("p (n a) -> p n a", a=1))
            dve.wait_ge(s["exp_ready"], 1)
            link(dve.reduce_sum(t["one"][:, :, :], t["prob"][:, :, :], AX.X))
            link(dve.reciprocal(t["two"][:, :, :], t["one"][:, :, :]))
            link(dve.tensor_tensor(t["prob"][:, :, :], t["prob"][:, :, :], wide(t["two"][:, :, :]), ALU.mult))

            def pick(values, top, hot):
                link(dve.reduce_max(top, values, AX.X))
                link(dve.tensor_tensor(hot, values, wide(top), ALU.is_equal))
                link(dve.tensor_tensor(t["shifted"][:, :, :], hot, w["rank"][:, :, :], ALU.mult))
                link(dve.reduce_max(t["place"][:, :, :], t["shifted"][:, :, :], AX.X))
                return dve.tensor_tensor(hot, w["rank"][:, :, :], wide(t["place"][:, :, :]), ALU.is_equal)

            link(pick(t["prob"][:, :, :], t["one"][:, :, :], t["hot1"][:, :, :]))
            link(dve.scalar_tensor_tensor(t["rest"][:, :, :], t["hot1"][:, :, :], -2.0, t["prob"][:, :, :], ALU.mult, ALU.add))
            link(pick(t["rest"][:, :, :], t["two"][:, :, :], t["hot2"][:, :, :]))
            dve.tensor_tensor(t["hot"][:, :, :], t["hot1"][:, :, :], t["hot2"][:, :, :], ALU.add).then_inc(s["chosen"], 1)
            link(dve.scalar_tensor_tensor(t["place"][:, :, :], t["one"][:, :, :], 1e-20, t["two"][:, :, :], ALU.add, ALU.add))
            link(dve.reciprocal(t["inv"][:, :, :], t["place"][:, :, :]))
            for c, top in enumerate(("one", "two")):
                dve.scalar_tensor_tensor(m["rows"][c][:, :, D + 1:D + 2], t[top][:, :, :], 0.5, t["inv"][:, :, :],
                                         ALU.mult, ALU.mult)
            dve.wait_ge(s["counted"], 1)
            link(dve.tensor_copy(totals[:, :, :], totals_ps[:, :, :].rearrange("p n e -> p e n")))
            flat = [a[:, :, :].rearrange("p e n -> p (e n)") for a in (up_to, w["runs"], totals)]
            link(dve.tensor_tensor_scan(flat[0], flat[1], flat[2], 0.0, ALU.mult, ALU.add))
            dve.tensor_tensor(offset[:, :, :], up_to[:, :, :], totals[:, :, :], ALU.subtract)
            link(dve.tensor_tensor(over[:, :, :], up_to[:, :, NT - 1:NT].to_broadcast([P, E, NT]), w["tile_starts"][:, :, :],
                                   ALU.is_gt))
            link(dve.reduce_sum(tiles[:, :, :], over[:, :, :], AX.X))
            link(dve.tensor_tensor_scan(tiles_to[:, :, 0], w["ones"][:, 0:E], tiles[:, :, 0], 0.0, ALU.mult, ALU.add))
            link(dve.tensor_tensor(base[:, :, :], tiles_to[:, :, :], tiles[:, :, :], ALU.subtract))
            link(dve.scalar_tensor_tensor(offset[:, :, :], base[:, :, :].to_broadcast([P, E, NT]), float(P), offset[:, :, :],
                                          ALU.mult, ALU.add))
            link(dve.tensor_tensor(t["place_in"][:, :, :], before_ps[:, :, :], offset[:, :, :].rearrange("p e n -> p n e"),
                                   ALU.add))
            for c, (hot, slot) in enumerate((("hot1", "slot1"), ("hot2", "slot2"))):
                link(dve.tensor_tensor(t[hot][:, :, :], t[hot][:, :, :], t["place_in"][:, :, :], ALU.mult))
                link(dve.reduce_sum(t[slot][:, :, :], t[hot][:, :, :], AX.X))
                dve.tensor_copy(m["slot"][c][:, :], t[slot][:, :, 0]).then_inc(s["rows_ready"], 1)
            link(dve.tensor_tensor(passed_by[:, :, :], w["slot_tile"][:, :, :],
                                   tiles_to[:, :, :].rearrange("p e a -> p a e").to_broadcast([P, SLOT_TILES, E]), ALU.is_ge))
            link(dve.reduce_sum(expert[:, :, :], passed_by[:, :, :], AX.X))
            dve.tensor_scalar(m["expert"][:, :], expert[:, :, 0], float(E - 1), None, ALU.min).then_inc(s["rows_ready"], 1)

        @block.tensor
        def _(pe):
            def logits(c):
                pe.wait_ge(s["xt_ready"], c + 1)
                for j in range(c * TC, (c + 1) * TC):
                    last = pe.matmul(logits_ps[:, j, :], m["xt"][:, j * P:(j + 1) * P], w["router"][:, :],
                                     start=True, stop=True)
                return last

            for c in range(CHUNKS):
                pe.wait_ge(s["xn_ready"], c + 1)
                if c > 1:
                    pe.wait_ge(s["xt_ready"], c - 1)
                for j in range(TC):
                    last = pe.transpose(turn_ps[c % 2][:, j * P:(j + 1) * P], m["rows"][0][:, c * TC + j, 0:D], k.ident[:, :])
                last.then_inc(s["turned"], 1)
                if c:
                    logits(c - 1)
            logits(CHUNKS - 1).then_inc(s["logits_ready"], 1)
            pe.wait_ge(s["chosen"], 1)
            pe.matmul(before_ps[:, :, :], w["before"][:, :], t["hot"][:, :, :], start=True, stop=True)
            pe.matmul(totals_ps[:, :, :], w["ones"][:, :], t["hot"][:, :, :], start=True, stop=True)\
              .then_inc(s["counted"], 1)

        @block.scalar
        def _(act):
            for c in range(CHUNKS):
                act.wait_ge(s["turned"], c + 1)
                act.activation(m["xt"][:, c * CH:(c + 1) * CH], turn_ps[c % 2][:, :], ACT.Copy).then_inc(s["xt_ready"], 1)
                if split:
                    for e in range(c * E // CHUNKS, (c + 1) * E // CHUNKS):
                        for n in ("gate", "up"):
                            last = act.activation(k.upper[n][:, e, :], w[n][:, e, :], ACT.Copy)
                        last.then_inc(s["upper_ready"], 1)
            act.wait_ge(s["shifted_ready"], 1)
            act.activation(t["prob"][:, :, :], t["shifted"][:, :, :], ACT.Exp).then_inc(s["exp_ready"], 1)
            for c in range(CHUNKS):
                tiles_of = slice(c * TC, (c + 1) * TC)
                act.activation(m["rows"][1][:, tiles_of, 0:D], m["rows"][0][:, tiles_of, 0:D], ACT.Copy)\
                   .then_inc(s["copied"], 1)


def shared_stage(k, w, m, slots, scattered):
    nc = k.nc
    s = k.sems("gate_ready silu_done hidden_done down_done added")
    with ExitStack() as ctx:
        silu = [k.sb(f"silu{j}", [P, CH], ctx=ctx) for j in range(2)]
        hidden = [[k.sb(f"hidden{j}{n}", [P, CH], ctx=ctx) for n in range(len(HID))] for j in range(2)]
        gate_ps = [k.ps(f"gate{j}", [P, CH], ctx) for j in range(2)]
        up_ps = [k.ps(f"up{j}", [P, CH], ctx) for j in range(2)]
        down_ps = [k.ps(f"down{j}", [P, TC, D], ctx) for j in range(2)]
        block = ctx.enter_context(nc.Block())

        @block.sync
        def _(sp):
            start(sp, s.values())

        @block.gpsimd
        def _(pool):
            pool.wait_ge(k.filled, k.fills)
            for n in range(NT):
                for c in range(CHOICES):
                    pool.indirect_dma_start(slots[:, :], bass.IndirectOffsetOnAxis(m["slot"][c][:, n:n + 1], 0),
                                            m["rows"][c][:, n, :], None).then_inc(scattered, 16)

        def run(eng, chunk):
            chunk(0, 0)
            chunk(1, 1)
            with eng.Fori(1, CHUNKS // 2) as i:
                chunk(i * 2, 0)
                chunk(i * 2 + 1, 1)

        @block.vector
        def _(dve):
            def add(n, c):
                dve.wait_ge(s["down_done"], nth(n + 1))
                tokens = k.x[:, ds(n * TC, TC), :]
                dve.scalar_tensor_tensor(tokens, down_ps[c][:, :, :], 0.5, tokens, ALU.mult, ALU.add)\
                   .then_inc(s["added"], 1)

            def chunk(n, c):
                for h, (_, width) in enumerate(HID):
                    q = c * len(HID) + h
                    dve.wait_ge(s["silu_done"], nth(n * len(HID) + h + 1))
                    if h == 0:
                        after(dve, s["down_done"], n - 1)
                    dve.tensor_tensor(hidden[c][h][0:width, :], silu[q % 2][0:width, :], up_ps[q % 2][0:width, :],
                                      ALU.mult).then_inc(s["hidden_done"], 1)
                    if h == 1 and not (isinstance(n, int) and n == 0):
                        add(n - 1, 1 - c)

            run(dve, chunk)
            add(CHUNKS - 1, 1)

        @block.tensor
        def _(pe):
            def up(n, c, h):
                first, width = HID[h]
                q = c * len(HID) + h
                tokens = m["xt"][:, ds(n * CH, CH)]
                after(pe, s["hidden_done"], n * len(HID) + h - 1)
                pe.matmul(gate_ps[q % 2][0:width, :], w["gate"][:, E, first:first + width], tokens, start=True, stop=True)
                pe.matmul(up_ps[q % 2][0:width, :], w["up"][:, E, first:first + width], tokens, start=True, stop=True)\
                  .then_inc(s["gate_ready"], 1)

            def down(n, c):
                pe.wait_ge(s["hidden_done"], nth((n + 1) * len(HID)))
                after(pe, s["added"], n - 1)
                for j in range(TC):
                    for h, (_, width) in enumerate(HID):
                        last = pe.matmul(down_ps[c][:, j, :], hidden[c][h][0:width, j * P:(j + 1) * P],
                                         w["down"][0:width, E, h, :], start=(h == 0), stop=(h == len(HID) - 1))
                last.then_inc(s["down_done"], 1)

            def chunk(n, c):
                up(n, c, 0)
                if not (isinstance(n, int) and n == 0):
                    down(n - 1, 1 - c)
                up(n, c, 1)
                up(n, c, 2)

            pe.wait_ge(s["added"], nth(0))
            run(pe, chunk)
            down(CHUNKS - 1, 1)

        @block.scalar
        def _(act):
            def chunk(n, c):
                for h, (_, width) in enumerate(HID):
                    q = (c * len(HID) + h) % 2
                    act.wait_ge(s["gate_ready"], nth(n * len(HID) + h + 1))
                    after(act, s["hidden_done"], n * len(HID) + h - 1)
                    act.activation(silu[q][0:width, :], gate_ps[q][0:width, :], ACT.Silu).then_inc(s["silu_done"], 1)

            run(act, chunk)


def expert_stage(k, w, m, slots, results, scattered):
    nc = k.nc
    DEPTH = 12
    s = k.sems("turned upper_ready xt_ready gate_ready silu_done hidden_done hidden_turned ht_ready down_done scaled")
    loaded, stored = ([k.sem(f"{n}{j}") for j in range(DEPTH)] for n in ("loaded", "stored"))
    pool_passed = k.sem("pool_passed")
    with ExitStack() as ctx:
        rows = [k.sb(f"rows{j}", [P, ROW], ctx=ctx) for j in range(DEPTH)]
        xt_upper, xt_lower = ([k.sb(f"{n}{j}", [P, P], F32R, ctx) for j in range(DEPTH)] for n in ("xt_upper", "xt_lower"))
        silu, hidden = ([k.sb(f"{n}{j}", [P, F], ctx=ctx) for j in range(2)] for n in ("silu", "hidden"))
        ht = [k.sb(f"ht{j}", [P, len(HID), P], ctx=ctx) for j in range(2)]
        index = [k.sb(f"index{j}", [P, 1], U32, ctx) for j in range(DEPTH)]
        y = [k.sb(f"y{j}", [P, D], ctx=ctx) for j in range(DEPTH)]
        gate_ps, up_ps = ([k.ps(f"{n}{j}", [P, F], ctx) for j in range(2)] for n in ("gate", "up"))
        turn_ps, ht_ps = k.ps("turn", [P, P], ctx), k.ps("ht", [P, len(HID), P], ctx)
        down_ps = [k.ps(f"down{j}", [P, D], ctx) for j in range(2)]
        block = ctx.enter_context(nc.Block())

        def within(n):
            return not isinstance(n, int) or 0 <= n < SLOT_TILES

        def steps(eng, step, ahead):
            for n in range(-ahead, DEPTH + 2):
                step(n, n % DEPTH)
            with eng.Fori(1, SLOT_TILES // DEPTH - 1) as i:
                for j in range(2, DEPTH + 2):
                    step(i * DEPTH + j, j % DEPTH)
            for n in range(SLOT_TILES - DEPTH + 2, SLOT_TILES + 2):
                step(n, n % DEPTH)

        def turn_of(n, j):
            return n // DEPTH if isinstance(n, int) else (n - j) // DEPTH

        @block.sync
        def _(sp):
            start(sp, [*s.values(), *loaded])
            sp.wait_ge(scattered, 16 * CHOICES * NT)

            def load(n, j):
                if within(n):
                    after(sp, s["scaled"], n - DEPTH + 1)
                    sp.dma_start(rows[j][:, :], slots[ds(n * P, P), :]).then_inc(loaded[j], 16)

            steps(sp, load, 0)

        @block.tensor
        def _(pe):
            held = {}

            def expert(n, j):
                if j not in held:
                    held[j] = nc.values_load(
                        m["expert"][0:1, ds(n, 1)], engines=[mybir.EngineType.PE], min_val=0, max_val=E - 1,
                        skip_runtime_bounds_check_because="route_stage counts up from 0 and takes the minimum with E - 1")
                return held[j]

            def step(n, j):
                if j == 2:
                    held.clear()
                if within(n):
                    e = expert(n, j)
                    pe.wait_ge(s["xt_ready"], nth(n + 1))
                    after(pe, s["hidden_done"], n - 1)
                    parts = []
                    for out, name in ((gate_ps, "gate"), (up_ps, "up")):
                        upper = k.upper[name][:, ds(e, 1), :].rearrange("p a f -> p (a f)")
                        lower = w[name][:, ds(e, 1), :].rearrange("p a f -> p (a f)").bitcast(F32R)
                        pe.matmul(out[j % 2][:, :], xt_upper[j][:, :], upper, start=True, stop=False)
                        pe.matmul(out[j % 2][:, :], xt_upper[j][:, :], lower, start=False, stop=False)
                        parts.append((out, upper))
                    for out, upper in parts:
                        last = pe.matmul(out[j % 2][:, :], xt_lower[j][:, :], upper, start=False, stop=True)
                    last.then_inc(s["gate_ready"], 1)
                if within(n - 2):
                    expert(n - 2, (j - 2) % DEPTH)
                if within(n + 1) and j != 1:
                    expert(n + 1, (j + 1) % DEPTH)
                if within(n - 1):
                    pe.wait_ge(s["hidden_done"], nth(n))
                    after(pe, s["ht_ready"], n - 1)
                    for h, (first, width) in enumerate(HID):
                        last = pe.transpose(ht_ps[0:width, h, :], hidden[(j - 1) % 2][:, first:first + width], k.ident[:, :])
                    last.then_inc(s["hidden_turned"], 1)
                if within(n + 2):
                    q = (j + 2) % DEPTH
                    pe.wait_ge(loaded[q], 16 * (turn_of(n + 2, q) + 1) + 1)
                    after(pe, s["xt_ready"], n + 2)
                    pe.transpose(turn_ps[:, :], rows[q][:, 0:D], k.ident[:, :]).then_inc(s["turned"], 1)
                if within(n - 2):
                    e = held.pop((j - 2) % DEPTH)
                    pe.wait_ge(s["ht_ready"], nth(n - 1))
                    after(pe, s["scaled"], n - 3)
                    for h, (_, width) in enumerate(HID):
                        last = pe.matmul(down_ps[j % 2][:, :], ht[j % 2][0:width, h, :],
                                         w["down"][0:width, ds(e, 1), h, :].rearrange("p a f -> p (a f)"),
                                         start=(h == 0), stop=(h == len(HID) - 1))
                    last.then_inc(s["down_done"], 1)

            steps(pe, step, 2)

        @block.scalar
        def _(act):
            def step(n, j):
                if within(n):
                    act.wait_ge(s["gate_ready"], nth(n + 1))
                    after(act, s["hidden_done"], n - 1)
                    act.activation(silu[j % 2][:, :], gate_ps[j % 2][:, :], ACT.Silu).then_inc(s["silu_done"], 1)
                if within(n - 1):
                    act.wait_ge(s["hidden_turned"], nth(n))
                    after(act, s["down_done"], n - 2)
                    q = (j - 1) % 2
                    act.activation(ht[q][:, 0:2, :], ht_ps[:, 0:2, :], ACT.Copy)
                    act.activation(ht[q][0:HID[2][1], 2, :], ht_ps[0:HID[2][1], 2, :], ACT.Copy).then_inc(s["ht_ready"], 1)
                if within(n + 2):
                    act.wait_ge(s["turned"], nth(n + 3))
                    after(act, s["gate_ready"], n + 3 - DEPTH)
                    act.activation(xt_upper[(j + 2) % DEPTH][:, :], turn_ps[:, :], ACT.Copy).then_inc(s["upper_ready"], 1)

            steps(act, step, 2)

        @block.vector
        def _(dve):
            def step(n, j):
                if within(n):
                    dve.wait_ge(s["silu_done"], nth(n + 1))
                    after(dve, s["hidden_turned"], n - 1)
                    dve.tensor_tensor(hidden[j % 2][:, :], silu[j % 2][:, :], up_ps[j % 2][:, :], ALU.mult)\
                       .then_inc(s["hidden_done"], 1)
                if within(n + 2):
                    q = (j + 2) % DEPTH
                    dve.wait_ge(s["upper_ready"], nth(n + 3))
                    after(dve, s["gate_ready"], n + 3 - DEPTH)
                    dve.tensor_tensor(xt_lower[q][:, :], turn_ps[:, :], xt_upper[q][:, :].bitcast(F32), ALU.subtract)\
                       .then_inc(s["xt_ready"], 1)
                if within(n - 2):
                    q = (j - 2) % DEPTH
                    if not isinstance(n, int) or n - 2 >= DEPTH:
                        dve.wait_ge(stored[q], 16 * turn_of(n - 2, q))
                    dve.wait_ge(loaded[q], 16 * (turn_of(n - 2, q) + 1) + 1)
                    dve.tensor_scalar(index[q][:, :], rows[q][:, D:D + 1], 1.0, None, ALU.mult)
                    dve.wait_ge(s["down_done"], nth(n - 1))
                    dve.tensor_scalar(y[q][:, :], down_ps[j % 2][:, :], rows[q][:, D + 1:D + 2], None, ALU.mult)\
                       .then_inc(s["scaled"], 1)

            steps(dve, step, 2)

        @block.gpsimd
        def _(pool):
            def store(n, j):
                if within(n):
                    pool.wait_ge(s["scaled"], nth(n + 1))
                    pool.sem_inc(pool_passed, 1)
                    pool.indirect_dma_start(results[:, :], bass.IndirectOffsetOnAxis(index[j][:, :], 0), y[j][:, :], None,
                                            bounds_check=B * T * CHOICES - 1, oob_is_err=False).then_inc(stored[j], 16)

            steps(pool, store, 0)
            for q in range(DEPTH):
                pool.wait_ge(stored[q], 16 * (SLOT_TILES // DEPTH))


def fetch_pairs(sp, results, both, fetched):
    pairs = results.rearrange("(n p c) d -> p n (c d)", p=P, c=CHOICES)
    for b in range(B):
        tiles = slice(b * TB, (b + 1) * TB)
        sp.dma_start(both[:, tiles, :], pairs[:, tiles, :]).then_inc(fetched[b], 16)


def join_pairs(pool, both, fetched, paired):
    for b in range(B):
        tiles = slice(b * TB, (b + 1) * TB)
        pool.wait_ge(fetched[b], 16)
        wait_if(pool, paired, b)
        pool.tensor_tensor(both[:, tiles, 0:D], both[:, tiles, 0:D], both[:, tiles, D:2 * D], ALU.add).then_inc(paired, 1)


def add_pairs(k, dve, both, paired, added, b):
    tiles = slice(b * TB, (b + 1) * TB)
    dve.wait_ge(paired, b + 1)
    dve.tensor_tensor(k.x[:, tiles, :], k.x[:, tiles, :], both[:, tiles, 0:D], ALU.add).then_inc(added, 1)


def output_stage(k, results, out):
    nc = k.nc
    fetched = [k.sem(f"fetched{b}") for b in range(B)]
    paired, added, stored = k.sem("paired"), k.sem("added"), k.sem("stored")
    with ExitStack() as ctx:
        both = k.sb("both", [P, NT, CHOICES * D], ctx=ctx)
        block = ctx.enter_context(nc.Block())

        @block.sync
        def _(sp):
            fetch_pairs(sp, results, both, fetched)
            out_tiles = out.rearrange("b (t p) d -> p (b t) d", p=P)
            for b in range(B):
                tiles = slice(b * TB, (b + 1) * TB)
                sp.wait_ge(added, b + 1)
                sp.dma_start(out_tiles[:, tiles, :], k.x[:, tiles, :]).then_inc(stored, 16)
            sp.wait_ge(stored, 16 * B)

        @block.vector
        def _(dve):
            for b in range(B):
                add_pairs(k, dve, both, paired, added, b)

        @block.gpsimd
        def _(pool):
            join_pairs(pool, both, fetched, paired)


def mixture(k, stage, name, w, slots, results, split):
    scattered = k.sem(name + "_scattered")
    k.fills += FILLED
    with ExitStack() as ctx:
        m = {"rows": [k.sb(f"{name}_rows{c}", [P, NT, ROW], ctx=ctx) for c in range(CHOICES)],
             "xt": k.sb(name + "_xt", [P, B * T], ctx=ctx),
             "slot": [k.sb(f"{name}_slot{c}", [P, NT], U32, ctx) for c in range(CHOICES)],
             "expert": k.sb(name + "_expert", [P, SLOT_TILES], U32, ctx)}
        stage(name + "_route", route_stage, w, m, split)
        stage(name + "_shared", shared_stage, w, m, slots, scattered)
        stage(name + "_experts", expert_stage, w, m, slots, results, scattered)


def recurrence_stage(k, w, results):
    nc = k.nc
    s = {n: k.sem(n) for n in ("xn_ready turned xt_ready input_ready driven scanned out_ready added exp_ready "
                               "consts paired joined normable").split()}
    fetched = [k.sem(f"fetched{b}") for b in range(B)]
    own, factors = Factors(k, "_own"), Factors(k)
    XT = 3
    with ExitStack() as ctx:
        xn = [k.sb(f"xn{c}", [P, TC, D], ctx=ctx) for c in range(2)]
        xt = [k.sb(f"xt{c}", [P, CH], ctx=ctx) for c in range(XT)]
        drive = [k.sb(f"drive{c}", [P, CH], ctx=ctx) for c in range(2)]
        state = [k.sb(f"state{c}", [P, CH], ctx=ctx) for c in range(2)]
        decay, one_decay = k.sb("decay", [P, CH], ctx=ctx), k.sb("one_decay", [P, 1], ctx=ctx)
        skip, bias = k.sb("skip", [P, D], ctx=ctx), k.sb("bias", [P, 1], ctx=ctx)
        turn_ps = [k.ps(f"turn{c}", [P, CH], ctx) for c in range(2)]
        in_ps = [k.ps(f"in{c}", [P, CH], ctx) for c in range(2)]
        out_ps = [k.ps(f"out{c}", [P, TC, D], ctx) for c in range(2)]
        both = k.sb("both", [P, NT, CHOICES * D], ctx=ctx)
        block = ctx.enter_context(nc.Block())

        @block.sync
        def _(sp):
            fetch_pairs(sp, results, both, fetched)

        def sequence(b):
            return slice(b * TB, (b + 1) * TB)

        @block.gpsimd
        def _(pool):
            join_pairs(pool, both, fetched, s["paired"])

        @block.vector
        def _(dve):
            dve.tensor_scalar(skip[:, :], k.ident[:, :], w["skip"][:, 0:1], None, ALU.mult)
            dve.tensor_tensor(bias[:, :], w["b_in"][:, :], w["b_vec"][:, :], ALU.mult)
            dve.memset(decay[:, :], -1.0).then_inc(s["consts"], 1)
            dve.wait_ge(s["consts"], 1)
            dve.wait_ge(s["exp_ready"], 1)
            dve.tensor_scalar(decay[:, :], decay[:, :], one_decay[:, 0:1], None, ALU.mult).then_inc(s["consts"], 1)
            dve.wait_ge(s["consts"], 2)

            def join(b):
                add_pairs(k, dve, both, s["paired"], s["joined"], b)
                dve.wait_ge(s["joined"], b + 1)
                for j in range(b * TB, (b + 1) * TB):
                    last = dve.bn_stats(k.stats[:, j, :], k.x[:, j, :])
                own.variance(dve, last, sequence(b), b)

            def finish(b):
                own.finish(dve, sequence(b), b)
                dve.sem_inc(s["normable"], 1)

            join(0)
            join(1)
            finish(0)
            finish(1)
            for n in range(CHUNKS + 1):
                if 1 <= n < B - 1:
                    finish(n + 1)
                if n < B - 2:
                    join(n + 2)
                if n < CHUNKS:
                    dve.wait_ge(s["driven"], n + 1)
                    wait_if(dve, s["out_ready"], n - 1)
                    wait_if(dve, s["scanned"], n)
                    dve.tensor_tensor_scan(state[n % 2][:, :], decay[:, :], drive[n % 2][:, :],
                                           state[0][:, CH - 1:CH] if n % 2 else 0.0, ALU.mult, ALU.add)\
                       .then_inc(s["scanned"], 1)
                if n > 0:
                    tiles = chunk_tiles(n - 1)
                    dve.wait_ge(s["out_ready"], n)
                    dve.tensor_tensor(k.x[:, tiles, :], out_ps[(n - 1) % 2][:, :, :], k.x[:, tiles, :], ALU.add)\
                       .then_inc(s["added"], 1)
                    last = chunk_sums(k, dve, s["added"], n, n - 1)
            factors.on_dve(dve, last)

        @block.tensor
        def _(pe):
            pe.wait_ge(s["consts"], 2)
            for n in range(-1, CHUNKS + 1):
                if n + 1 < CHUNKS:
                    pe.wait_ge(s["xn_ready"], n + 2)
                    wait_if(pe, s["xt_ready"], n)
                    turn(k, pe, turn_ps[(n + 1) % 2], xn[(n + 1) % 2], TC).then_inc(s["turned"], 1)
                if 0 <= n < CHUNKS:
                    pe.wait_ge(s["xt_ready"], n + 1)
                    wait_if(pe, s["driven"], n - 1)
                    pe.matmul(in_ps[n % 2][:, :], w["in"][:, :], xt[n % XT][:, :], start=True, stop=True)\
                      .then_inc(s["input_ready"], 1)
                if n > 0:
                    c = (n - 1) % 2
                    pe.wait_ge(s["scanned"], n)
                    wait_if(pe, s["added"], n - 2)
                    for j in range(TC):
                        pe.matmul(out_ps[c][:, j, :], state[c][:, j * P:(j + 1) * P], w["out"][:, :], start=True, stop=False)
                        last = pe.matmul(out_ps[c][:, j, :], xt[(n - 1) % XT][:, j * P:(j + 1) * P], skip[:, :],
                                         start=False, stop=True)
                    last.then_inc(s["out_ready"], 1)

        @block.scalar
        def _(act):
            act.activation(one_decay[:, :], w["log_a"][:, :], ACT.Exp).then_inc(s["exp_ready"], 1)
            act.wait_ge(s["consts"], 1)
            for n in range(-2, CHUNKS):
                if n == -2:
                    own.root(act, sequence(0), 0)
                    own.root(act, sequence(1), 1)
                if n % 2 == 0 and n + 2 < CHUNKS:
                    act.wait_ge(s["normable"], (n + 2) // 2 + 1)
                if n + 2 < CHUNKS:
                    wait_if(act, s["turned"], n + 1)
                    chunk_norm(k, act, xn[n % 2], n + 2).then_inc(s["xn_ready"], 1)
                if 0 <= n + 1 < CHUNKS:
                    act.wait_ge(s["turned"], n + 2)
                    wait_if(act, s["out_ready"], n - 1)
                    act.activation(xt[(n + 1) % XT][:, :], turn_ps[(n + 1) % 2][:, :], ACT.Copy).then_inc(s["xt_ready"], 1)
                if n >= 0:
                    act.wait_ge(s["input_ready"], n + 1)
                    wait_if(act, s["scanned"], n - 1)
                    act.activation(drive[n % 2][:, :], in_ps[n % 2][:, :], ACT.Identity, bias=bias[:, 0:1],
                                   scale=w["b_vec"][:, 0:1]).then_inc(s["driven"], 1)
                if 2 <= n + 3 < B:
                    own.root(act, sequence(n + 3), n + 3)
            factors.on_act(act)


WEIGHTS = {
    "mix_r": [P, D], "mix_k": [P, D], "mix_v": [P, D], "mu_r": [P, 1], "mu_k": [P, 1],
    "q": [P, D], "q_swap": [P, D], "k": [P, HKV * HD], "k_swap": [P, HKV * HD], "v": [P, HKV * HD], "o": [P, D],
    "in": [P, D], "out": [P, D], "log_a": [P, 1], "b_in": [P, 1], "b_vec": [P, 1], "skip": [P, 1],
    "router": [P, E], "gate": [P, E + 1, F], "up": [P, E + 1, F], "down": [P, E + 1, 3, D],
    **CONSTANTS,
}


def macaron_kernel(nc, x, sources, out):
    with ExitStack() as ctx:
        k = Core(nc, ctx)
        k.x = k.sb("x", [P, NT, D])
        k.mean, k.var, k.root, k.rstd, k.shift = (k.sb(n, [P, NT]) for n in "mean var root rstd shift".split())
        k.stats = k.sb("stats", [P, NT, 6])
        k.ident, k.eps = k.sb("ident", [P, P]), k.sb("eps", [P, 1])
        k.filler = k.sb("filler", [P, FILL, ROW])
        k.filled, k.fills = ctx.enter_context(nc.semaphore("filled")), 0
        w = {n: k.sb("w_" + n, shape) for n, shape in WEIGHTS.items()}
        slots = [nc.dram_tensor(f"slots{j}", (SLOTS, ROW), F32).ap() for j in range(2)]
        results = [nc.dram_tensor(f"results{j}", (B * T * CHOICES, D), F32).ap() for j in range(2)]
        qd = nc.dram_tensor("query_parts", (U, HD, PARTS, 2, G, CH), BF16).ap()
        kd = nc.dram_tensor("key_parts", (U, HD, PARTS, T), BF16).ap()

        def stage(name, build, *args):
            k.stage = name + "_"
            build(k, *args)

        first = "mix_r mix_k mix_v mu_r mu_k".split()
        stage("load", load_stage, x, [(w[n][:], sources[n]) for n in first])
        stage("mix1", token_mix_stage, w, [(w[n][:], sources[n]) for n in WEIGHTS if n not in first], slots)
        with ExitStack() as attention:
            k.values, k.attended = (k.sb(n, [P, U, KT, VW], ctx=attention) for n in ("values", "attended"))
            units = Units(k, attention, qd, kd)
            stage("project", project_stage, w, units)
            stage("attend", attention_stage, units)
            stage("attended", attention_out_stage, w)
        stage("recycle", recycle_stage)
        stage("mix2", token_mix_stage, w)
        k.upper = {n: k.sb("upper_" + n, [P, E, F], F32R) for n in ("gate", "up")}
        mixture(k, stage, "moe1", w, slots[0], results[0], True)
        stage("recur", recurrence_stage, w, results[0])
        mixture(k, stage, "moe2", w, slots[1], results[1], False)
        stage("output", output_stage, results[1], out)


def lay_out(a):
    def column(v):
        return v.reshape(D, 1)

    def swap(m, heads):
        return m.reshape(D, heads, 2, HD // 2)[:, :, ::-1].reshape(D, heads * HD)

    def by_feature_of_unit(m):
        return m.reshape(D, HKV, G, HD).transpose(0, 1, 3, 2).reshape(D, D)

    def by_feature(experts, shared):
        return np.concatenate([experts, shared[None]]).transpose(2, 0, 1)

    down = np.zeros((E + 1, 3 * P, D), np.float32)
    down[:, :F] = np.concatenate([a["L1_ffn_expert_down"], a["L1_ffn_shared_down"][None]]).transpose(0, 2, 1)
    return {
        "mix_r": a["L0_ffn_W_r"].T, "mix_k": a["L0_ffn_W_k"].T, "mix_v": a["L0_ffn_W_v"].T,
        "mu_r": column(a["L0_ffn_mu_r"]), "mu_k": column(a["L0_ffn_mu_k"]),
        "q": by_feature_of_unit(a["L0_attn_w_q"]), "q_swap": by_feature_of_unit(swap(a["L0_attn_w_q"], H)),
        "k": a["L0_attn_w_k"], "k_swap": swap(a["L0_attn_w_k"], HKV),
        "v": a["L0_attn_w_v"], "o": a["L0_attn_w_o"],
        "in": a["L1_attn_W_in"], "out": a["L1_attn_C"],
        "log_a": column(a["L1_attn_log_A"]), "b_in": column(a["L1_attn_b_in"]), "b_vec": column(a["L1_attn_B_vec"]),
        "skip": column(a["L1_attn_D"]), "router": a["L1_ffn_gate_w"].T,
        "gate": by_feature(a["L1_ffn_expert_gate"], a["L1_ffn_shared_gate"]),
        "up": by_feature(a["L1_ffn_expert_up"], a["L1_ffn_shared_up"]),
        "down": down.reshape(E + 1, 3, P, D).transpose(2, 0, 1, 3),
        **moe_constants(),
    }


def kernel(**inputs):
    import concourse.bacc as bacc
    from concourse.bass_utils import run_bass_kernel_spmd

    inputs = {n: np.asarray(v) for n, v in inputs.items()}
    nc = bacc.Bacc("TRN2", target_bir_lowering=False, num_devices=1)
    arrays = {"in_x": np.ascontiguousarray(inputs["L0_attn_x"])}
    arrays.update({"in_" + n: np.ascontiguousarray(v) for n, v in lay_out(inputs).items()})
    aps = {n: nc.dram_tensor(n, v.shape, F32, kind="ExternalInput").ap() for n, v in arrays.items()}
    out = nc.dram_tensor("out_x", (B, T, D), F32, kind="ExternalOutput").ap()
    macaron_kernel(nc, aps["in_x"], {n: aps["in_" + n] for n in WEIGHTS}, out)
    return run_bass_kernel_spmd(nc, [arrays], core_ids=[0]).results[0]["out_x"]
```
